# Optimizing a Trainium2 kernel written in Bass

```python
import numpy as np
import jax
import jax.numpy as jnp

def _softmax(x, axis=-1):
    return jax.nn.softmax(x, axis=axis)

def _gelu(x):
    return jax.nn.gelu(x, approximate=True)

def _silu(x):
    return jax.nn.silu(x)

def _sigmoid(x):
    return jax.nn.sigmoid(x)

def _layernorm(x, axis=-1, eps=1e-05):
    m = jnp.mean(x, axis=axis, keepdims=True)
    v = jnp.var(x, axis=axis, keepdims=True)
    return (x - m) / jnp.sqrt(v + eps)

def _scatter_add(tgt, idx, src, axis=0):
    return tgt.at[idx].add(src)

def _segment_sum(src, seg, n):
    return jax.ops.segment_sum(src, seg, n)
kernel_name = 'mk_gnn_preln_d4_gnn_r32_dcf47e'

def setup_inputs(seed: int=0):
    np.random.seed(seed)
    _w = jnp.asarray

    def _rec_inputs():
        import jax
        import jax.numpy as jnp
        _gk = jax.random.key(seed)
        x = -0.000202 + 1 * jax.random.normal(jax.random.fold_in(_gk, 1), (3125, 128), jnp.float32)
        src = jax.random.randint(jax.random.fold_in(_gk, 2), (100000,), 0, 3125, jnp.int32)
        dst = jnp.minimum((3125 * jax.random.uniform(jax.random.fold_in(_gk, 3), (100000,)) ** 2.0).astype(jnp.int32), 99999)
        _o = jnp.argsort(dst, stable=True)
        src = src[_o]
        dst = dst[_o]
        edge_attr_50 = 0.000164634 + 1.0002 * jax.random.normal(jax.random.fold_in(_gk, 11), (100000, 50), jnp.float32)
        edge_type_8 = jax.random.randint(jax.random.fold_in(_gk, 13), (100000,), 0, 8, jnp.int32)
        node_type_8 = jax.random.randint(jax.random.fold_in(_gk, 14), (3125,), 0, 8, jnp.int32)
        return (x, src, dst, edge_attr_50, edge_type_8, node_type_8)
    x, src, dst, edge_attr_50, edge_type_8, node_type_8 = _rec_inputs()

    def _L0_gnn_setup():
        import jax, jax.numpy as jnp
        import numpy as np
        N_NODES = 50000
        N_EDGES = 25000
        NODE_DIM = 128
        EDGE_DIM = 50
        HIDDEN_DIM = 128

        def _linear_params(key, fan_in, fan_out):
            kw, kb = jax.random.split(key)
            bound = 1.0 / np.sqrt(fan_in)
            W = jax.random.uniform(kw, (fan_in, fan_out), minval=-bound, maxval=bound, dtype=jnp.float32)
            b = jax.random.uniform(kb, (fan_out,), minval=-bound, maxval=bound, dtype=jnp.float32)
            return (W, b)
        key = jax.random.key(seed)
        ks = jax.random.split(key, 7)
        x = jax.random.normal(ks[0], (N_NODES, NODE_DIM), dtype=jnp.float32)
        edge_index = jax.random.randint(ks[1], (2, N_EDGES), 0, N_NODES, dtype=jnp.int64)
        edge_features = jax.random.normal(ks[2], (N_EDGES, EDGE_DIM), dtype=jnp.float32)
        We1, be1 = _linear_params(ks[3], EDGE_DIM, HIDDEN_DIM)
        We2, be2 = _linear_params(ks[4], HIDDEN_DIM, NODE_DIM)
        Wn1, bn1 = _linear_params(ks[5], NODE_DIM, HIDDEN_DIM)
        Wn2, bn2 = _linear_params(ks[6], HIDDEN_DIM, NODE_DIM)
        return {'x': x, 'edge_index': edge_index, 'edge_features': edge_features, 'We1': We1, 'be1': be1, 'We2': We2, 'be2': be2, 'Wn1': Wn1, 'bn1': bn1, 'Wn2': Wn2, 'bn2': bn2}
    _L0_gnn_all = _L0_gnn_setup()
    _L0_gnn_in = {k: v for k, v in _L0_gnn_all.items() if k in ('We1', 'be1', 'We2', 'be2', 'Wn1', 'bn1', 'Wn2', 'bn2')}
    del _L0_gnn_all

    def _L1_gnn_setup():
        import jax, jax.numpy as jnp
        import numpy as np
        N = 3125
        E = 50000
        IN_DIM = 128
        OUT_DIM = 128
        BN_EPS = 1e-05
        key = jax.random.key(seed)
        ks = jax.random.split(key, 8)
        x = jax.random.normal(ks[0], (N, IN_DIM), dtype=jnp.float32)
        edge_index = jax.random.randint(ks[1], (2, E), 0, N, dtype=jnp.int32)
        s1 = 1.0 / np.sqrt(IN_DIM)
        s2 = 1.0 / np.sqrt(OUT_DIM)
        W1 = jax.random.uniform(ks[2], (IN_DIM, OUT_DIM), minval=-s1, maxval=s1, dtype=jnp.float32)
        b1 = jax.random.uniform(ks[3], (OUT_DIM,), minval=-s1, maxval=s1, dtype=jnp.float32)
        W2 = jax.random.uniform(ks[4], (OUT_DIM, OUT_DIM), minval=-s2, maxval=s2, dtype=jnp.float32)
        b2 = jax.random.uniform(ks[5], (OUT_DIM,), minval=-s2, maxval=s2, dtype=jnp.float32)
        eps = jnp.float32(0.0)
        gamma = jnp.ones((OUT_DIM,), dtype=jnp.float32)
        beta = jnp.zeros((OUT_DIM,), dtype=jnp.float32)
        return {'x': x, 'edge_index': edge_index, 'W1': W1, 'b1': b1, 'W2': W2, 'b2': b2, 'eps': eps, 'gamma': gamma, 'beta': beta}
    _L1_gnn_all = _L1_gnn_setup()
    _L1_gnn_in = {k: v for k, v in _L1_gnn_all.items() if k in ('W1', 'b1', 'W2', 'b2', 'eps', 'gamma', 'beta')}
    del _L1_gnn_all

    def _L2_gnn_setup():
        import jax, jax.numpy as jnp
        import numpy as np
        N = 50000
        E = 12500
        HID = 128
        H = 8
        HS = HID // H
        TN = 8
        R = 8
        L = 2
        OUT = 128
        EPS = 1e-05
        SQRT_D = float(np.sqrt(HS))

        def typed_linear(x, types, W):
            out = jnp.zeros((x.shape[0], W.shape[-1]), x.dtype)
            for t in range(W.shape[0]):
                out = out + jnp.where((types == t)[:, None], x @ W[t], 0.0)
            return out

        def rel_apply(h, etype, W):
            out = jnp.zeros_like(h)
            for r in range(W.shape[1]):
                out = out + jnp.where((etype == r)[:, None, None], jnp.einsum('ehi,hio->eho', h, W[:, r]), 0.0)
            return out

        def gt_layer(x, src, dst, ntype, etype, Wk, Wq, Wv, Wa, pri, Watt, Wmsg, skip, g, b):
            n = x.shape[0]
            k = typed_linear(x, ntype, Wk).reshape(n, H, HS)
            q = typed_linear(x, ntype, Wq).reshape(n, H, HS)
            v = typed_linear(x, ntype, Wv).reshape(n, H, HS)
            k_j, q_i, v_j = (k[src], q[dst], v[src])
            kw = rel_apply(k_j, etype, Watt)
            a = (kw * q_i).sum(-1) * pri[:, etype].T / SQRT_D
            amax = jax.ops.segment_max(a, dst, num_segments=n)
            ex = jnp.exp(a - amax[dst])
            den = jax.ops.segment_sum(ex, dst, num_segments=n)
            alpha = ex / (den[dst] + 1e-16)
            m = rel_apply(v_j, etype, Wmsg)
            agg = jax.ops.segment_sum(alpha[..., None] * m, dst, num_segments=n)
            out = jax.nn.silu(typed_linear(agg.reshape(n, HID), ntype, Wa))
            al = jax.nn.sigmoid(skip[ntype])[:, None]
            out = out * al + x * (1.0 - al)
            mu = out.mean(-1, keepdims=True)
            var = ((out - mu) ** 2).mean(-1, keepdims=True)
            return (out - mu) / jnp.sqrt(var + EPS) * g + b
        key = jax.random.key(seed)
        ks = jax.random.split(key, 12)
        s = 1.0 / np.sqrt(HID)
        sh = 1.0 / np.sqrt(HS)
        return {'x': jax.random.normal(ks[0], (N, HID), jnp.float32), 'edge_index': jax.random.randint(ks[1], (2, E), 0, N, dtype=jnp.int32), 'ntype': jax.random.randint(ks[2], (N,), 0, TN, dtype=jnp.int32), 'etype': jax.random.randint(ks[3], (E,), 0, R, dtype=jnp.int32), 'Wk': jax.random.normal(ks[4], (L, TN, HID, HID), jnp.float32) * s, 'Wq': jax.random.normal(ks[5], (L, TN, HID, HID), jnp.float32) * s, 'Wv': jax.random.normal(ks[6], (L, TN, HID, HID), jnp.float32) * s, 'Wa': jax.random.normal(ks[7], (L, TN, HID, HID), jnp.float32) * s, 'pri': jnp.ones((L, H, R), jnp.float32), 'Watt': jax.random.normal(ks[8], (L, H, R, HS, HS), jnp.float32) * sh, 'Wmsg': jax.random.normal(ks[9], (L, H, R, HS, HS), jnp.float32) * sh, 'skip': jnp.ones((L, TN), jnp.float32), 'ln_g': jnp.ones((L, HID), jnp.float32), 'ln_b': jnp.zeros((L, HID), jnp.float32), 'Wff': jax.random.normal(ks[10], (HID, OUT), jnp.float32) * s, 'bff': jnp.zeros((OUT,), jnp.float32)}
    _L2_gnn_all = _L2_gnn_setup()
    _L2_gnn_in = {k: v for k, v in _L2_gnn_all.items() if k in ('Wk', 'Wq', 'Wv', 'Wa', 'pri', 'Watt', 'Wmsg', 'skip', 'ln_g', 'ln_b', 'Wff', 'bff')}
    del _L2_gnn_all

    def _L3_gnn_setup():
        import jax, jax.numpy as jnp
        import numpy as np
        N_NODES = 50000
        N_EDGES = 25000
        DIM = 128
        BN_EPS = 1e-05
        key = jax.random.key(seed)
        ks = jax.random.split(key, 12)
        d = DIM
        s = 1.0 / np.sqrt(d)
        x = jax.random.normal(ks[0], (N_NODES, d), dtype=jnp.float32)
        edge_index = jax.random.randint(ks[1], (2, N_EDGES), 0, N_NODES, dtype=jnp.int64)
        W_msg = jax.random.uniform(ks[2], (d, d), jnp.float32, -s, s)
        b_msg = jax.random.uniform(ks[3], (d,), jnp.float32, -s, s)
        sa = 1.0 / np.sqrt(2 * d)
        W_att = jax.random.uniform(ks[4], (2 * d, 1), jnp.float32, -sa, sa)
        b_att = jax.random.uniform(ks[5], (1,), jnp.float32, -sa, sa)
        W_ih = jax.random.uniform(ks[6], (3 * d, d), jnp.float32, -s, s)
        b_ih = jax.random.uniform(ks[7], (3 * d,), jnp.float32, -s, s)
        W_hh = jax.random.uniform(ks[8], (3 * d, d), jnp.float32, -s, s)
        b_hh = jax.random.uniform(ks[9], (3 * d,), jnp.float32, -s, s)
        gamma = jnp.ones((d,), jnp.float32)
        beta = jnp.zeros((d,), jnp.float32)
        return {'x': x, 'edge_index': edge_index, 'W_msg': W_msg, 'b_msg': b_msg, 'W_att': W_att, 'b_att': b_att, 'W_ih': W_ih, 'b_ih': b_ih, 'W_hh': W_hh, 'b_hh': b_hh, 'gamma': gamma, 'beta': beta}
    _L3_gnn_all = _L3_gnn_setup()
    _L3_gnn_in = {k: v for k, v in _L3_gnn_all.items() if k in ('W_msg', 'b_msg', 'W_att', 'b_att', 'W_ih', 'b_ih', 'W_hh', 'b_hh', 'gamma', 'beta')}
    del _L3_gnn_all
    return {'x': x, 'src': src, 'dst': dst, 'edge_attr_50': edge_attr_50, 'edge_type_8': edge_type_8, 'node_type_8': node_type_8, 'L0_gnn_We1': _L0_gnn_in['We1'], 'L0_gnn_be1': _L0_gnn_in['be1'], 'L0_gnn_We2': _L0_gnn_in['We2'], 'L0_gnn_be2': _L0_gnn_in['be2'], 'L0_gnn_Wn1': _L0_gnn_in['Wn1'], 'L0_gnn_bn1': _L0_gnn_in['bn1'], 'L0_gnn_Wn2': _L0_gnn_in['Wn2'], 'L0_gnn_bn2': _L0_gnn_in['bn2'], 'L1_gnn_W1': _L1_gnn_in['W1'], 'L1_gnn_b1': _L1_gnn_in['b1'], 'L1_gnn_W2': _L1_gnn_in['W2'], 'L1_gnn_b2': _L1_gnn_in['b2'], 'L1_gnn_eps': _L1_gnn_in['eps'], 'L1_gnn_gamma': _L1_gnn_in['gamma'], 'L1_gnn_beta': _L1_gnn_in['beta'], 'L2_gnn_Wk': _L2_gnn_in['Wk'], 'L2_gnn_Wq': _L2_gnn_in['Wq'], 'L2_gnn_Wv': _L2_gnn_in['Wv'], 'L2_gnn_Wa': _L2_gnn_in['Wa'], 'L2_gnn_pri': _L2_gnn_in['pri'], 'L2_gnn_Watt': _L2_gnn_in['Watt'], 'L2_gnn_Wmsg': _L2_gnn_in['Wmsg'], 'L2_gnn_skip': _L2_gnn_in['skip'], 'L2_gnn_ln_g': _L2_gnn_in['ln_g'], 'L2_gnn_ln_b': _L2_gnn_in['ln_b'], 'L2_gnn_Wff': _L2_gnn_in['Wff'], 'L2_gnn_bff': _L2_gnn_in['bff'], 'L3_gnn_W_msg': _L3_gnn_in['W_msg'], 'L3_gnn_b_msg': _L3_gnn_in['b_msg'], 'L3_gnn_W_att': _L3_gnn_in['W_att'], 'L3_gnn_b_att': _L3_gnn_in['b_att'], 'L3_gnn_W_ih': _L3_gnn_in['W_ih'], 'L3_gnn_b_ih': _L3_gnn_in['b_ih'], 'L3_gnn_W_hh': _L3_gnn_in['W_hh'], 'L3_gnn_b_hh': _L3_gnn_in['b_hh'], 'L3_gnn_gamma': _L3_gnn_in['gamma'], 'L3_gnn_beta': _L3_gnn_in['beta']}

def reference(x, src, dst, edge_attr_50, edge_type_8, node_type_8, L0_gnn_We1, L0_gnn_be1, L0_gnn_We2, L0_gnn_be2, L0_gnn_Wn1, L0_gnn_bn1, L0_gnn_Wn2, L0_gnn_bn2, L1_gnn_W1, L1_gnn_b1, L1_gnn_W2, L1_gnn_b2, L1_gnn_eps, L1_gnn_gamma, L1_gnn_beta, L2_gnn_Wk, L2_gnn_Wq, L2_gnn_Wv, L2_gnn_Wa, L2_gnn_pri, L2_gnn_Watt, L2_gnn_Wmsg, L2_gnn_skip, L2_gnn_ln_g, L2_gnn_ln_b, L2_gnn_Wff, L2_gnn_bff, L3_gnn_W_msg, L3_gnn_b_msg, L3_gnn_W_att, L3_gnn_b_att, L3_gnn_W_ih, L3_gnn_b_ih, L3_gnn_W_hh, L3_gnn_b_hh, L3_gnn_gamma, L3_gnn_beta):
    import jax
    import jax.numpy as jnp

    def _L0_gnn_ref(x, edge_index, edge_features, We1, be1, We2, be2, Wn1, bn1, Wn2, bn2):
        import jax, jax.numpy as jnp
        import numpy as np
        N_NODES = 50000
        N_EDGES = 25000
        NODE_DIM = 128
        EDGE_DIM = 50
        HIDDEN_DIM = 128

        def _linear_params(key, fan_in, fan_out):
            kw, kb = jax.random.split(key)
            bound = 1.0 / np.sqrt(fan_in)
            W = jax.random.uniform(kw, (fan_in, fan_out), minval=-bound, maxval=bound, dtype=jnp.float32)
            b = jax.random.uniform(kb, (fan_out,), minval=-bound, maxval=bound, dtype=jnp.float32)
            return (W, b)
        src = edge_index[0]
        dst = edge_index[1]
        edge_weights = jax.nn.silu(edge_features @ We1 + be1) @ We2 + be2
        messages = x[src] * edge_weights
        agg = jax.ops.segment_sum(messages, dst, num_segments=x.shape[0])
        out = jax.nn.silu(agg @ Wn1 + bn1) @ Wn2 + bn2
        return x + out

    def _L1_gnn_ref(x, edge_index, W1, b1, W2, b2, eps, gamma, beta):
        import jax, jax.numpy as jnp
        import numpy as np
        N = 3125
        E = 50000
        IN_DIM = 128
        OUT_DIM = 128
        BN_EPS = 1e-05
        src = edge_index[0]
        dst = edge_index[1]
        agg = jax.ops.segment_sum(x[src], dst, num_segments=x.shape[0])
        h = (1.0 + eps) * x + agg
        h = jnp.maximum(h @ W1 + b1, 0.0)
        h = h @ W2 + b2
        mean = jnp.mean(h, axis=0)
        var = jnp.mean(jnp.square(h - mean), axis=0)
        h = (h - mean) * jax.lax.rsqrt(var + BN_EPS) * gamma + beta
        return jnp.maximum(h, 0.0)

    def _L2_gnn_ref(x, edge_index, ntype, etype, Wk, Wq, Wv, Wa, pri, Watt, Wmsg, skip, ln_g, ln_b, Wff, bff):
        import jax, jax.numpy as jnp
        import numpy as np
        N = 50000
        E = 12500
        HID = 128
        H = 8
        HS = HID // H
        TN = 8
        R = 8
        L = 2
        OUT = 128
        EPS = 1e-05
        SQRT_D = float(np.sqrt(HS))

        def typed_linear(x, types, W):
            out = jnp.zeros((x.shape[0], W.shape[-1]), x.dtype)
            for t in range(W.shape[0]):
                out = out + jnp.where((types == t)[:, None], x @ W[t], 0.0)
            return out

        def rel_apply(h, etype, W):
            out = jnp.zeros_like(h)
            for r in range(W.shape[1]):
                out = out + jnp.where((etype == r)[:, None, None], jnp.einsum('ehi,hio->eho', h, W[:, r]), 0.0)
            return out

        def gt_layer(x, src, dst, ntype, etype, Wk, Wq, Wv, Wa, pri, Watt, Wmsg, skip, g, b):
            n = x.shape[0]
            k = typed_linear(x, ntype, Wk).reshape(n, H, HS)
            q = typed_linear(x, ntype, Wq).reshape(n, H, HS)
            v = typed_linear(x, ntype, Wv).reshape(n, H, HS)
            k_j, q_i, v_j = (k[src], q[dst], v[src])
            kw = rel_apply(k_j, etype, Watt)
            a = (kw * q_i).sum(-1) * pri[:, etype].T / SQRT_D
            amax = jax.ops.segment_max(a, dst, num_segments=n)
            ex = jnp.exp(a - amax[dst])
            den = jax.ops.segment_sum(ex, dst, num_segments=n)
            alpha = ex / (den[dst] + 1e-16)
            m = rel_apply(v_j, etype, Wmsg)
            agg = jax.ops.segment_sum(alpha[..., None] * m, dst, num_segments=n)
            out = jax.nn.silu(typed_linear(agg.reshape(n, HID), ntype, Wa))
            al = jax.nn.sigmoid(skip[ntype])[:, None]
            out = out * al + x * (1.0 - al)
            mu = out.mean(-1, keepdims=True)
            var = ((out - mu) ** 2).mean(-1, keepdims=True)
            return (out - mu) / jnp.sqrt(var + EPS) * g + b
        src, dst = (edge_index[0], edge_index[1])
        emb = x
        for l in range(L):
            emb = gt_layer(emb, src, dst, ntype, etype, Wk[l], Wq[l], Wv[l], Wa[l], pri[l], Watt[l], Wmsg[l], skip[l], ln_g[l], ln_b[l])
        return emb @ Wff + bff

    def _L3_gnn_ref(x, edge_index, W_msg, b_msg, W_att, b_att, W_ih, b_ih, W_hh, b_hh, gamma, beta):
        import jax, jax.numpy as jnp
        import numpy as np
        N_NODES = 50000
        N_EDGES = 25000
        DIM = 128
        BN_EPS = 1e-05
        num_nodes, d = x.shape
        src = edge_index[0]
        dst = edge_index[1]
        xs = x[src]
        xd = x[dst]
        att = jax.nn.sigmoid(xs @ W_att[:d] + xd @ W_att[d:] + b_att)
        messages = (xs @ W_msg + b_msg) * att
        aggregated = jax.ops.segment_sum(messages, dst, num_segments=num_nodes)
        gi = aggregated @ W_ih.T + b_ih
        gh = x @ W_hh.T + b_hh
        i_r, i_z, i_n = jnp.split(gi, 3, axis=1)
        h_r, h_z, h_n = jnp.split(gh, 3, axis=1)
        r = jax.nn.sigmoid(i_r + h_r)
        z = jax.nn.sigmoid(i_z + h_z)
        n = jnp.tanh(i_n + r * h_n)
        h_new = (1.0 - z) * n + z * x
        mean = jnp.mean(h_new, axis=0)
        var = jnp.var(h_new, axis=0)
        return gamma * (h_new - mean) * jax.lax.rsqrt(var + BN_EPS) + beta
    edge_index = jnp.stack([src, dst])
    h = jnp.maximum(_layernorm(x, axis=-1), 0.0)
    x = x + _L0_gnn_ref(h, edge_index, edge_attr_50, L0_gnn_We1, L0_gnn_be1, L0_gnn_We2, L0_gnn_be2, L0_gnn_Wn1, L0_gnn_bn1, L0_gnn_Wn2, L0_gnn_bn2)
    h = jnp.maximum(_layernorm(x, axis=-1), 0.0)
    x = x + _L1_gnn_ref(h, edge_index, L1_gnn_W1, L1_gnn_b1, L1_gnn_W2, L1_gnn_b2, L1_gnn_eps, L1_gnn_gamma, L1_gnn_beta)
    h = jnp.maximum(_layernorm(x, axis=-1), 0.0)
    x = x + _L2_gnn_ref(h, edge_index, node_type_8, edge_type_8, L2_gnn_Wk, L2_gnn_Wq, L2_gnn_Wv, L2_gnn_Wa, L2_gnn_pri, L2_gnn_Watt, L2_gnn_Wmsg, L2_gnn_skip, L2_gnn_ln_g, L2_gnn_ln_b, L2_gnn_Wff, L2_gnn_bff)
    h = jnp.maximum(_layernorm(x, axis=-1), 0.0)
    x = x + _L3_gnn_ref(h, edge_index, L3_gnn_W_msg, L3_gnn_b_msg, L3_gnn_W_att, L3_gnn_b_att, L3_gnn_W_ih, L3_gnn_b_ih, L3_gnn_W_hh, L3_gnn_b_hh, L3_gnn_gamma, L3_gnn_beta)
    return x

_drawn_inputs = setup_inputs


def setup_inputs(seed=0):
    import zlib

    import numpy as np

    out = dict(_drawn_inputs(seed))
    spreads = {'L1_gnn_gamma': (1.0, 0.2),
     'L1_gnn_beta': (0.0, 0.1),
     'L2_gnn_pri': (1.0, 0.2),
     'L2_gnn_skip': (1.0, 0.2),
     'L2_gnn_ln_g': (1.0, 0.2),
     'L2_gnn_ln_b': (0.0, 0.1),
     'L2_gnn_bff': (0.0, 0.1),
     'L3_gnn_gamma': (1.0, 0.2),
     'L3_gnn_beta': (0.0, 0.1)}
    factors = {'L0_gnn_bn1': 4.363,
     'L1_gnn_b1': 28.217,
     'L1_gnn_b2': 64.0,
     'L3_gnn_b_ih': 6.934,
     'L3_gnn_b_hh': 7.19}
    for name, (base, spread) in spreads.items():
        noise = np.random.default_rng([zlib.crc32(name.encode()), seed]).standard_normal(out[name].shape)
        drawn = base * np.exp(spread * noise) if base else spread * noise
        out[name] = jnp.asarray(drawn.astype(out[name].dtype))
    for name, factor in factors.items():
        out[name] = (out[name] * factor).astype(out[name].dtype)
    return out
```

```python
from contextlib import ExitStack

import concourse.bass as bass
from concourse import mybir

P = 128
N = 3125
E = 100000
D = 128
EF = 50
TILES = -(-N // P)
NP = TILES * P
CHUNKS = -(-E // P)
G = 4
GROUPS = -(-(CHUNKS + TILES - 1) // G)
VISITS = GROUPS * G
CT = -(-VISITS // P)
HEADS, HS, REL, TYPES, LAYERS = 8, 16, 8, 8, 2
LANES = P // HEADS
LV = -(-VISITS // LANES)
SV = LV * LANES
LE = LV * P
PAD_DST = 30000
BIG = 1.0e38
EPS = 1e-5
ROW3 = 132
AW = D + HEADS

F32 = mybir.dt.float32
BF16 = mybir.dt.bfloat16
I32 = mybir.dt.int32
U32 = mybir.dt.uint32
ALU = mybir.AluOpType
ACT = mybir.ActivationFunctionType
AX = mybir.AxisListType

TBANKS = -(-TILES // 4)
CODE = (TILES - 1).bit_length()
BLOCKS = [(b, min(4, TILES - b)) for b in range(0, TILES, 4)]


class Tensors:
    pass


class Chain:

    def __init__(self, eng, sem):
        self.eng, self.sem, self.n = eng, sem, 0

    def __call__(self, ins):
        self.n += 1
        ins.then_inc(self.sem, 1)
        self.eng.wait_ge(self.sem, self.n)


def stack(nc, ctx, stage=""):
    def sb(name, shape, dt=F32):
        return ctx.enter_context(nc.sbuf_tensor(stage + name, shape, dt))

    def ps(name, shape, dt=F32):
        return ctx.enter_context(nc.psum_tensor(stage + name, shape, dt))

    def sem(name):
        return ctx.enter_context(nc.semaphore(stage + name))

    return sb, ps, sem


def setup(nc, A, T):
    with ExitStack() as ctx:
        sb, ps, sem = stack(nc, ctx, "setup_")
        ctab = sb("ctab", [P, CT, 3, P], I32)
        last = sb("last", [P, CT])
        thr = sb("thr", [P, TILES - 1, CT])
        cmp1 = sb("cmp1", [P, TILES - 1, CT])
        cnt = sb("cnt", [P, TILES - 1])
        tio = sb("tio", [P, TILES - 1])
        ends = sb("ends", [P, TILES - 1])
        vio = sb("vio", [P, CT])
        cmp2 = sb("cmp2", [P, CT, TILES - 1])
        tvp = sb("tvp", [P, CT])
        cvp = sb("cvp", [P, CT])
        cvi = sb("cvi", [P, CT], I32)
        base = sb("base", [P, CT])
        viorow = sb("viorow", [P, VISITS])
        tvrow = sb("tvrow", [P, VISITS])
        ones = sb("ones", [P, P])
        vt = sb("vt", [P, CT, 3 * P], I32)
        fld = sb("fld", [P, 4, CT, P])
        vtf = sb("vtf", [P, 2, CT, P])
        zeros = sb("zeros", [P, 16 * EF])
        pc = ps("pc", [P, 512])
        pt = [ps(f"pt{i}", [P, 4, P]) for i in range(2)]
        loaded, stored, padded = sem("ctab_loaded"), sem("ctab_stored"), sem("ctab_padded")
        copied, x_in, zeroed = sem("attr_copied"), sem("x_in"), sem("zeroed")
        consts, chain, counted = sem("consts"), sem("setup_chain"), sem("counted")
        ends_ready, cvi_ready, rows_in = sem("ends_ready"), sem("cvi_ready"), T.rows_in
        fields, turned, taken = sem("fields"), sem("turned"), sem("taken")
        block = ctx.enter_context(nc.Block())
        chunked = T.chunk_table.rearrange("(j p) (k e) -> p j k e", p=P, e=P)
        full = (CT - 1) * P
        more = E // P - full
        tail = E - (full + more) * P

        @block.sync
        def _(sp):
            sp.wait_ge(padded, 3)
            for k, a in enumerate((A["dst"], A["src"], A["edge_type_8"])):
                sp.dma_start(ctab[:, 0:CT - 1, k, :], a[0:full * P].rearrange("(j p e) -> p j e", p=P, e=P)).then_inc(loaded, 16)
                sp.dma_start(ctab[0:more, CT - 1, k, :], a[full * P:(full + more) * P].rearrange("(p e) -> p e", e=P)).then_inc(loaded, 16)
                sp.dma_start(ctab[more:more + 1, CT - 1, k, 0:tail], a[(full + more) * P:E].rearrange("(p e) -> p e", p=1)).then_inc(loaded, 16)
            sp.wait_ge(loaded, 9 * 16)
            for j in range(CT):
                sp.dma_start(chunked[:, j], ctab[:, j]).then_inc(stored, 16)
            full_tiles = N // P
            sp.wait_ge(zeroed, 2)
            sp.dma_start(T.X[:, 0:full_tiles, :], A["x"][0:full_tiles * P, :].rearrange("(t p) f -> p t f", p=P)).then_inc(x_in, 16)
            sp.dma_start(T.X[0:N - full_tiles * P, full_tiles, :], A["x"][full_tiles * P:N, :]).then_inc(x_in, 16)
            sp.wait_ge(x_in, 32)
            sp.wait_ge(stored, 16 * CT)

        @block.scalar
        def _(act):
            rows = E // 4
            for q in range(4):
                act.dma_start(T.attr[q * rows:(q + 1) * rows, :].rearrange("(a b) f -> a (b f)", b=50),
                              A["edge_attr_50"][q * rows:(q + 1) * rows, :].rearrange("(a b) f -> a (b f)", b=50)).then_inc(copied, 16)
            act.wait_ge(zeroed, 1)
            pad = T.attr.shape[0] - E
            act.dma_start(T.attr[E:E + pad, :].rearrange("(q r) f -> q (r f)", r=16),
                          zeros[0:pad // 16, 0:16 * EF]).then_inc(copied, 16)
            act.wait_ge(copied, 5 * 16)

        @block.gpsimd
        def _(pool):
            pool.memset(ctab[:, CT - 1, 0, :], PAD_DST).then_inc(padded, 1)
            pool.memset(ctab[:, CT - 1, 1, :], 0).then_inc(padded, 1)
            pool.memset(ctab[:, CT - 1, 2, :], 0).then_inc(padded, 1)
            pool.memset(T.ident[:, :], 0.0).then_inc(consts, 1)
            pool.wait_ge(consts, 1)
            pool.affine_select(out=T.ident[:, :], in_=T.ident[:, :], compare_op=ALU.not_equal, fill=1.0, base=0,
                               pattern=[[-1, P]], channel_multiplier=1).then_inc(consts, 1)
            pool.iota(thr[:, :, :], [[P, TILES - 1], [0, CT]], base=P, channel_multiplier=0,
                      allow_small_or_imprecise_dtypes=True).then_inc(consts, 1)
            pool.iota(tio[:, :], [[1, TILES - 1]], base=0, channel_multiplier=0,
                      allow_small_or_imprecise_dtypes=True).then_inc(consts, 1)
            pool.iota(vio[:, :], [[P, CT]], base=0, channel_multiplier=1,
                      allow_small_or_imprecise_dtypes=True).then_inc(consts, 1)
            pool.iota(viorow[:, :], [[1, VISITS]], base=0, channel_multiplier=0,
                      allow_small_or_imprecise_dtypes=True).then_inc(consts, 1)
            pool.iota(T.iota[:, :], [[1, P]], base=0, channel_multiplier=0,
                      allow_small_or_imprecise_dtypes=True).then_inc(consts, 1)
            pool.memset(ones[:, :], 1.0).then_inc(consts, 1)
            pool.wait_ge(cvi_ready, 1)
            pool.wait_ge(stored, 16 * CT)
            for j in range(CT):
                pool.indirect_dma_start(out=vt[:, j, :], out_offset=None, in_=T.chunk_table,
                                        in_offset=bass.IndirectOffsetOnAxis(ap=cvi[:, j:j + 1].bitcast(U32), axis=0),
                                        bounds_check=CT * P - 1).then_inc(rows_in, 16)

        @block.tensor
        def _(pe):
            pe.wait_ge(counted, 1)
            pe.wait_ge(consts, 8)
            pe.matmul(pc[:, 0:TILES - 1], ones[:, :], cnt[:, :], start=True, stop=True).then_inc(ends_ready, 1)
            pe.wait_ge(fields, 1)
            for b in range(CT):
                if b >= 2:
                    pe.wait_ge(taken, b - 1)
                for k in range(4):
                    tr = pe.transpose(pt[b % 2][:, k, :], fld[:, k, b, :], T.ident[:, :])
                tr.then_inc(turned, 1)

        @block.vector
        def _(dve):
            then = Chain(dve, chain)
            dve.memset(zeros[:, :], 0.0).then_inc(zeroed, 1)
            dve.memset(T.X[:, TILES - 1, :], 0.0).then_inc(zeroed, 1)
            dve.wait_ge(loaded, 9 * 16)
            dve.wait_ge(consts, 8)
            then(dve.tensor_copy(last[:, :], ctab[:, :, 0, P - 1]))
            then(dve.tensor_tensor(cmp1[:, :, :], last[:, :].unsqueeze(1).to_broadcast([P, TILES - 1, CT]), thr[:, :, :], ALU.is_lt))
            dve.tensor_reduce(cnt[:, :], cmp1[:, :, :], AX.X, ALU.add).then_inc(counted, 1)
            dve.wait_ge(ends_ready, 1)
            then(dve.tensor_tensor(ends[:, :], pc[:, 0:TILES - 1], tio[:, :], ALU.add))
            then(dve.tensor_tensor(cmp2[:, :, :], ends[:, :].unsqueeze(1).to_broadcast([P, CT, TILES - 1]),
                                   vio[:, :].unsqueeze(2).to_broadcast([P, CT, TILES - 1]), ALU.is_lt))
            then(dve.tensor_reduce(tvp[:, :], cmp2[:, :, :], AX.X, ALU.add))
            then(dve.tensor_tensor(cvp[:, :], vio[:, :], tvp[:, :], ALU.subtract))
            dve.tensor_copy(cvi[:, :], cvp[:, :]).then_inc(cvi_ready, 1)
            then(dve.tensor_scalar(base[:, :], tvp[:, :], float(P), None, ALU.mult))
            then(dve.tensor_scalar(tvrow[:, :], viorow[:, :], ends[:, 0:1], None, ALU.is_gt))
            for t in range(1, TILES - 1):
                then(dve.scalar_tensor_tensor(out=tvrow[:, :], in0=viorow[:, :], scalar=ends[:, t:t + 1],
                                              in1=tvrow[:, :], op0=ALU.is_gt, op1=ALU.add))
            tiles = tvrow[0:1, :].rearrange("o (g k) -> o g k", k=G)
            for k in range(G - 2, -1, -1):
                then(dve.scalar_tensor_tensor(out=tiles[:, :, k], in0=tiles[:, :, k + 1], scalar=float(1 << CODE),
                                              in1=tiles[:, :, k], op0=ALU.mult, op1=ALU.add))
            then(dve.tensor_copy(T.tile_codes[:, :], tiles[:, :, 0]))
            dve.wait_ge(rows_in, 16 * CT)
            rows = vt[:, :, :].rearrange("p j (k e) -> p j k e", e=P)
            then(dve.tensor_copy(vtf[:, 0, :, :], rows[:, :, 0, :]))
            then(dve.tensor_copy(fld[:, 2, :, :], rows[:, :, 1, :]))
            then(dve.tensor_copy(vtf[:, 1, :, :], rows[:, :, 2, :]))
            for j in range(CT):
                then(dve.tensor_scalar(fld[:, 0, j, :], vtf[:, 0, j, :], base[:, j:j + 1], None, ALU.subtract))
            then(dve.scalar_tensor_tensor(out=fld[:, 3, :, :], in0=fld[:, 2, :, :], scalar=float(REL),
                                          in1=vtf[:, 1, :, :], op0=ALU.mult, op1=ALU.add))
            then(dve.tensor_scalar(vtf[:, 1, :, :], fld[:, 0, :, :], 0.0, None, ALU.is_ge))
            then(dve.scalar_tensor_tensor(out=vtf[:, 1, :, :], in0=fld[:, 0, :, :], scalar=float(P),
                                          in1=vtf[:, 1, :, :], op0=ALU.is_lt, op1=ALU.mult))
            dve.scalar_tensor_tensor(out=fld[:, 1, :, :], in0=vtf[:, 0, :, :], scalar=1.0,
                                     in1=vtf[:, 1, :, :], op0=ALU.add, op1=ALU.mult).then_inc(fields, 1)
            for b in range(CT):
                dve.wait_ge(turned, b + 1)
                to = slice(b * P, (b + 1) * P)
                dve.tensor_copy(T.rel[:, to], pt[b % 2][:, 0, :])
                dve.tensor_copy(T.key[:, to], pt[b % 2][:, 1, :])
                dve.tensor_copy(T.src[:, to], pt[b % 2][:, 2, :])
                dve.tensor_copy(T.srcrel[:, to], pt[b % 2][:, 3, :]).then_inc(taken, 1)


def layernorm_relu(nc, T, name, store):
    with ExitStack() as ctx:
        sb, ps, sem = stack(nc, ctx)
        sq = sb(name + "_sq", [P, TILES, D])
        st = sb(name + "_st", [P, 4, TILES])
        chain, centred, squared = sem(name + "_chain"), sem(name + "_centred"), sem(name + "_squared")
        var_ready, root, h_ready, stored = sem(name + "_var"), sem(name + "_root"), sem(name + "_h"), sem(name + "_stored")
        block = ctx.enter_context(nc.Block())

        def wide(k):
            return st[:, k, :].unsqueeze(2).to_broadcast([P, TILES, D])

        @block.vector
        def _(dve):
            then = Chain(dve, chain)
            then(dve.tensor_reduce(st[:, 0, :], T.X[:, :, :], AX.X, ALU.add))
            then(dve.tensor_scalar(st[:, 0, :], st[:, 0, :], 1.0 / D, None, ALU.mult))
            dve.tensor_tensor(T.H[:, :, :], T.X[:, :, :], wide(0), ALU.subtract).then_inc(centred, 1)
            dve.wait_ge(squared, 1)
            then(dve.tensor_reduce(st[:, 1, :], sq[:, :, :], AX.X, ALU.add))
            dve.tensor_scalar(st[:, 1, :], st[:, 1, :], 1.0 / D, EPS, ALU.mult, ALU.add).then_inc(var_ready, 1)
            dve.wait_ge(root, 1)
            then(dve.reciprocal(st[:, 3, :], st[:, 2, :]))
            dve.scalar_tensor_tensor(out=T.H[:, :, :], in0=T.H[:, :, :], scalar=0.0, in1=wide(3),
                                     op0=ALU.max, op1=ALU.mult).then_inc(h_ready, 1)

        @block.scalar
        def _(act):
            act.wait_ge(centred, 1)
            act.activation(sq[:, :, :], T.H[:, :, :], ACT.Square).then_inc(squared, 1)
            act.wait_ge(var_ready, 1)
            act.activation(st[:, 2, :], st[:, 1, :], ACT.Sqrt).then_inc(root, 1)

        @block.sync
        def _(sp):
            if store:
                sp.wait_ge(h_ready, 1)
                sp.dma_start(T.h_table.rearrange("(t p) f -> p t f", p=P), T.H[:, :, :]).then_inc(stored, 16)
                sp.wait_ge(stored, 16)


def pipeline(eng, step, drain=()):
    step(0, 0)
    step(1, 1)
    with eng.Fori(0, (GROUPS - 2) // 2) as i:
        step(2 * i + 2, 0)
        step(2 * i + 3, 1)
    for g in drain:
        step(g, g % 2)


assert GROUPS % 2 == 0


GATHERED = 16 * G * (GROUPS // 2)


def wait_gathers(eng, T, n, g, s):
    if isinstance(g, int):
        eng.wait_ge(T.gathered[s], n * GATHERED + 16 * G * (g // 2 + 1))
    else:
        eng.wait_ge(T.gathered[s], (g - s) * (8 * G) + (n * GATHERED + 16 * G))


def load_tiles(nc, eng, T, g):
    code = nc.s_assert_within(eng.value_load(T.tile_codes[0:1, bass.ds(g, 1)]), 0, (1 << CODE * G) - 1,
                              skip_runtime_bounds_check_because="setup packs G numbers of CODE bits")
    return [nc.s_assert_within(eng.snap((code >> (CODE * k)) & ((1 << CODE) - 1)), 0, TILES - 1,
                               skip_runtime_bounds_check_because="they are numbers of tiles") for k in range(G)]


def past(g, k):
    return not isinstance(g, int) or g >= k


def within(g):
    return not isinstance(g, int) or g < GROUPS


def edge_mlp_pass(nc, A, T):
    with ExitStack() as ctx:
        sb, ps, sem = stack(nc, ctx, "edge_mlp_pass_")
        we1 = sb("we1", [EF, D])
        be1 = sb("be1", [D, 1])
        we2 = sb("we2", [D, D])
        be2 = sb("be2", [1, D])
        one = sb("one", [1, P])
        attr = sb("attr_sb", [P, 2, G, P])
        attr_t = sb("attr_t", [EF, 2, G * P])
        hid = sb("hid", [P, 2, G * P])
        idx = sb("idx", [P, 2, G], I32)
        hx = sb("hx", [P, 2, G, D])
        oh = sb("oh", [P, 2, G, P])
        msg = sb("msg", [P, 2, G, D])
        p_at = [ps(f"p_at{i}", [P, 512]) for i in range(2)]
        p_h = [ps(f"p_h{i}", [P, 512]) for i in range(2)]
        p_w = [ps(f"p_w{i}", [P, G, D]) for i in range(2)]
        p_a = [ps(f"p_a{i}", [P, G, D]) for i in range(2)]
        params, set_up, attr_zero = sem("l0_params"), sem("l0_set_up"), sem("l0_attr_zero")
        attr_in = [sem(f"l0_attr_in{i}") for i in range(2)]
        attr_turned, attr_kept, hidden, acted = sem("l0_attr_turned"), sem("l0_attr_kept"), sem("l0_hidden"), sem("l0_acted")
        weighed, messages, summed = sem("l0_weighed"), sem("l0_messages"), sem("l0_summed")
        idx_ready, onehots, opened = sem("l0_idx_ready"), sem("l0_onehots"), sem("l0_opened")
        added = sem("l0_added")
        block = ctx.enter_context(nc.Block())
        chunks = T.attr.rearrange("(c p) f -> c p f", p=P)

        @block.sync
        def _(sp):
            sp.dma_start(we1[:, :], A["L0_gnn_We1"]).then_inc(params, 16)
            sp.dma_start(be1[:, :], A["L0_gnn_be1"].rearrange("(p o) -> p o", o=1)).then_inc(params, 16)
            sp.dma_start(we2[:, :], A["L0_gnn_We2"]).then_inc(params, 16)
            sp.dma_start(be2[:, :], A["L0_gnn_be2"].rearrange("(o f) -> o f", o=1)).then_inc(params, 16)
            sp.wait_ge(attr_zero, 1)

            def step(g, s):
                sp.wait_ge(attr_turned, g + 1)
                for k, tile in enumerate(load_tiles(nc, sp, T, g)):
                    chunk = nc.s_assert_within(sp.snap(g * G + k - tile), 0, VISITS - TILES,
                                               skip_runtime_bounds_check_because="a visit's number is its chunk plus its tile")
                    sp.dma_start(attr[:, s, k, 0:EF], chunks[bass.ds(chunk, 1)].rearrange("c p f -> (c p) f")).then_inc(attr_in[s], 16)

            pipeline(sp, step)

        @block.gpsimd
        def _(pool):
            bound = pool.to_reg(NP - 1)

            def step(g, s):
                pool.wait_ge(idx_ready, g + 3)
                pool.wait_ge(messages, g + 1)
                pool.sem_inc(opened, 1)
                for k in range(G):
                    pool.indirect_dma_start(out=hx[:, s, k, :], out_offset=None, in_=T.h_table,
                                            in_offset=bass.IndirectOffsetOnAxis(ap=idx[:, s, k:k + 1].bitcast(U32), axis=0),
                                            bounds_check=bound).then_inc(T.gathered[s], 16)

            pipeline(pool, step)

        @block.scalar
        def _(act):
            act.sem_inc(idx_ready, 2)
            act.sem_inc(attr_kept, 2)
            act.sem_inc(acted, 2)
            act.wait_ge(params, 64)

            def step(g, s):
                act.wait_ge(messages, g + 1)
                act.activation(idx[:, s, :], T.src[:, bass.ds(g * G, G)], ACT.Copy).then_inc(idx_ready, 1)
                act.wait_ge(attr_turned, g + 3)
                act.wait_ge(hidden, g + 1)
                act.activation(attr_t[:, s, :], p_at[s][0:EF, :], ACT.Copy).then_inc(attr_kept, 1)
                act.wait_ge(hidden, g + 3)
                act.wait_ge(weighed, g + 1)
                act.activation(hid[:, s, :], p_h[s][:, :], ACT.Silu, bias=be1[:, 0:1]).then_inc(acted, 1)

            pipeline(act, step)

        @block.tensor
        def _(pe):
            for q in (attr_turned, hidden, weighed, summed):
                pe.sem_inc(q, 2)
            pe.wait_ge(params, 64)
            pe.wait_ge(set_up, 2)

            def weigh(g, s):
                pe.wait_ge(acted, g + 3)
                pe.wait_ge(messages, g + 1)
                for k in range(G):
                    pe.matmul(p_w[s][:, k, :], hid[:, s, k * P:(k + 1) * P], we2[:, :], start=True, stop=False)
                    mm = pe.matmul(p_w[s][:, k, :], one[:, :], be2[:, :], start=False, stop=True)
                mm.then_inc(weighed, 1)

            def scatter(g, s):
                pe.wait_ge(messages, g + 3)
                pe.wait_ge(onehots, g + 3)
                if past(g, 2):
                    pe.wait_ge(added, (g - 1) * G + 1)
                for k in range(G):
                    mm = pe.matmul(p_a[s][:, k, :], oh[:, s, k, :], msg[:, s, k, :], start=True, stop=True)
                mm.then_inc(summed, 1)

            def step(g, s):
                if within(g):
                    if isinstance(g, int):
                        pe.wait_ge(attr_in[s], 16 * G * (g // 2 + 1))
                    else:
                        pe.wait_ge(attr_in[s], (g - s) * (8 * G) + 16 * G)
                    pe.wait_ge(attr_kept, g + 1)
                    for k in range(G):
                        tr = pe.transpose(p_at[s][:, k * P:(k + 1) * P], attr[:, s, k, :], T.ident[:, :])
                    tr.then_inc(attr_turned, 1)
                if past(g, 1):
                    weigh(g - 1, 1 - s)
                if within(g):
                    pe.wait_ge(attr_kept, g + 3)
                    pe.wait_ge(acted, g + 1)
                    pe.matmul(p_h[s][:, :], we1[:, :], attr_t[:, s, :], start=True, stop=True).then_inc(hidden, 1)
                if past(g, 1):
                    scatter(g - 1, 1 - s)

            pipeline(pe, step, drain=(GROUPS,))

        @block.vector
        def _(dve):
            dve.sem_inc(messages, 2)
            dve.sem_inc(onehots, 2)
            dve.sem_inc(added, 1)
            dve.memset(attr[:, :, :, :], 0.0).then_inc(attr_zero, 1)
            dve.memset(one[:, :], 1.0).then_inc(set_up, 1)
            dve.memset(T.agg[:, :, :], 0.0).then_inc(set_up, 1)
            dve.wait_ge(set_up, 2)

            def step(g, s):
                if within(g):
                    dve.wait_ge(summed, g + 1)
                    dve.tensor_tensor(oh[:, s, :, :], T.iota[:, :].unsqueeze(1).to_broadcast([P, G, P]),
                                      T.rel[:, bass.ds(g * G, G)].unsqueeze(2).to_broadcast([P, G, P]),
                                      ALU.is_equal).then_inc(onehots, 1)
                if past(g, 1) and within(g - 1):
                    h, q = g - 1, 1 - s
                    wait_gathers(dve, T, 0, h, q)
                    dve.wait_ge(weighed, h + 3)
                    dve.wait_ge(summed, h + 1)
                    dve.tensor_tensor(msg[:, q, :, :], hx[:, q, :, :], p_w[q][:, :, :], ALU.mult).then_inc(messages, 1)
                if past(g, 2):
                    h = g - 2
                    dve.wait_ge(summed, h + 3)
                    for k, t in enumerate(load_tiles(nc, dve, T, h)):
                        into = T.agg[:, bass.ds(t, 1), 0:D].rearrange("p t f -> p (t f)")
                        dve.wait_ge(added, h * G + k + 1)
                        dve.tensor_tensor(into, into, p_a[s][:, k, :], ALU.add).then_inc(added, 1)

            pipeline(dve, step, drain=(GROUPS, GROUPS + 1))


def node_mlp(nc, A, T):
    with ExitStack() as ctx:
        sb, ps, sem = stack(nc, ctx, "node_mlp_")
        w1, b1, w2, b2 = sb("wn1", [D, D]), sb("bn1", [D, 1]), sb("wn2", [D, D]), sb("bn2", [1, D])
        one = sb("one_n0", [1, P])
        agg_t, hid = sb("agg_t", [P, 2, 512]), sb("hid_n0", [P, 2, 512])
        p_t = [ps(f"p_t{i}", [P, 512]) for i in range(2)]
        p_h = [ps(f"p_h{i}", [P, 512]) for i in range(2)]
        p_o = [ps(f"p_o{i}", [P, 4, D]) for i in range(2)]
        params, set_up, chain = sem("n0_params"), sem("n0_set_up"), sem("n0_chain")
        turned, kept, hidden, acted, made, taken = (sem("n0_" + n) for n in ("turned", "kept", "hidden", "acted", "made", "taken"))
        block = ctx.enter_context(nc.Block())

        @block.sync
        def _(sp):
            sp.dma_start(w1[:, :], A["L0_gnn_Wn1"]).then_inc(params, 16)
            sp.dma_start(b1[:, :], A["L0_gnn_bn1"].rearrange("(p o) -> p o", o=1)).then_inc(params, 16)
            sp.dma_start(w2[:, :], A["L0_gnn_Wn2"]).then_inc(params, 16)
            sp.dma_start(b2[:, :], A["L0_gnn_bn2"].rearrange("(o f) -> o f", o=1)).then_inc(params, 16)

        @block.tensor
        def _(pe):
            def out(b):
                t0, n = BLOCKS[b]
                pe.wait_ge(acted, b + 1)
                if b >= 2:
                    pe.wait_ge(taken, b - 1)
                for k in range(n):
                    pe.matmul(p_o[b % 2][:, k, :], hid[:, b % 2, k * P:(k + 1) * P], w2[:, :], start=True, stop=False)
                    mm = pe.matmul(p_o[b % 2][:, k, :], one[:, :], b2[:, :], start=False, stop=True)
                mm.then_inc(made, 1)

            pe.wait_ge(set_up, 1)
            for b, (t0, n) in enumerate(BLOCKS):
                if b >= 2:
                    pe.wait_ge(kept, b - 1)
                for k in range(n):
                    tr = pe.transpose(p_t[b % 2][:, k * P:(k + 1) * P], T.agg[:, t0 + k, 0:D], T.ident[:, :])
                tr.then_inc(turned, 1)
                if b == 0:
                    pe.wait_ge(params, 64)
                else:
                    out(b - 1)
                pe.wait_ge(kept, b + 1)
                if b >= 2:
                    pe.wait_ge(acted, b - 1)
                pe.matmul(p_h[b % 2][:, 0:n * P], w1[:, :], agg_t[:, b % 2, 0:n * P], start=True, stop=True).then_inc(hidden, 1)
            out(len(BLOCKS) - 1)

        @block.scalar
        def _(act):
            act.wait_ge(params, 64)
            for b, (t0, n) in enumerate(BLOCKS):
                act.wait_ge(turned, b + 1)
                if b >= 2:
                    act.wait_ge(hidden, b - 1)
                act.activation(agg_t[:, b % 2, 0:n * P], p_t[b % 2][:, 0:n * P], ACT.Copy).then_inc(kept, 1)
                act.wait_ge(hidden, b + 1)
                if b >= 2:
                    act.wait_ge(made, b - 1)
                act.activation(hid[:, b % 2, 0:n * P], p_h[b % 2][:, 0:n * P], ACT.Silu, bias=b1[:, 0:1]).then_inc(acted, 1)

        @block.vector
        def _(dve):
            then = Chain(dve, chain)
            dve.memset(one[:, :], 1.0).then_inc(set_up, 1)
            then(dve.tensor_tensor(T.X[:, :, :], T.X[:, :, :], T.H[:, :, :], ALU.add))
            for b, (t0, n) in enumerate(BLOCKS):
                dve.wait_ge(made, b + 1)
                dve.tensor_tensor(T.X[:, t0:t0 + n, :], T.X[:, t0:t0 + n, :], p_o[b % 2][:, 0:n, :], ALU.add).then_inc(taken, 1)


class AggInPsum:

    def __init__(self, sb, ps, sem):
        self.sums = ps("sums", [P, TBANKS * 4, D])
        self.nil = sb("nil", [P, 512], BF16)
        self.nil_ready, self.closed = sem("nil_ready"), sem("sums_closed")

    def clear(self, dve):
        dve.memset(self.nil[:, :], 0.0).then_inc(self.nil_ready, 1)

    def sweep(self, pe, first):
        if first:
            pe.wait_ge(self.nil_ready, 1)
        for b in range(TBANKS):
            mm = pe.matmul(self.sums[:, 4 * b:4 * b + 4, :], self.nil[:, 0:P], self.nil[:, :],
                           start=first, stop=not first, skip_group_check=True)
        if not first:
            mm.then_inc(self.closed, 1)

    def add(self, pe, tile, onehot, rows):
        return pe.matmul(self.sums[:, bass.ds(tile, 1), :].rearrange("p t f -> p (t f)"), onehot, rows,
                         start=False, stop=False, skip_group_check=True)

    def store(self, dve, T):
        dve.wait_ge(self.closed, 1)
        for b, (t0, n) in enumerate(BLOCKS):
            dve.tensor_copy(T.agg[:, t0:t0 + n, 0:D], self.sums[:, t0:t0 + n, :])


def sum_pass(nc, A, T):
    with ExitStack() as ctx:
        sb, ps, sem = stack(nc, ctx, "sum_pass_")
        idx = sb("idx1", [P, 2, G], I32)
        hx = sb("hx1", [P, 2, G, D])
        oh = sb("oh1", [P, 2, G, P])
        agg = AggInPsum(sb, ps, sem)
        summed, idx_ready, onehots = sem("l1_summed"), sem("l1_idx_ready"), sem("l1_onehots")
        opened = sem("l1_opened")
        block = ctx.enter_context(nc.Block())

        @block.gpsimd
        def _(pool):
            bound = pool.to_reg(NP - 1)

            def step(g, s):
                pool.wait_ge(idx_ready, g + 3)
                pool.wait_ge(summed, g + 1)
                pool.sem_inc(opened, 1)
                for k in range(G):
                    pool.indirect_dma_start(out=hx[:, s, k, :], out_offset=None, in_=T.h_table,
                                            in_offset=bass.IndirectOffsetOnAxis(ap=idx[:, s, k:k + 1].bitcast(U32), axis=0),
                                            bounds_check=bound).then_inc(T.gathered[s], 16)

            pipeline(pool, step)

        @block.scalar
        def _(act):
            act.sem_inc(idx_ready, 2)

            def step(g, s):
                act.wait_ge(summed, g + 1)
                act.activation(idx[:, s, :], T.src[:, bass.ds(g * G, G)], ACT.Copy).then_inc(idx_ready, 1)

            pipeline(act, step)

        @block.tensor
        def _(pe):
            pe.sem_inc(summed, 2)
            agg.sweep(pe, True)

            def step(g, s):
                tiles = load_tiles(nc, pe, T, g)
                pe.wait_ge(onehots, g + 3)
                wait_gathers(pe, T, 1, g, s)
                for k in range(G):
                    mm = agg.add(pe, tiles[k], oh[:, s, k, :], hx[:, s, k, :])
                mm.then_inc(summed, 1)

            pipeline(pe, step)
            agg.sweep(pe, False)

        @block.vector
        def _(dve):
            dve.sem_inc(onehots, 2)
            agg.clear(dve)

            def step(g, s):
                dve.wait_ge(summed, g + 1)
                dve.tensor_tensor(oh[:, s, :, :], T.iota[:, :].unsqueeze(1).to_broadcast([P, G, P]),
                                  T.rel[:, bass.ds(g * G, G)].unsqueeze(2).to_broadcast([P, G, P]),
                                  ALU.is_equal).then_inc(onehots, 1)

            pipeline(dve, step)
            agg.store(dve, T)


class Batchnorm:

    def __init__(self, sb, sem, name, Y):
        self.Y, self.sq = Y, sb(name + "_sq", [P, N])
        self.st, self.gb = sb(name + "_st", [P, 6]), sb(name + "_gb", [P, 2])
        self.centred, self.squared, self.var_ready, self.root, self.scaled, self.done, self.params = (
            sem(name + n) for n in ("_centred", "_squared", "_var", "_root", "_scaled", "_done", "_gb_in"))

    def load(self, sp, gamma, beta):
        sp.dma_start(self.gb[:, 0:1], gamma.rearrange("(p o) -> p o", o=1)).then_inc(self.params, 16)
        sp.dma_start(self.gb[:, 1:2], beta.rearrange("(p o) -> p o", o=1)).then_inc(self.params, 16)

    def on_vector(self, dve, then):
        st, Y = self.st, self.Y
        then(dve.tensor_reduce(st[:, 0:1], Y[:, 0:N], AX.X, ALU.add))
        then(dve.tensor_scalar(st[:, 0:1], st[:, 0:1], 1.0 / N, None, ALU.mult))
        dve.tensor_scalar(Y[:, :], Y[:, :], st[:, 0:1], None, ALU.subtract).then_inc(self.centred, 1)
        dve.wait_ge(self.squared, 1)
        then(dve.tensor_reduce(st[:, 1:2], self.sq[:, :], AX.X, ALU.add))
        dve.tensor_scalar(st[:, 1:2], st[:, 1:2], 1.0 / N, EPS, ALU.mult, ALU.add).then_inc(self.var_ready, 1)
        dve.wait_ge(self.root, 1)
        then(dve.reciprocal(st[:, 3:4], st[:, 2:3]))
        dve.wait_ge(self.params, 32)
        dve.tensor_tensor(st[:, 4:5], st[:, 3:4], self.gb[:, 0:1], ALU.mult).then_inc(self.scaled, 1)

    def on_scalar(self, act, func):
        st, Y = self.st, self.Y
        act.wait_ge(self.centred, 1)
        act.activation(self.sq[:, :], Y[:, 0:N], ACT.Square).then_inc(self.squared, 1)
        act.wait_ge(self.var_ready, 1)
        act.activation(st[:, 2:3], st[:, 1:2], ACT.Sqrt).then_inc(self.root, 1)
        act.wait_ge(self.scaled, 1)
        act.activation(Y[:, :], Y[:, :], func, bias=self.gb[:, 1:2], scale=st[:, 4:5]).then_inc(self.done, 1)


def node_gin(nc, A, T):
    with ExitStack() as ctx:
        sb, ps, sem = stack(nc, ctx, "node_gin_")
        w1, w2 = sb("w1", [D, D]), sb("w2", [D, D])
        bias = sb("bias_n1", [P, 3])
        Z, Y = sb("Z", [P, TILES, D]), sb("Y", [P, NP])
        in_t, hid = sb("in_t", [P, 2, 512]), sb("hid_n1", [P, 2, 512])
        p_t = [ps(f"p_t{i}", [P, 512]) for i in range(2)]
        p_h = [ps(f"p_h{i}", [P, 512]) for i in range(2)]
        p_y = [ps(f"p_y{i}", [P, 512]) for i in range(2)]
        p_b = [ps(f"p_b{i}", [P, 4, D]) for i in range(2)]
        params, chain, z_ready = sem("n1_params"), sem("n1_chain"), sem("n1_z_ready")
        turned, kept, hidden, acted, made, y_ready, back, taken = (
            sem("n1_" + n) for n in ("turned", "kept", "hidden", "acted", "made", "y_ready", "back", "taken"))
        bn = Batchnorm(sb, sem, "bn1_", Y)
        block = ctx.enter_context(nc.Block())
        NB = len(BLOCKS)

        @block.sync
        def _(sp):
            sp.dma_start(bias[:, 2:3], A["L1_gnn_eps"].partition_broadcast(P)).then_inc(params, 16)
            sp.dma_start(w1[:, :], A["L1_gnn_W1"]).then_inc(params, 16)
            sp.dma_start(w2[:, :], A["L1_gnn_W2"]).then_inc(params, 16)
            sp.dma_start(bias[:, 0:1], A["L1_gnn_b1"].rearrange("(p o) -> p o", o=1)).then_inc(params, 16)
            sp.dma_start(bias[:, 1:2], A["L1_gnn_b2"].rearrange("(p o) -> p o", o=1)).then_inc(params, 16)
            bn.load(sp, A["L1_gnn_gamma"], A["L1_gnn_beta"])

        @block.tensor
        def _(pe):
            pe.wait_ge(z_ready, 1)
            pe.wait_ge(params, 80)
            for b, (t0, n) in enumerate(BLOCKS):
                if b >= 2:
                    pe.wait_ge(kept, b - 1)
                for k in range(n):
                    tr = pe.transpose(p_t[b % 2][:, k * P:(k + 1) * P], Z[:, t0 + k, :], T.ident[:, :])
                tr.then_inc(turned, 1)
                pe.wait_ge(kept, b + 1)
                if b >= 2:
                    pe.wait_ge(acted, b - 1)
                pe.matmul(p_h[b % 2][:, 0:n * P], w1[:, :], in_t[:, b % 2, 0:n * P], start=True, stop=True).then_inc(hidden, 1)
                pe.wait_ge(acted, b + 1)
                if b >= 2:
                    pe.wait_ge(y_ready, b - 1)
                pe.matmul(p_y[b % 2][:, 0:n * P], w2[:, :], hid[:, b % 2, 0:n * P], start=True, stop=True).then_inc(made, 1)
            pe.wait_ge(bn.done, 1)
            for b, (t0, n) in enumerate(BLOCKS):
                if b >= 2:
                    pe.wait_ge(taken, b - 1)
                for k in range(n):
                    tr = pe.transpose(p_b[b % 2][:, k, :], Y[:, (t0 + k) * P:(t0 + k + 1) * P], T.ident[:, :])
                tr.then_inc(back, 1)

        @block.scalar
        def _(act):
            act.wait_ge(params, 80)
            for b, (t0, n) in enumerate(BLOCKS):
                act.wait_ge(turned, b + 1)
                if b >= 2:
                    act.wait_ge(hidden, b - 1)
                act.activation(in_t[:, b % 2, 0:n * P], p_t[b % 2][:, 0:n * P], ACT.Copy).then_inc(kept, 1)
                act.wait_ge(hidden, b + 1)
                if b >= 2:
                    act.wait_ge(made, b - 1)
                act.activation(hid[:, b % 2, 0:n * P], p_h[b % 2][:, 0:n * P], ACT.Relu, bias=bias[:, 0:1]).then_inc(acted, 1)
                act.wait_ge(made, b + 1)
                act.activation(Y[:, t0 * P:(t0 + n) * P], p_y[b % 2][:, 0:n * P], ACT.Identity, bias=bias[:, 1:2]).then_inc(y_ready, 1)
            bn.on_scalar(act, ACT.Relu)

        @block.vector
        def _(dve):
            then = Chain(dve, chain)
            dve.wait_ge(params, 80)
            then(dve.tensor_scalar(bias[:, 2:3], bias[:, 2:3], 1.0, None, ALU.add))
            dve.scalar_tensor_tensor(out=Z[:, :, :], in0=T.H[:, :, :], scalar=bias[:, 2:3], in1=T.agg[:, :, 0:D],
                                     op0=ALU.mult, op1=ALU.add).then_inc(z_ready, 1)
            dve.wait_ge(y_ready, NB)
            bn.on_vector(dve, then)
            for b, (t0, n) in enumerate(BLOCKS):
                dve.wait_ge(back, b + 1)
                dve.tensor_tensor(T.X[:, t0:t0 + n, :], T.X[:, t0:t0 + n, :], p_b[b % 2][:, 0:n, :], ALU.add).then_inc(taken, 1)


def scan_flags(nc, A, T):
    with ExitStack() as ctx:
        sb, ps, sem = stack(nc, ctx, "scan_flags_")
        keys = sb("keys", [P, LE + 2])
        shift = sb("shift", [P, 2, P])
        whole = sb("whole", [P, 2])
        nti, nbi = sb("nti", [TILES, P], I32), sb("nbi", [P, NP], I32)
        ntf = sb("ntf", [TILES, P])
        typed = sem("typed")
        p_k = [ps(f"p_k{i}", [P, 4, P]) for i in range(2)]
        p_e, p_r = ps("p_e", [P, 512]), ps("p_r", [P, 512])
        chain, turned, taken, shifts, edges, set_up = (sem("fl_" + n) for n in ("chain", "turned", "taken", "shifts", "edges", "set_up"))
        wholes, rows, types_in = sem("fl_wholes"), sem("fl_rows"), sem("fl_types_in")
        block = ctx.enter_context(nc.Block())
        spread = sem("spread")
        lanes = T.att[:, :, :].rearrange("p v h -> p (v h)").rearrange("p (j l h) -> p j l h", l=LANES, h=HEADS)
        quads = [(j, min(4, LV - j)) for j in range(0, LV, 4)]

        @block.sync
        def _(sp):
            full = N // P
            sp.wait_ge(set_up, 2)
            nt = A["node_type_8"]
            sp.dma_start(nti[0:full, :], nt[0:full * P].rearrange("(t p) -> t p", p=P)).then_inc(types_in, 16)
            sp.dma_start(nti[full:full + 1, 0:N - full * P], nt[full * P:N].rearrange("(o p) -> o p", o=1)).then_inc(types_in, 16)
            sp.dma_start(nbi[:, 0:N], nt.partition_broadcast(P)).then_inc(types_in, 16)

        @block.gpsimd
        def _(pool):
            pool.memset(shift[:, :, :], 0.0).then_inc(shifts, 1)
            pool.wait_ge(shifts, 1)
            pool.affine_select(out=shift[:, 0, :], in_=shift[:, 0, :], compare_op=ALU.not_equal, fill=1.0, base=HEADS,
                               pattern=[[-1, P]], channel_multiplier=1).then_inc(shifts, 1)
            pool.affine_select(out=shift[:, 1, :], in_=shift[:, 1, :], compare_op=ALU.not_equal, fill=1.0, base=-HEADS,
                               pattern=[[-1, P]], channel_multiplier=1).then_inc(shifts, 1)

        @block.tensor
        def _(pe):
            pe.wait_ge(spread, 1)
            for b, (j, n) in enumerate(quads):
                if b >= 2:
                    pe.wait_ge(taken, b - 1)
                for k in range(n):
                    tr = pe.transpose(p_k[b % 2][:, k, :], lanes[:, j + k].rearrange("p l h -> p (l h)"), T.ident[:, :])
                tr.then_inc(turned, 1)
            pe.wait_ge(taken, len(quads))
            pe.wait_ge(shifts, 3)
            pe.matmul(p_e[:, 0:1], shift[:, 0, :], keys[:, LE:LE + 1], start=True, stop=True)
            pe.matmul(p_e[:, 1:2], shift[:, 1, :], keys[:, 1:2], start=True, stop=True).then_inc(edges, 1)
            pe.wait_ge(wholes, 1)
            pe.transpose(p_r[0:1, 0:P], whole[:, 0:1], T.ident[:, :])
            pe.transpose(p_r[0:1, P:2 * P], whole[:, 1:2], T.ident[:, :]).then_inc(rows, 1)
            pe.wait_ge(typed, 1)
            pe.transpose(p_e[:, 2:2 + TILES], ntf[:, :], T.ident[0:TILES, 0:TILES]).then_inc(rows, 1)

        @block.vector
        def _(dve):
            then = Chain(dve, chain)
            dve.memset(nti[:, :], -1).then_inc(set_up, 1)
            dve.memset(nbi[:, :], -1).then_inc(set_up, 1)
            dve.tensor_copy(lanes, T.key[:, 0:SV].rearrange("p (l j) -> p j l", j=LV).unsqueeze(3).to_broadcast([P, LV, LANES, HEADS])).then_inc(spread, 1)
            for b, (j, n) in enumerate(quads):
                dve.wait_ge(turned, b + 1)
                dve.tensor_copy(keys[:, 1 + j * P:1 + (j + n) * P], p_k[b % 2][:, 0:n, :].rearrange("p k e -> p (k e)")).then_inc(taken, 1)
            dve.wait_ge(edges, 1)
            then(dve.tensor_copy(keys[:, 0:1], p_e[:, 0:1]))
            then(dve.tensor_copy(keys[:, LE + 1:LE + 2], p_e[:, 1:2]))
            then(dve.tensor_tensor(T.flag[:, :], keys[:, 1:LE + 2], keys[:, 0:LE + 1], ALU.not_equal))
            then(dve.tensor_scalar(T.flag[:, :], T.flag[:, :], -BIG, None, ALU.mult))
            then(dve.tensor_reduce(whole[:, 0:1], T.flag[:, 0:LE], AX.X, ALU.min))
            then(dve.tensor_reduce(whole[:, 1:2], T.flag[:, 1:LE + 1], AX.X, ALU.min))
            dve.sem_inc(wholes, 1)
            dve.wait_ge(rows, 1)
            dve.tensor_copy(T.whole[:, :, :], p_r[0:1, 0:2 * P].rearrange("o (k p) -> o k p", k=2))
            dve.wait_ge(types_in, 48)
            dve.tensor_copy(ntf[:, :], nti[:, :]).then_inc(typed, 1)
            dve.wait_ge(rows, 2)
            dve.tensor_copy(T.type_of[:, :], p_e[:, 2:2 + TILES])
            dve.tensor_copy(T.type_row[:, :], nbi[:, :])
            dve.memset(T.att[:, VISITS:SV, :], 0.0)


def typed_qkv(nc, A, T, l):
    with ExitStack() as ctx:
        sb, ps, sem = stack(nc, ctx)
        nm = f"qkv{l}_"
        w = [sb(f"{nm}w{k}", [D, TYPES, D]) for k in range(3)]
        bd = [sb(f"{nm}bd{k}", [D, REL, D]) for k in range(2)]
        pri = sb(nm + "pri", [P, REL])
        e_t = sb(nm + "e_t", [P, 512])
        xm = sb(nm + "xm", [P, TYPES, 512])
        kv_t = sb(nm + "kv_t", [P, 2, 512])
        rows = sb(nm + "rows", [P, 2, REL, 2, D])
        p_t, p_q = ps(nm + "p_t", [P, 512]), ps(nm + "p_q", [P, 4, D])
        p_kv = [ps(f"{nm}p_kv{k}", [P, 512]) for k in range(2)]
        p_r = [ps(f"{nm}p_r{k}", [P, 4, D]) for k in range(4)]
        params, zeroed, chain, bd_ready = (sem(nm + n) for n in ("params", "zeroed", "chain", "bd_ready"))
        turned, kept, masked, projected, cast, q_made, q_kept = (
            sem(nm + n) for n in ("turned", "kept", "masked", "projected", "cast", "q_made", "q_kept"))
        related = sem(nm + "related")
        by_act, by_dve = sem(nm + "by_act"), sem(nm + "by_dve")
        stored = [sem(f"{nm}stored{i}") for i in range(2)]
        block = ctx.enter_context(nc.Block())
        table = T.kv_table.rearrange("(n r) (c f) -> n r c f", r=REL, f=D)

        @block.sync
        def _(sp):
            for k, name in enumerate(("Wk", "Wv", "Wq")):
                sp.dma_start(w[k][:, :, :], A["L2_gnn_" + name][l].rearrange("t i o -> i t o")).then_inc(params, 16)
            sp.wait_ge(zeroed, 2)
            for h in range(HEADS):
                of = slice(h * HS, (h + 1) * HS)
                sp.dma_start(bd[0][of, :, of], A["L2_gnn_Watt"][l, h].rearrange("r i o -> i r o")).then_inc(params, 16)
                sp.dma_start(bd[1][of, :, of], A["L2_gnn_Wmsg"][l, h].rearrange("r i o -> i r o")).then_inc(params, 16)
                sp.dma_start(pri[of, :], A["L2_gnn_pri"][l, h].partition_broadcast(HS)).then_inc(params, 16)
            for t in range(TILES):
                sp.wait_ge(by_act, 2 * (t + 1))
                sp.wait_ge(by_dve, 2 * (t + 1))
                sp.dma_start(table[t * P:(t + 1) * P], rows[:, t % 2]).then_inc(stored[t % 2], 16)
            sp.wait_ge(stored[0], 16 * ((TILES + 1) // 2))
            sp.wait_ge(stored[1], 16 * (TILES // 2))

        @block.tensor
        def _(pe):
            pe.wait_ge(params, 16 * (3 + 3 * HEADS))
            for b, (t0, n) in enumerate(BLOCKS):
                if b >= 1:
                    pe.wait_ge(kept, b)
                for k in range(n):
                    tr = pe.transpose(p_t[:, k * P:(k + 1) * P], T.H[:, t0 + k, :], T.ident[:, :])
                tr.then_inc(turned, 1)
                pe.wait_ge(masked, b + 1)
                for c in range(2):
                    if b >= 1:
                        pe.wait_ge(cast, 2 * b - 1 + c)
                    for t in range(TYPES):
                        mm = pe.matmul(p_kv[c][:, 0:n * P], w[c][:, t, :], xm[:, t, 0:n * P], start=(t == 0), stop=(t == TYPES - 1))
                    mm.then_inc(projected, 1)
                if b >= 1:
                    pe.wait_ge(q_kept, b)
                for k in range(n):
                    for t in range(TYPES):
                        mm = pe.matmul(p_q[:, k, :], xm[:, t, k * P:(k + 1) * P], w[2][:, t, :], start=(t == 0), stop=(t == TYPES - 1))
                mm.then_inc(q_made, 1)
                pe.wait_ge(cast, 2 * (b + 1))
                pe.wait_ge(bd_ready, 1)
                for k in range(n):
                    t = t0 + k
                    for c in range(2):
                        for half in range(2):
                            if t >= 1:
                                pe.wait_ge(by_dve if c else by_act, 2 * t - 1 + half)
                            pe.matmul(p_r[2 * c + half][:, :, :], kv_t[:, c, k * P:(k + 1) * P],
                                      bd[c][:, 4 * half:4 * half + 4, :], start=True, stop=True).then_inc(related, 1)

        @block.scalar
        def _(act):
            for b, (t0, n) in enumerate(BLOCKS):
                act.wait_ge(turned, b + 1)
                if b >= 1:
                    act.wait_ge(masked, b)
                act.activation(e_t[:, 0:n * P], p_t[:, 0:n * P], ACT.Copy).then_inc(kept, 1)
                for c in range(2):
                    act.wait_ge(projected, 2 * b + c + 1)
                    if b >= 1:
                        act.wait_ge(related, 4 * t0)
                    act.activation(kv_t[:, c, 0:n * P], p_kv[c][:, 0:n * P], ACT.Copy).then_inc(cast, 1)
                act.wait_ge(q_made, b + 1)
                act.activation(T.Q[:, t0:t0 + n, :], p_q[:, 0:n, :], ACT.Copy).then_inc(q_kept, 1)
                for k in range(n):
                    t = t0 + k
                    if t >= 2:
                        act.wait_ge(stored[t % 2], 16 * (t // 2))
                    for half in range(2):
                        act.wait_ge(related, 4 * t + half + 1)
                        act.activation(rows[:, t % 2, 4 * half:4 * half + 4, 0, :], p_r[half][:, :, :], ACT.Copy).then_inc(by_act, 1)

        @block.vector
        def _(dve):
            then = Chain(dve, chain)
            for c in range(2):
                dve.memset(bd[c][:, :, :], 0.0).then_inc(zeroed, 1)
            dve.wait_ge(params, 16 * (3 + 3 * HEADS))
            then(dve.tensor_scalar(pri[:, :], pri[:, :], 1.0 / float(HS) ** 0.5, None, ALU.mult))
            dve.tensor_tensor(bd[0][:, :, :], bd[0][:, :, :], pri[:, :].unsqueeze(2).to_broadcast([P, REL, D]), ALU.mult).then_inc(bd_ready, 1)
            for b, (t0, n) in enumerate(BLOCKS):
                dve.wait_ge(kept, b + 1)
                if b >= 1:
                    dve.wait_ge(q_made, b)
                for t in range(TYPES):
                    ins = dve.scalar_tensor_tensor(out=xm[:, t, 0:n * P], in0=T.type_row[:, t0 * P:(t0 + n) * P], scalar=float(t),
                                                   in1=e_t[:, 0:n * P], op0=ALU.is_equal, op1=ALU.mult)
                ins.then_inc(masked, 1)
                for k in range(n):
                    t = t0 + k
                    if t >= 2:
                        dve.wait_ge(stored[t % 2], 16 * (t // 2))
                    for half in range(2):
                        dve.wait_ge(related, 4 * t + half + 3)
                        dve.tensor_copy(rows[:, t % 2, 4 * half:4 * half + 4, 1, :], p_r[2 + half][:, :, :]).then_inc(by_dve, 1)


def score_pass(nc, A, T, l):
    with ExitStack() as ctx:
        sb, ps, sem = stack(nc, ctx)
        nm = f"sc{l}_"
        idx = sb(nm + "idx", [P, 2, G], I32)
        kv = sb(nm + "kv", [P, 2, G, 2 * D])
        oh = sb(nm + "oh", [P, 2, G, P])
        oh_t = sb(nm + "oh_t", [P, 2, G, P])
        prod = sb(nm + "prod", [P, G, D])
        p_t = [ps(f"{nm}p_t{i}", [P, G, P]) for i in range(2)]
        p_q = [ps(f"{nm}p_q{i}", [P, G, D]) for i in range(2)]
        m_out = [sem(f"{nm}m_out{i}") for i in range(2)]
        idx_ready, onehots, turned, kept, spread, scored = (sem(nm + n) for n in ("idx_ready", "onehots", "turned", "kept", "spread", "scored"))
        opened, multiplied = sem(nm + "opened"), sem(nm + "multiplied")
        block = ctx.enter_context(nc.Block())
        m_slots = T.m_table.rearrange("(v p) f -> p v f", p=P)

        @block.sync
        def _(sp):
            def step(g, s):
                wait_gathers(sp, T, 2 + l, g, s)
                sp.dma_start(m_slots[:, bass.ds(g * G, G), :], kv[:, s, :, D:2 * D]).then_inc(m_out[s], 16)

            pipeline(sp, step)
            for s in range(2):
                sp.wait_ge(m_out[s], 16 * (GROUPS // 2 + 1))

        @block.gpsimd
        def _(pool):
            bound = pool.to_reg(NP * REL - 1)
            for s in range(2):
                pool.sem_inc(m_out[s], 16)

            def step(g, s):
                pool.wait_ge(idx_ready, g + 3)
                pool.wait_ge(scored, g + 1)
                pool.wait_ge(m_out[s], 16 * (g // 2 + 1) if isinstance(g, int) else (g - s) * 8 + 16)
                pool.sem_inc(opened, 1)
                for k in range(G):
                    pool.indirect_dma_start(out=kv[:, s, k, :], out_offset=None, in_=T.kv_table,
                                            in_offset=bass.IndirectOffsetOnAxis(ap=idx[:, s, k:k + 1].bitcast(U32), axis=0),
                                            bounds_check=bound).then_inc(T.gathered[s], 16)

            pipeline(pool, step)

        @block.scalar
        def _(act):
            act.sem_inc(idx_ready, 2)
            act.sem_inc(kept, 2)

            def step(g, s):
                act.wait_ge(scored, g + 1)
                act.activation(idx[:, s, :], T.srcrel[:, bass.ds(g * G, G)], ACT.Copy).then_inc(idx_ready, 1)
                act.wait_ge(turned, g + 3)
                act.wait_ge(spread, g + 1)
                act.activation(oh_t[:, s, :, :], p_t[s][:, :, :], ACT.Copy).then_inc(kept, 1)

            pipeline(act, step)

        @block.tensor
        def _(pe):
            pe.sem_inc(turned, 2)
            pe.sem_inc(spread, 2)

            def step(g, s):
                pe.wait_ge(onehots, g + 3)
                pe.wait_ge(kept, g + 1)
                tiles = load_tiles(nc, pe, T, g)
                for k in range(G):
                    tr = pe.transpose(p_t[s][:, k, :], oh[:, s, k, :], T.ident[:, :])
                tr.then_inc(turned, 1)
                pe.wait_ge(kept, g + 3)
                pe.wait_ge(scored, g + 1)
                for k in range(G):
                    q = T.Q[:, bass.ds(tiles[k], 1), :].rearrange("p t f -> p (t f)")
                    mm = pe.matmul(p_q[s][:, k, :], oh_t[:, s, k, :], q, start=True, stop=True)
                mm.then_inc(spread, 1)

            pipeline(pe, step)

        @block.vector
        def _(dve):
            dve.sem_inc(onehots, 2)
            dve.sem_inc(scored, 2)

            def step(g, s):
                if within(g):
                    dve.wait_ge(turned, g + 1)
                    dve.tensor_tensor(oh[:, s, :, :], T.iota[:, :].unsqueeze(1).to_broadcast([P, G, P]),
                                      T.rel[:, bass.ds(g * G, G)].unsqueeze(2).to_broadcast([P, G, P]),
                                      ALU.is_equal).then_inc(onehots, 1)
                if past(g, 1):
                    h, q = g - 1, 1 - s
                    wait_gathers(dve, T, 2 + l, h, q)
                    dve.wait_ge(spread, h + 3)
                    if past(h, 1):
                        dve.wait_ge(scored, h + 2)
                    dve.tensor_tensor(prod[:, :, :], kv[:, q, :, 0:D], p_q[q][:, :, :], ALU.mult).then_inc(multiplied, 1)
                    dve.wait_ge(multiplied, h + 1)
                    dve.tensor_reduce(T.att[:, bass.ds(h * G, G), :].rearrange("p v h -> p (v h)"),
                                      prod[:, :, :].rearrange("p k (h o) -> p (k h) o", o=HS), AX.X, ALU.add).then_inc(scored, 1)

            pipeline(dve, step, drain=(GROUPS,))


def softmax_shift(nc, A, T, l):
    with ExitStack() as ctx:
        sb, ps, sem = stack(nc, ctx)
        nm = f"mx{l}_"
        a_t, top = sb(nm + "a_t", [P, LE]), sb(nm + "top", [P, LE])
        whole_max = T.att[:, :, :].rearrange("p v h -> p (v h)")
        ends, into = sb(nm + "ends", [1, 2, P]), sb(nm + "into", [1, 2, P])
        start = sb(nm + "start", [P, 2])
        p_l = [ps(f"{nm}p_l{i}", [P, 4, P]) for i in range(3)]
        p_e, p_s = ps(nm + "p_e", [P, 512]), ps(nm + "p_s", [P, 512])
        chain, turned, by_act, by_dve, ended, row_made, carried, started = (
            sem(nm + n) for n in ("chain", "turned", "by_act", "by_dve", "ended", "row_made", "carried", "started"))
        shifted, exped, back, placed = (sem(nm + n) for n in ("shifted", "exped", "back", "placed"))
        block = ctx.enter_context(nc.Block())
        lanes = top[:, :].rearrange("p (j l h) -> p j l h", l=LANES, h=HEADS)
        ordered = sem(nm + "ordered")
        quads = [(j, min(4, LV - j)) for j in range(0, LV, 4)]
        NQ = len(quads)

        @block.tensor
        def _(pe):
            pe.wait_ge(ordered, 1)
            for b, (j, n) in enumerate(quads):
                if b >= 3:
                    pe.wait_ge(by_act, b - 2)
                for k in range(n):
                    tr = pe.transpose(p_l[b % 3][:, k, :], lanes[:, j + k].rearrange("p l h -> p (l h)"), T.ident[:, :])
                tr.then_inc(turned, 1)
            for d in range(2):
                pe.wait_ge(ended, d + 1)
                last = top[:, LE - 1:LE] if d == 0 else whole_max[:, 0:1]
                pe.transpose(p_e[0:1, d * P:(d + 1) * P], last, T.ident[:, :]).then_inc(row_made, 1)
                pe.wait_ge(carried, d + 1)
                pe.transpose(p_s[:, d:d + 1], into[0:1, d, :], T.ident[0:1, 0:1]).then_inc(started, 1)
            for b, (j, n) in enumerate(quads):
                pe.wait_ge(exped, b + 1)
                if b >= 3:
                    pe.wait_ge(placed, b - 2)
                else:
                    pe.wait_ge(by_act, NQ)
                for k in range(n):
                    tr = pe.transpose(p_l[b % 3][:, k, :], a_t[:, (j + k) * P:(j + k + 1) * P], T.ident[:, :])
                tr.then_inc(back, 1)

        @block.scalar
        def _(act):
            for b, (j, n) in enumerate(quads):
                act.wait_ge(turned, b + 1)
                act.activation(a_t[:, j * P:(j + n) * P], p_l[b % 3][:, 0:n, :].rearrange("p k e -> p (k e)"), ACT.Copy).then_inc(by_act, 1)
            act.wait_ge(shifted, 1)
            for b, (j, n) in enumerate(quads):
                act.activation(a_t[:, j * P:(j + n) * P], a_t[:, j * P:(j + n) * P], ACT.Exp).then_inc(exped, 1)

        @block.vector
        def _(dve):
            then = Chain(dve, chain)
            dve.tensor_copy(lanes, T.att[:, :, :].rearrange("p (l j) h -> p j l h", j=LV)).then_inc(ordered, 1)
            dve.wait_ge(by_act, NQ)

            def forwards(initial):
                return dve.tensor_tensor_scan(top[:, :], T.flag[:, 0:LE], a_t[:, :], initial, ALU.add, ALU.max)

            def backwards(initial):
                return dve.tensor_tensor_scan(whole_max[:, ::-1], T.flag[:, 1:LE + 1][:, ::-1], top[:, ::-1], initial, ALU.add, ALU.max)

            for d, scan in enumerate((forwards, backwards)):
                scan(-BIG).then_inc(ended, 1)
                dve.wait_ge(row_made, d + 1)
                then(dve.tensor_copy(ends[:, d, :], p_e[0:1, d * P:(d + 1) * P]))
                for h in range(HEADS):
                    def along(row):
                        v = row.rearrange("o (l h) -> o l h", h=HEADS)[:, :, h]
                        return v[:, ::-1] if d else v
                    ins = dve.tensor_tensor_scan(along(ends[:, d, :]), along(T.whole[:, d, :]), along(ends[:, d, :]), -BIG, ALU.add, ALU.max)
                    then(ins)
                then(dve.memset(into[:, d, :], -BIG))
                if d == 0:
                    dve.tensor_copy(into[:, 0, HEADS:P], ends[:, 0, 0:P - HEADS]).then_inc(carried, 1)
                else:
                    dve.tensor_copy(into[:, 1, 0:P - HEADS], ends[:, 1, HEADS:P]).then_inc(carried, 1)
                dve.wait_ge(started, d + 1)
                then(dve.tensor_copy(start[:, d:d + 1], p_s[:, d:d + 1]))
                then(scan(start[:, d:d + 1]))
            dve.tensor_tensor(a_t[:, :], a_t[:, :], whole_max, ALU.subtract).then_inc(shifted, 1)
            for b, (j, n) in enumerate(quads):
                dve.wait_ge(back, b + 1)
                if b == 0:
                    dve.wait_ge(shifted, 1)
                dve.tensor_copy(T.att[:, :, :].rearrange("p (l j) h -> p j l h", j=LV)[:, j:j + n],
                                p_l[b % 3][:, 0:n, :].rearrange("p k (l h) -> p k l h", h=HEADS)).then_inc(placed, 1)


def message_pass(nc, A, T, l):
    with ExitStack() as ctx:
        sb, ps, sem = stack(nc, ctx)
        nm = f"ms{l}_"
        m = sb(nm + "m", [P, 2, G, D])
        oh = sb(nm + "oh", [P, 2, G, P])
        msg = sb(nm + "msg", [P, 2, G, AW])
        p_a = [[ps(f"{nm}p_a{i}{j}", [P, 2, 256]) for j in range(2)] for i in range(2)]
        m_in = [sem(f"{nm}m_in{i}") for i in range(2)]
        onehots, messages, weights, summed = (sem(nm + n) for n in ("onehots", "messages", "weights", "summed"))
        added, set_up = sem(nm + "added"), sem(nm + "set_up")
        block = ctx.enter_context(nc.Block())
        m_slots = T.m_table.rearrange("(v p) f -> p v f", p=P)

        @block.sync
        def _(sp):
            def step(g, s):
                sp.wait_ge(messages, g + 1)
                sp.dma_start(m[:, s, :, :], m_slots[:, bass.ds(g * G, G), :]).then_inc(m_in[s], 16)

            pipeline(sp, step)

        @block.scalar
        def _(act):
            act.sem_inc(weights, 2)

            def step(g, s):
                act.wait_ge(summed, g + 1)
                act.activation(msg[:, s, :, D:AW], T.att[:, bass.ds(g * G, G), :], ACT.Copy).then_inc(weights, 1)

            pipeline(act, step)

        @block.tensor
        def _(pe):
            pe.sem_inc(summed, 2)

            def step(g, s):
                pe.wait_ge(onehots, g + 3)
                pe.wait_ge(messages, g + 3)
                pe.wait_ge(weights, g + 3)
                if past(g, 2):
                    pe.wait_ge(added, (g - 1) * G + 1)
                for k in range(G):
                    mm = pe.matmul(p_a[s][k // 2][:, k % 2, 0:AW], oh[:, s, k, :], msg[:, s, k, :], start=True, stop=True)
                mm.then_inc(summed, 1)

            pipeline(pe, step)

        @block.vector
        def _(dve):
            dve.sem_inc(onehots, 2)
            dve.sem_inc(messages, 2)
            dve.sem_inc(added, 1)
            dve.memset(T.agg[:, :, :], 0.0).then_inc(set_up, 1)
            dve.wait_ge(set_up, 1)

            def step(g, s):
                if within(g):
                    dve.wait_ge(summed, g + 1)
                    dve.tensor_tensor(oh[:, s, :, :], T.iota[:, :].unsqueeze(1).to_broadcast([P, G, P]),
                                      T.rel[:, bass.ds(g * G, G)].unsqueeze(2).to_broadcast([P, G, P]),
                                      ALU.is_equal).then_inc(onehots, 1)
                    if isinstance(g, int):
                        dve.wait_ge(m_in[s], 16 * (g // 2 + 1))
                    else:
                        dve.wait_ge(m_in[s], (g - s) * 8 + 16)
                    dve.tensor_tensor(msg[:, s, :, 0:D].rearrange("p k (h o) -> p k h o", o=HS),
                                      m[:, s, :, :].rearrange("p k (h o) -> p k h o", o=HS),
                                      T.att[:, bass.ds(g * G, G), :].unsqueeze(3).to_broadcast([P, G, HEADS, HS]), ALU.mult).then_inc(messages, 1)
                if past(g, 1):
                    h = g - 1
                    dve.wait_ge(summed, h + 3)
                    for k, t in enumerate(load_tiles(nc, dve, T, h)):
                        into = T.agg[:, bass.ds(t, 1), :].rearrange("p t f -> p (t f)")
                        dve.wait_ge(added, h * G + k + 1)
                        dve.tensor_tensor(into, into, p_a[1 - s][k // 2][:, k % 2, 0:AW], ALU.add).then_inc(added, 1)

            pipeline(dve, step, drain=(GROUPS,))


def node_update(nc, A, T, l):
    with ExitStack() as ctx:
        sb, ps, sem = stack(nc, ctx)
        nm = f"up{l}_"
        wa = sb(nm + "wa", [D, TYPES, D])
        par = sb(nm + "par", [P, 2, D])
        skip = sb(nm + "skip", [P, TYPES])
        den = sb(nm + "den", [P, TILES, HEADS])
        al = sb(nm + "al", [P, 2, TILES])
        Z, O = sb(nm + "Z", [P, TILES, D]), sb(nm + "O", [P, TILES, D])
        st = sb(nm + "st", [P, 4, TILES])
        z_t, xm = sb(nm + "z_t", [P, 512]), sb(nm + "xm", [P, TYPES, 512])
        p_t, p_o = ps(nm + "p_t", [P, 512]), [ps(f"{nm}p_o{i}", [P, 4, D]) for i in range(2)]
        params, chain, z_ready, turned, kept, masked, made, silued, al_sum, al_ready = (
            sem(nm + n) for n in ("params", "chain", "z_ready", "turned", "kept", "masked", "made", "silued", "al_sum", "al_ready"))
        centred, squared, var_ready, root = (sem(nm + n) for n in ("centred", "squared", "var_ready", "root"))
        block = ctx.enter_context(nc.Block())
        NB = len(BLOCKS)

        @block.sync
        def _(sp):
            sp.dma_start(skip[:, :], A["L2_gnn_skip"][l].partition_broadcast(P)).then_inc(params, 16)
            sp.dma_start(wa[:, :, :], A["L2_gnn_Wa"][l].rearrange("t i o -> i t o")).then_inc(params, 16)
            sp.dma_start(par[:, 0, :], A["L2_gnn_ln_g"][l].partition_broadcast(P)).then_inc(params, 16)
            sp.dma_start(par[:, 1, :], A["L2_gnn_ln_b"][l].partition_broadcast(P)).then_inc(params, 16)

        @block.tensor
        def _(pe):
            pe.wait_ge(z_ready, 1)
            pe.wait_ge(params, 64)
            for b, (t0, n) in enumerate(BLOCKS):
                if b >= 1:
                    pe.wait_ge(kept, b)
                for k in range(n):
                    tr = pe.transpose(p_t[:, k * P:(k + 1) * P], Z[:, t0 + k, :], T.ident[:, :])
                tr.then_inc(turned, 1)
                pe.wait_ge(masked, b + 1)
                if b >= 2:
                    pe.wait_ge(silued, b - 1)
                for k in range(n):
                    for t in range(TYPES):
                        mm = pe.matmul(p_o[b % 2][:, k, :], xm[:, t, k * P:(k + 1) * P], wa[:, t, :], start=(t == 0), stop=(t == TYPES - 1))
                mm.then_inc(made, 1)

        @block.scalar
        def _(act):
            for b, (t0, n) in enumerate(BLOCKS):
                act.wait_ge(turned, b + 1)
                if b >= 1:
                    act.wait_ge(masked, b)
                act.activation(z_t[:, 0:n * P], p_t[:, 0:n * P], ACT.Copy).then_inc(kept, 1)
                act.wait_ge(made, b + 1)
                act.activation(O[:, t0:t0 + n, :], p_o[b % 2][:, 0:n, :], ACT.Silu).then_inc(silued, 1)
            act.wait_ge(al_sum, 1)
            act.activation(al[:, 1, :], al[:, 0, :], ACT.Sigmoid).then_inc(al_ready, 1)
            act.wait_ge(centred, 1)
            act.activation(Z[:, :, :], O[:, :, :], ACT.Square).then_inc(squared, 1)
            act.wait_ge(var_ready, 1)
            act.activation(st[:, 2, :], st[:, 1, :], ACT.Sqrt).then_inc(root, 1)

        @block.vector
        def _(dve):
            then = Chain(dve, chain)

            def wide(a):
                return a.unsqueeze(2).to_broadcast([P, TILES, D])

            then(dve.tensor_scalar(den[:, :, :], T.agg[:, :, D:AW], 1e-16, None, ALU.add))
            then(dve.reciprocal(den[:, :, :], den[:, :, :]))
            for h in range(HEADS):
                of = slice(h * HS, (h + 1) * HS)
                ins = dve.tensor_tensor(Z[:, :, of], T.agg[:, :, of], den[:, :, h].unsqueeze(2).to_broadcast([P, TILES, HS]), ALU.mult)
            ins.then_inc(z_ready, 1)
            for b, (t0, n) in enumerate(BLOCKS):
                dve.wait_ge(kept, b + 1)
                if b >= 1:
                    dve.wait_ge(made, b)
                for t in range(TYPES):
                    ins = dve.scalar_tensor_tensor(out=xm[:, t, 0:n * P], in0=T.type_row[:, t0 * P:(t0 + n) * P], scalar=float(t),
                                                   in1=z_t[:, 0:n * P], op0=ALU.is_equal, op1=ALU.mult)
                ins.then_inc(masked, 1)
            dve.wait_ge(params, 64)
            then(dve.tensor_scalar(al[:, 0, :], T.type_of[:, :], 0.0, skip[:, 0:1], ALU.is_equal, ALU.mult))
            for t in range(1, TYPES):
                then(dve.tensor_scalar(al[:, 1, :], T.type_of[:, :], float(t), skip[:, t:t + 1], ALU.is_equal, ALU.mult))
                then(dve.tensor_tensor(al[:, 0, :], al[:, 0, :], al[:, 1, :], ALU.add))
            dve.sem_inc(al_sum, 1)
            dve.wait_ge(silued, NB)
            dve.wait_ge(al_ready, 1)
            then(dve.tensor_tensor(O[:, :, :], O[:, :, :], T.H[:, :, :], ALU.subtract))
            then(dve.tensor_tensor(O[:, :, :], O[:, :, :], wide(al[:, 1, :]), ALU.mult))
            then(dve.tensor_tensor(O[:, :, :], O[:, :, :], T.H[:, :, :], ALU.add))
            then(dve.tensor_reduce(st[:, 0, :], O[:, :, :], AX.X, ALU.add))
            then(dve.tensor_scalar(st[:, 0, :], st[:, 0, :], 1.0 / D, None, ALU.mult))
            dve.tensor_tensor(O[:, :, :], O[:, :, :], wide(st[:, 0, :]), ALU.subtract).then_inc(centred, 1)
            dve.wait_ge(squared, 1)
            then(dve.tensor_reduce(st[:, 1, :], Z[:, :, :], AX.X, ALU.add))
            dve.tensor_scalar(st[:, 1, :], st[:, 1, :], 1.0 / D, EPS, ALU.mult, ALU.add).then_inc(var_ready, 1)
            dve.wait_ge(root, 1)
            then(dve.reciprocal(st[:, 3, :], st[:, 2, :]))
            then(dve.tensor_tensor(O[:, :, :], O[:, :, :], wide(st[:, 3, :]), ALU.mult))
            then(dve.tensor_tensor(O[:, :, :], O[:, :, :], par[:, 0, :].unsqueeze(1).to_broadcast([P, TILES, D]), ALU.mult))
            then(dve.tensor_tensor(T.H[:, :, :], O[:, :, :], par[:, 1, :].unsqueeze(1).to_broadcast([P, TILES, D]), ALU.add))


def feed_out(nc, A, T):
    with ExitStack() as ctx:
        sb, ps, sem = stack(nc, ctx, "feed_out_")
        w, b0, one = sb("wff", [D, D]), sb("bff", [1, D]), sb("one_ff", [1, P])
        h_t = sb("ff_h_t", [P, 2, 512])
        p_t = [ps(f"ff_p_t{i}", [P, 512]) for i in range(2)]
        p_o = [ps(f"ff_p_o{i}", [P, 4, D]) for i in range(2)]
        params, set_up, turned, kept, made, taken = (sem("ff_" + n) for n in ("params", "set_up", "turned", "kept", "made", "taken"))
        block = ctx.enter_context(nc.Block())

        @block.sync
        def _(sp):
            sp.dma_start(w[:, :], A["L2_gnn_Wff"]).then_inc(params, 16)
            sp.dma_start(b0[:, :], A["L2_gnn_bff"].rearrange("(o f) -> o f", o=1)).then_inc(params, 16)

        @block.tensor
        def _(pe):
            pe.wait_ge(set_up, 1)
            pe.wait_ge(params, 32)
            for b, (t0, n) in enumerate(BLOCKS):
                if b >= 2:
                    pe.wait_ge(kept, b - 1)
                for k in range(n):
                    tr = pe.transpose(p_t[b % 2][:, k * P:(k + 1) * P], T.H[:, t0 + k, :], T.ident[:, :])
                tr.then_inc(turned, 1)
                pe.wait_ge(kept, b + 1)
                if b >= 2:
                    pe.wait_ge(taken, b - 1)
                for k in range(n):
                    pe.matmul(p_o[b % 2][:, k, :], h_t[:, b % 2, k * P:(k + 1) * P], w[:, :], start=True, stop=False)
                    mm = pe.matmul(p_o[b % 2][:, k, :], one[:, :], b0[:, :], start=False, stop=True)
                mm.then_inc(made, 1)

        @block.scalar
        def _(act):
            for b, (t0, n) in enumerate(BLOCKS):
                act.wait_ge(turned, b + 1)
                if b >= 2:
                    act.wait_ge(made, b - 1)
                act.activation(h_t[:, b % 2, 0:n * P], p_t[b % 2][:, 0:n * P], ACT.Copy).then_inc(kept, 1)

        @block.vector
        def _(dve):
            dve.memset(one[:, :], 1.0).then_inc(set_up, 1)
            for b, (t0, n) in enumerate(BLOCKS):
                dve.wait_ge(made, b + 1)
                dve.tensor_tensor(T.X[:, t0:t0 + n, :], T.X[:, t0:t0 + n, :], p_o[b % 2][:, 0:n, :], ALU.add).then_inc(taken, 1)


def gate_tables(nc, A, T):
    with ExitStack() as ctx:
        sb, ps, sem = stack(nc, ctx, "gate_tables_")
        w = sb("gt_w", [D, ROW3])
        row_b, one = sb("gt_row_b", [1, ROW3]), sb("gt_one", [1, P])
        w_dst, w_dst_wide, b_att = sb("gt_w_dst", [D, 1]), sb("gt_w_dst_wide", [D, P]), sb("gt_b_att", [P, 1])
        rows = sb("gt_rows", [P, TILES, ROW3])
        p_t = [ps(f"gt_p_t{i}", [P, 512]) for i in range(2)]
        p_o = [[ps(f"gt_p_o{i}{j}", [P, 2, 256]) for j in range(2)] for i in range(2)]
        p_d = [ps(f"gt_p_d{i}", [P, 512]) for i in range(2)]
        params, set_up, turned, kept, made, taken, dsts, dst_kept, stored, widened = (
            sem("gt_" + n) for n in ("params", "set_up", "turned", "kept", "made", "taken", "dsts", "dst_kept", "stored", "widened"))
        block = ctx.enter_context(nc.Block())
        W_att = A["L3_gnn_W_att"]

        @block.sync
        def _(sp):
            sp.wait_ge(set_up, 3)
            sp.dma_start(w[:, 0:D], A["L3_gnn_W_msg"]).then_inc(params, 16)
            sp.dma_start(w[:, D:D + 1], W_att[0:D, :]).then_inc(params, 16)
            sp.dma_start(w_dst[:, :], W_att[D:2 * D, :]).then_inc(params, 16)
            sp.dma_start(row_b[:, 0:D], A["L3_gnn_b_msg"].rearrange("(o f) -> o f", o=1)).then_inc(params, 16)
            sp.dma_start(b_att[:, :], A["L3_gnn_b_att"].partition_broadcast(P)).then_inc(params, 16)
            sp.wait_ge(taken, 2 * len(BLOCKS) - 1)
            sp.dma_start(T.gate_table.rearrange("(t p) f -> p t f", p=P), rows[:, :, :]).then_inc(stored, 16)
            sp.wait_ge(stored, 16)

        @block.tensor
        def _(pe):
            pe.wait_ge(widened, 1)
            done = 0
            for b, (t0, n) in enumerate(BLOCKS):
                if b >= 2:
                    pe.wait_ge(kept, b - 1)
                for k in range(n):
                    tr = pe.transpose(p_t[b % 2][:, k * P:(k + 1) * P], T.H[:, t0 + k, :], T.ident[:, :])
                tr.then_inc(turned, 1)
                pe.wait_ge(kept, b + 1)
                if b >= 2:
                    pe.wait_ge(taken, 2 * (b - 1))
                    pe.wait_ge(dst_kept, b - 1)
                for k in range(n):
                    at = p_o[b % 2][k // 2][:, k % 2, 0:ROW3]
                    pe.matmul(at, T.H_t[:, (t0 + k) * P:(t0 + k + 1) * P], w[:, :], start=True, stop=False)
                    mm = pe.matmul(at, one[:, :], row_b[:, :], start=False, stop=True)
                mm.then_inc(made, 1)
                pe.matmul(p_d[b % 2][:, 0:n * P], w_dst_wide[:, :], T.H_t[:, t0 * P:(t0 + n) * P], start=True, stop=True).then_inc(dsts, 1)

        @block.scalar
        def _(act):
            act.wait_ge(params, 80)
            for b, (t0, n) in enumerate(BLOCKS):
                act.wait_ge(turned, b + 1)
                act.activation(T.H_t[:, t0 * P:(t0 + n) * P], p_t[b % 2][:, 0:n * P], ACT.Copy).then_inc(kept, 1)
                act.wait_ge(dsts, b + 1)
                act.activation(T.dst_row[:, t0 * P:(t0 + n) * P], p_d[b % 2][:, 0:n * P], ACT.Identity, bias=b_att[:, 0:1]).then_inc(dst_kept, 1)

        @block.vector
        def _(dve):
            dve.memset(w[:, :], 0.0).then_inc(set_up, 1)
            dve.memset(row_b[:, :], 0.0).then_inc(set_up, 1)
            dve.memset(one[:, :], 1.0).then_inc(set_up, 1)
            dve.wait_ge(params, 80)
            dve.tensor_copy(w_dst_wide[:, :], w_dst[:, 0:1].to_broadcast([D, P])).then_inc(widened, 1)
            for b, (t0, n) in enumerate(BLOCKS):
                dve.wait_ge(made, b + 1)
                for j in range((n + 1) // 2):
                    m = min(2, n - 2 * j)
                    dve.tensor_copy(rows[:, t0 + 2 * j:t0 + 2 * j + m, :], p_o[b % 2][j][:, 0:m, 0:ROW3]).then_inc(taken, 1)


def gate_pass(nc, A, T):
    with ExitStack() as ctx:
        sb, ps, sem = stack(nc, ctx, "gate_pass_")
        idx = sb("idx3", [P, 2, G], I32)
        hx = sb("hx3", [P, 2, G, ROW3])
        oh = sb("oh3", [P, 2, G, P])
        pick = sb("pick", [P, 2, G, P])
        dst_term = sb("dst_term", [P, 2, G])
        z, gate = sb("z3", [P, 2, G]), sb("gate", [P, 2, G])
        msg = sb("msg3", [P, 2, G, D])
        p_a = [ps(f"p_a{i}", [P, G, D]) for i in range(2)]
        idx_ready, onehots, messages, summed, gates, terms = (sem("l3_" + n) for n in ("idx_ready", "onehots", "messages", "summed", "gates", "terms"))
        picked, dst_terms, added, opened, set_up = (sem("l3_" + n) for n in ("picked", "dst_terms", "added", "opened", "set_up"))
        block = ctx.enter_context(nc.Block())

        @block.gpsimd
        def _(pool):
            bound = pool.to_reg(NP - 1)

            def step(g, s):
                pool.wait_ge(idx_ready, g + 3)
                pool.wait_ge(messages, g + 1)
                pool.sem_inc(opened, 1)
                for k in range(G):
                    pool.indirect_dma_start(out=hx[:, s, k, :], out_offset=None, in_=T.gate_table,
                                            in_offset=bass.IndirectOffsetOnAxis(ap=idx[:, s, k:k + 1].bitcast(U32), axis=0),
                                            bounds_check=bound).then_inc(T.gathered[s], 16)

            pipeline(pool, step)

        @block.scalar
        def _(act):
            act.sem_inc(idx_ready, 2)
            act.sem_inc(gates, 2)

            def step(g, s):
                if within(g):
                    act.wait_ge(messages, g + 1)
                    act.activation(idx[:, s, :], T.src[:, bass.ds(g * G, G)], ACT.Copy).then_inc(idx_ready, 1)
                if past(g, 1):
                    h, q = g - 1, 1 - s
                    act.wait_ge(terms, h + 3)
                    act.activation(gate[:, q, :], z[:, q, :], ACT.Sigmoid).then_inc(gates, 1)

            pipeline(act, step, drain=(GROUPS,))

        @block.tensor
        def _(pe):
            pe.sem_inc(summed, 2)

            def step(g, s):
                pe.wait_ge(messages, g + 3)
                pe.wait_ge(onehots, g + 3)
                if past(g, 2):
                    pe.wait_ge(added, (g - 1) * G + 1)
                for k in range(G):
                    mm = pe.matmul(p_a[s][:, k, :], oh[:, s, k, :], msg[:, s, k, :], start=True, stop=True)
                mm.then_inc(summed, 1)

            pipeline(pe, step)

        @block.vector
        def _(dve):
            dve.sem_inc(onehots, 2)
            dve.sem_inc(messages, 2)
            dve.sem_inc(terms, 2)
            dve.sem_inc(added, 1)
            dve.memset(T.agg[:, :, :], 0.0).then_inc(set_up, 1)
            dve.wait_ge(set_up, 1)

            def step(g, s):
                q = 1 - s
                if past(g, 1) and within(g - 1):
                    h = g - 1
                    wait_gathers(dve, T, 4, h, q)
                    dve.wait_ge(dst_terms, h + 1)
                    dve.wait_ge(gates, h + 1)
                    dve.tensor_tensor(z[:, q, :], hx[:, q, :, D], dst_term[:, q, :], ALU.add).then_inc(terms, 1)
                if within(g):
                    dve.wait_ge(summed, g + 1)
                    dve.tensor_tensor(oh[:, s, :, :], T.iota[:, :].unsqueeze(1).to_broadcast([P, G, P]),
                                      T.rel[:, bass.ds(g * G, G)].unsqueeze(2).to_broadcast([P, G, P]),
                                      ALU.is_equal).then_inc(onehots, 1)
                    dve.wait_ge(onehots, g + 3)
                    if past(g, 2):
                        dve.wait_ge(dst_terms, g - 1)
                        dve.wait_ge(terms, g + 1)
                    for k, t in enumerate(load_tiles(nc, dve, T, g)):
                        dve.tensor_tensor(pick[:, s, k, :], oh[:, s, k, :], T.dst_row[:, bass.ds(t * P, P)], ALU.mult).then_inc(picked, 1)
                    dve.wait_ge(picked, g * G + G)
                    dve.tensor_reduce(dst_term[:, s, :], pick[:, s, :, :], AX.X, ALU.add).then_inc(dst_terms, 1)
                if past(g, 1) and within(g - 1):
                    h = g - 1
                    dve.wait_ge(gates, h + 3)
                    dve.wait_ge(summed, h + 1)
                    dve.tensor_tensor(msg[:, q, :, :], hx[:, q, :, 0:D], gate[:, q, :].unsqueeze(2).to_broadcast([P, G, D]), ALU.mult).then_inc(messages, 1)
                if past(g, 2):
                    h = g - 2
                    dve.wait_ge(summed, h + 3)
                    for k, t in enumerate(load_tiles(nc, dve, T, h)):
                        into = T.agg[:, bass.ds(t, 1), 0:D].rearrange("p t f -> p (t f)")
                        dve.wait_ge(added, h * G + k + 1)
                        dve.tensor_tensor(into, into, p_a[s][:, k, :], ALU.add).then_inc(added, 1)

            pipeline(dve, step, drain=(GROUPS, GROUPS + 1))


def node_gru(nc, A, T, out):
    with ExitStack() as ctx:
        sb, ps, sem = stack(nc, ctx, "node_gru_")
        raw = sb("gru_raw", [P, 2, 3, D])
        w_t = sb("gru_w_t", [P, 2, 3, D])
        bias = sb("gru_bias", [P, 2, 3])
        both = sb("gru_both", [P, 2])
        agg_t = sb("gru_agg_t", [P, 2, 512])
        r, z, nn, hn = (sb("gru_" + n, [P, 2, 512]) for n in ("r", "z", "nn", "hn"))
        Y = sb("gru_Y", [P, NP])
        p_t = [ps(f"gru_p_t{i}", [P, 512]) for i in range(2)]
        p_r, p_z, p_i, p_h = (ps("gru_p_" + n, [P, 512]) for n in "rzih")
        p_b = [ps(f"gru_p_b{i}", [P, 4, D]) for i in range(2)]
        params, chain, w_turned, w_kept, turned, kept, gated, sig, steps, tanhed, biased = (
            sem("gru_" + n) for n in ("params", "chain", "w_turned", "w_kept", "turned", "kept", "gated", "sig", "steps", "tanhed", "biased"))
        back, taken, n_read, i_summed, done = (sem("gru_" + n) for n in ("back", "taken", "n_read", "i_summed", "done"))
        bn = Batchnorm(sb, sem, "bn3_", Y)
        block = ctx.enter_context(nc.Block())
        NB = len(BLOCKS)

        @block.sync
        def _(sp):
            for k, name in enumerate(("ih", "hh")):
                sp.dma_start(raw[:, k, :, :], A["L3_gnn_W_" + name].rearrange("(g p) f -> p g f", p=P)).then_inc(params, 16)
                for g in range(3):
                    sp.dma_start(bias[:, k, g:g + 1], A["L3_gnn_b_" + name][g * P:(g + 1) * P].rearrange("(p o) -> p o", o=1)).then_inc(params, 16)
            bn.load(sp, A["L3_gnn_gamma"], A["L3_gnn_beta"])
            full = N // P
            sp.wait_ge(taken, NB)
            sp.dma_start(out[0:full * P, :].rearrange("(t p) f -> p t f", p=P), T.X[:, 0:full, :]).then_inc(done, 16)
            sp.dma_start(out[full * P:N, :], T.X[0:N - full * P, full, :]).then_inc(done, 16)
            sp.wait_ge(done, 32)

        @block.tensor
        def _(pe):
            pe.wait_ge(params, 128)
            for k in range(2):
                for g in range(3):
                    tr = pe.transpose(p_t[k][:, g * P:(g + 1) * P], raw[:, k, g, :], T.ident[:, :])
                tr.then_inc(w_turned, 1)
            pe.wait_ge(w_kept, 2)
            for b, (t0, n) in enumerate(BLOCKS):
                if b >= 2:
                    pe.wait_ge(kept, b - 1)
                for k in range(n):
                    tr = pe.transpose(p_t[b % 2][:, k * P:(k + 1) * P], T.agg[:, t0 + k, 0:D], T.ident[:, :])
                tr.then_inc(turned, 1)
                pe.wait_ge(kept, b + 1)
                w = n * P
                a, h = agg_t[:, b % 2, 0:w], T.H_t[:, t0 * P:t0 * P + w]
                if b >= 1:
                    pe.wait_ge(sig, 2 * b)
                for g, bank in enumerate((p_r, p_z)):
                    pe.matmul(bank[:, 0:w], w_t[:, 0, g, :], a, start=True, stop=False)
                    pe.matmul(bank[:, 0:w], w_t[:, 1, g, :], h, start=False, stop=True).then_inc(gated, 1)
                if b >= 1:
                    pe.wait_ge(n_read, b)
                    pe.wait_ge(i_summed, b)
                pe.matmul(p_h[:, 0:w], w_t[:, 1, 2, :], h, start=True, stop=True).then_inc(gated, 1)
                pe.matmul(p_i[:, 0:w], w_t[:, 0, 2, :], a, start=True, stop=True).then_inc(gated, 1)
            pe.wait_ge(bn.done, 1)
            for b, (t0, n) in enumerate(BLOCKS):
                if b >= 2:
                    pe.wait_ge(taken, b - 1)
                for k in range(n):
                    tr = pe.transpose(p_b[b % 2][:, k, :], Y[:, (t0 + k) * P:(t0 + k + 1) * P], T.ident[:, :])
                tr.then_inc(back, 1)

        @block.scalar
        def _(act):
            act.wait_ge(params, 128)
            for k in range(2):
                act.wait_ge(w_turned, k + 1)
                act.activation(w_t[:, k, :, :], p_t[k][:, 0:3 * P].rearrange("p (g o) -> p g o", g=3), ACT.Copy).then_inc(w_kept, 1)
            act.wait_ge(biased, 1)
            for b, (t0, n) in enumerate(BLOCKS):
                w, s = n * P, b % 2
                act.wait_ge(turned, b + 1)
                if b >= 2:
                    act.wait_ge(gated, 4 * (b - 1))
                act.activation(agg_t[:, s, 0:w], p_t[s][:, 0:w], ACT.Copy).then_inc(kept, 1)
                if b >= 2:
                    act.wait_ge(steps, 4 * (b - 1))
                act.wait_ge(gated, 4 * b + 1)
                act.activation(r[:, s, 0:w], p_r[:, 0:w], ACT.Sigmoid, bias=both[:, 0:1]).then_inc(sig, 1)
                act.wait_ge(gated, 4 * b + 2)
                act.activation(z[:, s, 0:w], p_z[:, 0:w], ACT.Sigmoid, bias=both[:, 1:2]).then_inc(sig, 1)
                act.wait_ge(gated, 4 * b + 3)
                act.activation(hn[:, s, 0:w], p_h[:, 0:w], ACT.Identity, bias=bias[:, 1, 2:3]).then_inc(n_read, 1)
                act.wait_ge(i_summed, b + 1)
                act.activation(nn[:, s, 0:w], nn[:, s, 0:w], ACT.Tanh, bias=bias[:, 0, 2:3]).then_inc(tanhed, 1)
            bn.on_scalar(act, ACT.Identity)

        @block.vector
        def _(dve):
            then = Chain(dve, chain)
            dve.wait_ge(params, 128)
            dve.tensor_tensor(both[:, :], bias[:, 0, 0:2], bias[:, 1, 0:2], ALU.add).then_inc(biased, 1)
            for b, (t0, n) in enumerate(BLOCKS):
                w, s = n * P, b % 2
                h, y = T.H_t[:, t0 * P:t0 * P + w], Y[:, t0 * P:t0 * P + w]
                dve.wait_ge(n_read, b + 1)
                dve.tensor_tensor(nn[:, s, 0:w], r[:, s, 0:w], hn[:, s, 0:w], ALU.mult).then_inc(steps, 1)
                dve.wait_ge(steps, 4 * b + 1)
                dve.wait_ge(gated, 4 * b + 4)
                dve.tensor_tensor(nn[:, s, 0:w], nn[:, s, 0:w], p_i[:, 0:w], ALU.add).then_inc(i_summed, 1)
                dve.wait_ge(tanhed, b + 1)
                dve.tensor_tensor(y, h, nn[:, s, 0:w], ALU.subtract).then_inc(steps, 1)
                dve.wait_ge(steps, 4 * b + 2)
                dve.tensor_tensor(y, y, z[:, s, 0:w], ALU.mult).then_inc(steps, 1)
                dve.wait_ge(steps, 4 * b + 3)
                dve.tensor_tensor(y, y, nn[:, s, 0:w], ALU.add).then_inc(steps, 1)
            dve.wait_ge(steps, 4 * NB)
            bn.on_vector(dve, then)
            for b, (t0, n) in enumerate(BLOCKS):
                dve.wait_ge(back, b + 1)
                dve.tensor_tensor(T.X[:, t0:t0 + n, :], T.X[:, t0:t0 + n, :], p_b[b % 2][:, 0:n, :], ALU.add).then_inc(taken, 1)


def clear_semaphores(nc):
    free = sorted(nc.free_semaphores)
    assert free == list(range(free[0], free[-1] + 1))
    with nc.Block() as block:
        @block.gpsimd
        def _(pool):
            pool.sem_clear(range(free[0], free[-1] + 1))


def program(nc, A, out):
    T = Tensors()
    with ExitStack() as ctx:
        sb, ps, sem = stack(nc, ctx)
        T.chunk_table = nc.dram_tensor("chunk_table", (CT * P, 3 * P), I32).ap()
        T.attr = nc.dram_tensor("attr_padded", ((VISITS - TILES + 1) * P, EF), F32).ap()
        T.h_table = nc.dram_tensor("h_table", (NP, D), F32).ap()
        T.kv_table = nc.dram_tensor("kv_table", (NP * REL, 2 * D), F32).ap()
        T.m_table = nc.dram_tensor("m_table", (VISITS * P, D), F32).ap()
        T.gate_table = nc.dram_tensor("gate_table", (NP, ROW3), F32).ap()
        T.X = sb("X", [P, TILES, D])
        T.H = sb("H", [P, TILES, D])
        T.agg = sb("agg", [P, TILES, AW])
        T.ident = sb("ident", [P, P])
        T.iota = sb("iota", [P, P])
        T.rel = sb("rel", [P, CT * P])
        T.key = sb("key", [P, CT * P])
        T.src = sb("src", [P, CT * P], I32)
        T.srcrel = sb("srcrel", [P, CT * P], I32)
        T.tile_codes = sb("tile_codes", [1, GROUPS], I32)
        T.gathered = [sem(f"gathered{i}") for i in range(2)]
        T.rows_in = sem("visit_rows_in")
        setup(nc, A, T)
        layernorm_relu(nc, T, "ln0", True)
        edge_mlp_pass(nc, A, T)
        node_mlp(nc, A, T)
        layernorm_relu(nc, T, "ln1", True)
        sum_pass(nc, A, T)
        node_gin(nc, A, T)
        clear_semaphores(nc)
        layernorm_relu(nc, T, "ln2", False)
        with ExitStack() as layer2:
            sb, ps, sem = stack(nc, layer2)
            T.type_row = sb("type_row", [P, NP])
            T.type_of = sb("type_of", [P, TILES])
            T.Q = sb("Q", [P, TILES, D])
            T.whole = sb("whole_lane", [1, 2, P])
            T.att = sb("att", [P, SV, HEADS])
            T.flag = sb("flag", [P, LE + 1])
            scan_flags(nc, A, T)
            for l in range(LAYERS):
                typed_qkv(nc, A, T, l)
                score_pass(nc, A, T, l)
                softmax_shift(nc, A, T, l)
                message_pass(nc, A, T, l)
                node_update(nc, A, T, l)
                clear_semaphores(nc)
        feed_out(nc, A, T)
        layernorm_relu(nc, T, "ln3", False)
        T.H_t = sb_outer(nc, ctx, "H_t", [P, NP])
        T.dst_row = sb_outer(nc, ctx, "dst_row", [P, NP])
        gate_tables(nc, A, T)
        gate_pass(nc, A, T)
        node_gru(nc, A, T, out)


def sb_outer(nc, ctx, name, shape):
    return ctx.enter_context(nc.sbuf_tensor(name, shape, F32))




def kernel(**inputs):
    import numpy as _np
    import concourse.bacc as _bacc
    from concourse.bass_utils import run_bass_kernel_spmd as _run

    nc = _bacc.Bacc("TRN2", target_bir_lowering=False, num_devices=1)
    arrays, args = {}, {}
    for name, value in inputs.items():
        a = _np.ascontiguousarray(value)
        arrays[f"in_{name}_dram"] = a
        args[name] = nc.dram_tensor(f"in_{name}_dram", a.shape, mybir.dt.from_np(a.dtype), kind="ExternalInput").ap()
    out = nc.dram_tensor("out_dram", (N, D), F32, kind="ExternalOutput").ap()
    program(nc, args, out)
    r = _run(nc, [arrays], core_ids=[0])
    return r.results[0]["out_dram"]
```

```python
from contextlib import ExitStack

import concourse.bass as bass
from concourse import mybir

P = 128
N = 3125
E = 100000
D = 128
EF = 50
TILES = -(-N // P)
NP = TILES * P
CHUNKS = -(-E // P)
G = 4
GROUPS = -(-(CHUNKS + TILES - 1) // G)
VISITS = GROUPS * G
CT = -(-VISITS // P)
HEADS, HS, REL, TYPES, LAYERS = 8, 16, 8, 8, 2
LANES = P // HEADS
LV = -(-VISITS // LANES)
SV = LV * LANES
LE = LV * P
PAD_DST = 30000
BIG = 1.0e38
EPS = 1e-5
ROW3 = 132
AW = D + HEADS

F32 = mybir.dt.float32
BF16 = mybir.dt.bfloat16
I32 = mybir.dt.int32
U32 = mybir.dt.uint32
ALU = mybir.AluOpType
ACT = mybir.ActivationFunctionType
AX = mybir.AxisListType

TBANKS = -(-TILES // 4)
CODE = (TILES - 1).bit_length()
BLOCKS = [(b, min(4, TILES - b)) for b in range(0, TILES, 4)]


class Tensors:
    pass


class Chain:

    def __init__(self, eng, sem):
        self.eng, self.sem, self.n = eng, sem, 0

    def __call__(self, ins):
        self.n += 1
        ins.then_inc(self.sem, 1)
        self.eng.wait_ge(self.sem, self.n)


def stack(nc, ctx, stage=""):
    def sb(name, shape, dt=F32):
        return ctx.enter_context(nc.sbuf_tensor(stage + name, shape, dt))

    def ps(name, shape, dt=F32):
        return ctx.enter_context(nc.psum_tensor(stage + name, shape, dt))

    def sem(name):
        return ctx.enter_context(nc.semaphore(stage + name))

    return sb, ps, sem


def setup(nc, A, T):
    with ExitStack() as ctx:
        sb, ps, sem = stack(nc, ctx, "setup_")
        ctab = sb("ctab", [P, CT, 3, P], I32)
        last = sb("last", [P, CT])
        thr = sb("thr", [P, TILES - 1, CT])
        cmp1 = sb("cmp1", [P, TILES - 1, CT])
        cnt = sb("cnt", [P, TILES - 1])
        tio = sb("tio", [P, TILES - 1])
        ends = sb("ends", [P, TILES - 1])
        vio = sb("vio", [P, CT])
        cmp2 = sb("cmp2", [P, CT, TILES - 1])
        tvp = sb("tvp", [P, CT])
        cvp = sb("cvp", [P, CT])
        cvi = sb("cvi", [P, CT], I32)
        base = sb("base", [P, CT])
        viorow = sb("viorow", [P, VISITS])
        tvrow = sb("tvrow", [P, VISITS])
        ones = sb("ones", [P, P])
        vt = sb("vt", [P, CT, 3 * P], I32)
        fld = sb("fld", [P, 4, CT, P])
        vtf = sb("vtf", [P, 2, CT, P])
        zeros = sb("zeros", [P, 16 * EF])
        pc = ps("pc", [P, 512])
        pt = [ps(f"pt{i}", [P, 4, P]) for i in range(2)]
        loaded, stored, padded = sem("ctab_loaded"), sem("ctab_stored"), sem("ctab_padded")
        copied, x_in, zeroed = sem("attr_copied"), sem("x_in"), sem("zeroed")
        consts, chain, counted = sem("consts"), sem("setup_chain"), sem("counted")
        ends_ready, cvi_ready, rows_in = sem("ends_ready"), sem("cvi_ready"), T.rows_in
        fields, turned, taken = sem("fields"), sem("turned"), sem("taken")
        block = ctx.enter_context(nc.Block())
        chunked = T.chunk_table.rearrange("(j p) (k e) -> p j k e", p=P, e=P)
        full = (CT - 1) * P
        more = E // P - full
        tail = E - (full + more) * P

        @block.sync
        def _(sp):
            sp.wait_ge(padded, 3)
            for k, a in enumerate((A["dst"], A["src"], A["edge_type_8"])):
                sp.dma_start(ctab[:, 0:CT - 1, k, :], a[0:full * P].rearrange("(j p e) -> p j e", p=P, e=P)).then_inc(loaded, 16)
                sp.dma_start(ctab[0:more, CT - 1, k, :], a[full * P:(full + more) * P].rearrange("(p e) -> p e", e=P)).then_inc(loaded, 16)
                sp.dma_start(ctab[more:more + 1, CT - 1, k, 0:tail], a[(full + more) * P:E].rearrange("(p e) -> p e", p=1)).then_inc(loaded, 16)
            sp.wait_ge(loaded, 9 * 16)
            for j in range(CT):
                sp.dma_start(chunked[:, j], ctab[:, j]).then_inc(stored, 16)
            full_tiles = N // P
            sp.wait_ge(zeroed, 2)
            sp.dma_start(T.X[:, 0:full_tiles, :], A["x"][0:full_tiles * P, :].rearrange("(t p) f -> p t f", p=P)).then_inc(x_in, 16)
            sp.dma_start(T.X[0:N - full_tiles * P, full_tiles, :], A["x"][full_tiles * P:N, :]).then_inc(x_in, 16)
            sp.wait_ge(x_in, 32)
            sp.wait_ge(stored, 16 * CT)

        @block.scalar
        def _(act):
            rows = E // 4
            for q in range(4):
                act.dma_start(T.attr[q * rows:(q + 1) * rows, :].rearrange("(a b) f -> a (b f)", b=50),
                              A["edge_attr_50"][q * rows:(q + 1) * rows, :].rearrange("(a b) f -> a (b f)", b=50)).then_inc(copied, 16)
            act.wait_ge(zeroed, 1)
            pad = T.attr.shape[0] - E
            act.dma_start(T.attr[E:E + pad, :].rearrange("(q r) f -> q (r f)", r=16),
                          zeros[0:pad // 16, 0:16 * EF]).then_inc(copied, 16)
            act.wait_ge(copied, 5 * 16)

        @block.gpsimd
        def _(pool):
            pool.memset(ctab[:, CT - 1, 0, :], PAD_DST).then_inc(padded, 1)
            pool.memset(ctab[:, CT - 1, 1, :], 0).then_inc(padded, 1)
            pool.memset(ctab[:, CT - 1, 2, :], 0).then_inc(padded, 1)
            pool.memset(T.ident[:, :], 0.0).then_inc(consts, 1)
            pool.wait_ge(consts, 1)
            pool.affine_select(out=T.ident[:, :], in_=T.ident[:, :], compare_op=ALU.not_equal, fill=1.0, base=0,
                               pattern=[[-1, P]], channel_multiplier=1).then_inc(consts, 1)
            pool.iota(thr[:, :, :], [[P, TILES - 1], [0, CT]], base=P, channel_multiplier=0,
                      allow_small_or_imprecise_dtypes=True).then_inc(consts, 1)
            pool.iota(tio[:, :], [[1, TILES - 1]], base=0, channel_multiplier=0,
                      allow_small_or_imprecise_dtypes=True).then_inc(consts, 1)
            pool.iota(vio[:, :], [[P, CT]], base=0, channel_multiplier=1,
                      allow_small_or_imprecise_dtypes=True).then_inc(consts, 1)
            pool.iota(viorow[:, :], [[1, VISITS]], base=0, channel_multiplier=0,
                      allow_small_or_imprecise_dtypes=True).then_inc(consts, 1)
            pool.iota(T.iota[:, :], [[1, P]], base=0, channel_multiplier=0,
                      allow_small_or_imprecise_dtypes=True).then_inc(consts, 1)
            pool.memset(ones[:, :], 1.0).then_inc(consts, 1)
            pool.wait_ge(cvi_ready, 1)
            pool.wait_ge(stored, 16 * CT)
            for j in range(CT):
                pool.indirect_dma_start(out=vt[:, j, :], out_offset=None, in_=T.chunk_table,
                                        in_offset=bass.IndirectOffsetOnAxis(ap=cvi[:, j:j + 1].bitcast(U32), axis=0),
                                        bounds_check=CT * P - 1).then_inc(rows_in, 16)

        @block.tensor
        def _(pe):
            pe.wait_ge(counted, 1)
            pe.wait_ge(consts, 8)
            pe.matmul(pc[:, 0:TILES - 1], ones[:, :], cnt[:, :], start=True, stop=True).then_inc(ends_ready, 1)
            pe.wait_ge(fields, 1)
            for b in range(CT):
                if b >= 2:
                    pe.wait_ge(taken, b - 1)
                for k in range(4):
                    tr = pe.transpose(pt[b % 2][:, k, :], fld[:, k, b, :], T.ident[:, :])
                tr.then_inc(turned, 1)

        @block.vector
        def _(dve):
            then = Chain(dve, chain)
            dve.memset(zeros[:, :], 0.0).then_inc(zeroed, 1)
            dve.memset(T.X[:, TILES - 1, :], 0.0).then_inc(zeroed, 1)
            dve.wait_ge(loaded, 9 * 16)
            dve.wait_ge(consts, 8)
            then(dve.tensor_copy(last[:, :], ctab[:, :, 0, P - 1]))
            then(dve.tensor_tensor(cmp1[:, :, :], last[:, :].unsqueeze(1).to_broadcast([P, TILES - 1, CT]), thr[:, :, :], ALU.is_lt))
            dve.tensor_reduce(cnt[:, :], cmp1[:, :, :], AX.X, ALU.add).then_inc(counted, 1)
            dve.wait_ge(ends_ready, 1)
            then(dve.tensor_tensor(ends[:, :], pc[:, 0:TILES - 1], tio[:, :], ALU.add))
            then(dve.tensor_tensor(cmp2[:, :, :], ends[:, :].unsqueeze(1).to_broadcast([P, CT, TILES - 1]),
                                   vio[:, :].unsqueeze(2).to_broadcast([P, CT, TILES - 1]), ALU.is_lt))
            then(dve.tensor_reduce(tvp[:, :], cmp2[:, :, :], AX.X, ALU.add))
            then(dve.tensor_tensor(cvp[:, :], vio[:, :], tvp[:, :], ALU.subtract))
            dve.tensor_copy(cvi[:, :], cvp[:, :]).then_inc(cvi_ready, 1)
            then(dve.tensor_scalar(base[:, :], tvp[:, :], float(P), None, ALU.mult))
            then(dve.tensor_scalar(tvrow[:, :], viorow[:, :], ends[:, 0:1], None, ALU.is_gt))
            for t in range(1, TILES - 1):
                then(dve.scalar_tensor_tensor(out=tvrow[:, :], in0=viorow[:, :], scalar=ends[:, t:t + 1],
                                              in1=tvrow[:, :], op0=ALU.is_gt, op1=ALU.add))
            tiles = tvrow[0:1, :].rearrange("o (g k) -> o g k", k=G)
            for k in range(G - 2, -1, -1):
                then(dve.scalar_tensor_tensor(out=tiles[:, :, k], in0=tiles[:, :, k + 1], scalar=float(1 << CODE),
                                              in1=tiles[:, :, k], op0=ALU.mult, op1=ALU.add))
            then(dve.tensor_copy(T.tile_codes[:, :], tiles[:, :, 0]))
            dve.wait_ge(rows_in, 16 * CT)
            rows = vt[:, :, :].rearrange("p j (k e) -> p j k e", e=P)
            then(dve.tensor_copy(vtf[:, 0, :, :], rows[:, :, 0, :]))
            then(dve.tensor_copy(fld[:, 2, :, :], rows[:, :, 1, :]))
            then(dve.tensor_copy(vtf[:, 1, :, :], rows[:, :, 2, :]))
            for j in range(CT):
                then(dve.tensor_scalar(fld[:, 0, j, :], vtf[:, 0, j, :], base[:, j:j + 1], None, ALU.subtract))
            then(dve.scalar_tensor_tensor(out=fld[:, 3, :, :], in0=fld[:, 2, :, :], scalar=float(REL),
                                          in1=vtf[:, 1, :, :], op0=ALU.mult, op1=ALU.add))
            then(dve.tensor_scalar(vtf[:, 1, :, :], fld[:, 0, :, :], 0.0, None, ALU.is_ge))
            then(dve.scalar_tensor_tensor(out=vtf[:, 1, :, :], in0=fld[:, 0, :, :], scalar=float(P),
                                          in1=vtf[:, 1, :, :], op0=ALU.is_lt, op1=ALU.mult))
            dve.scalar_tensor_tensor(out=fld[:, 1, :, :], in0=vtf[:, 0, :, :], scalar=1.0,
                                     in1=vtf[:, 1, :, :], op0=ALU.add, op1=ALU.mult).then_inc(fields, 1)
            for b in range(CT):
                dve.wait_ge(turned, b + 1)
                to = slice(b * P, (b + 1) * P)
                dve.tensor_copy(T.rel[:, to], pt[b % 2][:, 0, :])
                dve.tensor_copy(T.key[:, to], pt[b % 2][:, 1, :])
                dve.tensor_copy(T.src[:, to], pt[b % 2][:, 2, :])
                dve.tensor_copy(T.srcrel[:, to], pt[b % 2][:, 3, :]).then_inc(taken, 1)


def layernorm_relu(nc, T, name, store):
    with ExitStack() as ctx:
        sb, ps, sem = stack(nc, ctx)
        sq = sb(name + "_sq", [P, TILES, D])
        st = sb(name + "_st", [P, 4, TILES])
        chain, centred, squared = sem(name + "_chain"), sem(name + "_centred"), sem(name + "_squared")
        var_ready, root, h_ready, stored = sem(name + "_var"), sem(name + "_root"), sem(name + "_h"), sem(name + "_stored")
        block = ctx.enter_context(nc.Block())

        def wide(k):
            return st[:, k, :].unsqueeze(2).to_broadcast([P, TILES, D])

        @block.vector
        def _(dve):
            then = Chain(dve, chain)
            then(dve.tensor_reduce(st[:, 0, :], T.X[:, :, :], AX.X, ALU.add))
            then(dve.tensor_scalar(st[:, 0, :], st[:, 0, :], 1.0 / D, None, ALU.mult))
            dve.tensor_tensor(T.H[:, :, :], T.X[:, :, :], wide(0), ALU.subtract).then_inc(centred, 1)
            dve.wait_ge(squared, 1)
            then(dve.tensor_reduce(st[:, 1, :], sq[:, :, :], AX.X, ALU.add))
            dve.tensor_scalar(st[:, 1, :], st[:, 1, :], 1.0 / D, EPS, ALU.mult, ALU.add).then_inc(var_ready, 1)
            dve.wait_ge(root, 1)
            then(dve.reciprocal(st[:, 3, :], st[:, 2, :]))
            dve.scalar_tensor_tensor(out=T.H[:, :, :], in0=T.H[:, :, :], scalar=0.0, in1=wide(3),
                                     op0=ALU.max, op1=ALU.mult).then_inc(h_ready, 1)

        @block.scalar
        def _(act):
            act.wait_ge(centred, 1)
            act.activation(sq[:, :, :], T.H[:, :, :], ACT.Square).then_inc(squared, 1)
            act.wait_ge(var_ready, 1)
            act.activation(st[:, 2, :], st[:, 1, :], ACT.Sqrt).then_inc(root, 1)

        @block.sync
        def _(sp):
            if store:
                sp.wait_ge(h_ready, 1)
                sp.dma_start(T.h_table.rearrange("(t p) f -> p t f", p=P), T.H[:, :, :]).then_inc(stored, 16)
                sp.wait_ge(stored, 16)


def pipeline(eng, step, drain=()):
    step(0, 0, 0)
    step(1, 1, 1)
    with eng.Fori(0, (GROUPS - 2) // 4) as i:
        for k in range(2, 6):
            step(4 * i + k, k % 2, k % 4)
    for g in drain:
        step(g, g % 2, g % 4)


assert GROUPS % 4 == 2


def gathered_before(n, r):
    return n * 16 * G * len(range(r, GROUPS, 4))


def turns(g, r, each):
    return each * (g // 4 + 1) if isinstance(g, int) else (g - r) * (each // 4) + each


def wait_gathers(eng, T, n, g, r):
    eng.wait_ge(T.gathered[r], turns(g, r, 16 * G) + gathered_before(n, r))


def load_tiles(nc, eng, T, g):
    code = nc.s_assert_within(eng.value_load(T.tile_codes[0:1, bass.ds(g, 1)]), 0, (1 << CODE * G) - 1,
                              skip_runtime_bounds_check_because="setup packs G numbers of CODE bits")
    return [nc.s_assert_within(eng.snap((code >> (CODE * k)) & ((1 << CODE) - 1)), 0, TILES - 1,
                               skip_runtime_bounds_check_because="they are numbers of tiles") for k in range(G)]


def past(g, k):
    return not isinstance(g, int) or g >= k


def within(g):
    return not isinstance(g, int) or g < GROUPS


def edge_mlp_pass(nc, A, T):
    with ExitStack() as ctx:
        sb, ps, sem = stack(nc, ctx, "edge_mlp_pass_")
        we1 = sb("we1", [EF, D])
        be1 = sb("be1", [D, 1])
        we2 = sb("we2", [D, D])
        be2 = sb("be2", [1, D])
        one = sb("one", [1, P])
        attr = sb("attr_sb", [P, 2, G, P])
        attr_t = sb("attr_t", [EF, 2, G * P])
        hid = sb("hid", [P, 2, G * P])
        idx = sb("idx", [P, 4, G], I32)
        hx = sb("hx", [P, 4, G, D])
        oh = sb("oh", [P, 2, G, P])
        msg = sb("msg", [P, 2, G, D])
        p_at = [ps(f"p_at{i}", [P, 512]) for i in range(2)]
        p_h = [ps(f"p_h{i}", [P, 512]) for i in range(2)]
        p_w = [ps(f"p_w{i}", [P, G, D]) for i in range(2)]
        p_a = [ps(f"p_a{i}", [P, G, D]) for i in range(2)]
        params, set_up, attr_zero = sem("l0_params"), sem("l0_set_up"), sem("l0_attr_zero")
        attr_in = [sem(f"l0_attr_in{i}") for i in range(2)]
        attr_turned, attr_kept, hidden, acted = sem("l0_attr_turned"), sem("l0_attr_kept"), sem("l0_hidden"), sem("l0_acted")
        weighed, messages, summed = sem("l0_weighed"), sem("l0_messages"), sem("l0_summed")
        idx_ready, onehots, opened = sem("l0_idx_ready"), sem("l0_onehots"), sem("l0_opened")
        added = sem("l0_added")
        block = ctx.enter_context(nc.Block())
        chunks = T.attr.rearrange("(c p) f -> c p f", p=P)

        @block.sync
        def _(sp):
            sp.dma_start(we1[:, :], A["L0_gnn_We1"]).then_inc(params, 16)
            sp.dma_start(be1[:, :], A["L0_gnn_be1"].rearrange("(p o) -> p o", o=1)).then_inc(params, 16)
            sp.dma_start(we2[:, :], A["L0_gnn_We2"]).then_inc(params, 16)
            sp.dma_start(be2[:, :], A["L0_gnn_be2"].rearrange("(o f) -> o f", o=1)).then_inc(params, 16)
            sp.wait_ge(attr_zero, 1)

            def step(g, s, r):
                sp.wait_ge(attr_turned, g + 1)
                for k, tile in enumerate(load_tiles(nc, sp, T, g)):
                    chunk = nc.s_assert_within(sp.snap(g * G + k - tile), 0, VISITS - TILES,
                                               skip_runtime_bounds_check_because="a visit's number is its chunk plus its tile")
                    sp.dma_start(attr[:, s, k, 0:EF], chunks[bass.ds(chunk, 1)].rearrange("c p f -> (c p) f")).then_inc(attr_in[s], 16)

            pipeline(sp, step)

        @block.gpsimd
        def _(pool):
            bound = pool.to_reg(NP - 1)

            def step(g, s, r):
                pool.wait_ge(idx_ready, g + 3)
                if past(g, 2):
                    pool.wait_ge(messages, g - 1)
                pool.sem_inc(opened, 1)
                for k in range(G):
                    pool.indirect_dma_start(out=hx[:, r, k, :], out_offset=None, in_=T.h_table,
                                            in_offset=bass.IndirectOffsetOnAxis(ap=idx[:, r, k:k + 1].bitcast(U32), axis=0),
                                            bounds_check=bound).then_inc(T.gathered[r], 16)

            pipeline(pool, step)

        @block.scalar
        def _(act):
            act.sem_inc(idx_ready, 2)
            act.sem_inc(attr_kept, 2)
            act.sem_inc(acted, 2)
            act.wait_ge(params, 64)

            def step(g, s, r):
                if past(g, 2):
                    act.wait_ge(messages, g - 1)
                act.activation(idx[:, r, :], T.src[:, bass.ds(g * G, G)], ACT.Copy).then_inc(idx_ready, 1)
                act.wait_ge(attr_turned, g + 3)
                act.wait_ge(hidden, g + 1)
                act.activation(attr_t[:, s, :], p_at[s][0:EF, :], ACT.Copy).then_inc(attr_kept, 1)
                act.wait_ge(hidden, g + 3)
                act.wait_ge(weighed, g + 1)
                act.activation(hid[:, s, :], p_h[s][:, :], ACT.Silu, bias=be1[:, 0:1]).then_inc(acted, 1)

            pipeline(act, step)

        @block.tensor
        def _(pe):
            for q in (attr_turned, hidden, weighed, summed):
                pe.sem_inc(q, 2)
            pe.wait_ge(params, 64)
            pe.wait_ge(set_up, 2)

            def weigh(g, s):
                pe.wait_ge(acted, g + 3)
                pe.wait_ge(messages, g + 1)
                for k in range(G):
                    pe.matmul(p_w[s][:, k, :], hid[:, s, k * P:(k + 1) * P], we2[:, :], start=True, stop=False)
                    mm = pe.matmul(p_w[s][:, k, :], one[:, :], be2[:, :], start=False, stop=True)
                mm.then_inc(weighed, 1)

            def scatter(g, s):
                pe.wait_ge(messages, g + 3)
                pe.wait_ge(onehots, g + 3)
                if past(g, 2):
                    pe.wait_ge(added, (g - 1) * G + 1)
                for k in range(G):
                    mm = pe.matmul(p_a[s][:, k, :], oh[:, s, k, :], msg[:, s, k, :], start=True, stop=True)
                mm.then_inc(summed, 1)

            def step(g, s, r):
                if within(g):
                    if isinstance(g, int):
                        pe.wait_ge(attr_in[s], 16 * G * (g // 2 + 1))
                    else:
                        pe.wait_ge(attr_in[s], (g - s) * (8 * G) + 16 * G)
                    pe.wait_ge(attr_kept, g + 1)
                    for k in range(G):
                        tr = pe.transpose(p_at[s][:, k * P:(k + 1) * P], attr[:, s, k, :], T.ident[:, :])
                    tr.then_inc(attr_turned, 1)
                if past(g, 1):
                    weigh(g - 1, 1 - s)
                if within(g):
                    pe.wait_ge(attr_kept, g + 3)
                    pe.wait_ge(acted, g + 1)
                    pe.matmul(p_h[s][:, :], we1[:, :], attr_t[:, s, :], start=True, stop=True).then_inc(hidden, 1)
                if past(g, 1):
                    scatter(g - 1, 1 - s)

            pipeline(pe, step, drain=(GROUPS,))

        @block.vector
        def _(dve):
            dve.sem_inc(messages, 2)
            dve.sem_inc(onehots, 2)
            dve.sem_inc(added, 1)
            dve.memset(attr[:, :, :, :], 0.0).then_inc(attr_zero, 1)
            dve.memset(one[:, :], 1.0).then_inc(set_up, 1)
            dve.memset(T.agg[:, :, :], 0.0).then_inc(set_up, 1)
            dve.wait_ge(set_up, 2)

            def step(g, s, r):
                if within(g):
                    dve.wait_ge(summed, g + 1)
                    dve.tensor_tensor(oh[:, s, :, :], T.iota[:, :].unsqueeze(1).to_broadcast([P, G, P]),
                                      T.rel[:, bass.ds(g * G, G)].unsqueeze(2).to_broadcast([P, G, P]),
                                      ALU.is_equal).then_inc(onehots, 1)
                if past(g, 1) and within(g - 1):
                    h, q = g - 1, 1 - s
                    wait_gathers(dve, T, 0, h, (r - 1) % 4)
                    dve.wait_ge(weighed, h + 3)
                    dve.wait_ge(summed, h + 1)
                    dve.tensor_tensor(msg[:, q, :, :], hx[:, (r - 1) % 4, :, :], p_w[q][:, :, :], ALU.mult).then_inc(messages, 1)
                if past(g, 2):
                    h = g - 2
                    dve.wait_ge(summed, h + 3)
                    for k, t in enumerate(load_tiles(nc, dve, T, h)):
                        into = T.agg[:, bass.ds(t, 1), 0:D].rearrange("p t f -> p (t f)")
                        dve.wait_ge(added, h * G + k + 1)
                        dve.tensor_tensor(into, into, p_a[s][:, k, :], ALU.add).then_inc(added, 1)

            pipeline(dve, step, drain=(GROUPS, GROUPS + 1))


def node_mlp(nc, A, T):
    with ExitStack() as ctx:
        sb, ps, sem = stack(nc, ctx, "node_mlp_")
        w1, b1, w2, b2 = sb("wn1", [D, D]), sb("bn1", [D, 1]), sb("wn2", [D, D]), sb("bn2", [1, D])
        one = sb("one_n0", [1, P])
        agg_t, hid = sb("agg_t", [P, 2, 512]), sb("hid_n0", [P, 2, 512])
        p_t = [ps(f"p_t{i}", [P, 512]) for i in range(2)]
        p_h = [ps(f"p_h{i}", [P, 512]) for i in range(2)]
        p_o = [ps(f"p_o{i}", [P, 4, D]) for i in range(2)]
        params, set_up, chain = sem("n0_params"), sem("n0_set_up"), sem("n0_chain")
        turned, kept, hidden, acted, made, taken = (sem("n0_" + n) for n in ("turned", "kept", "hidden", "acted", "made", "taken"))
        block = ctx.enter_context(nc.Block())

        @block.sync
        def _(sp):
            sp.dma_start(w1[:, :], A["L0_gnn_Wn1"]).then_inc(params, 16)
            sp.dma_start(b1[:, :], A["L0_gnn_bn1"].rearrange("(p o) -> p o", o=1)).then_inc(params, 16)
            sp.dma_start(w2[:, :], A["L0_gnn_Wn2"]).then_inc(params, 16)
            sp.dma_start(b2[:, :], A["L0_gnn_bn2"].rearrange("(o f) -> o f", o=1)).then_inc(params, 16)

        @block.tensor
        def _(pe):
            def out(b):
                t0, n = BLOCKS[b]
                pe.wait_ge(acted, b + 1)
                if b >= 2:
                    pe.wait_ge(taken, b - 1)
                for k in range(n):
                    pe.matmul(p_o[b % 2][:, k, :], hid[:, b % 2, k * P:(k + 1) * P], w2[:, :], start=True, stop=False)
                    mm = pe.matmul(p_o[b % 2][:, k, :], one[:, :], b2[:, :], start=False, stop=True)
                mm.then_inc(made, 1)

            pe.wait_ge(set_up, 1)
            for b, (t0, n) in enumerate(BLOCKS):
                if b >= 2:
                    pe.wait_ge(kept, b - 1)
                for k in range(n):
                    tr = pe.transpose(p_t[b % 2][:, k * P:(k + 1) * P], T.agg[:, t0 + k, 0:D], T.ident[:, :])
                tr.then_inc(turned, 1)
                if b == 0:
                    pe.wait_ge(params, 64)
                else:
                    out(b - 1)
                pe.wait_ge(kept, b + 1)
                if b >= 2:
                    pe.wait_ge(acted, b - 1)
                pe.matmul(p_h[b % 2][:, 0:n * P], w1[:, :], agg_t[:, b % 2, 0:n * P], start=True, stop=True).then_inc(hidden, 1)
            out(len(BLOCKS) - 1)

        @block.scalar
        def _(act):
            act.wait_ge(params, 64)
            for b, (t0, n) in enumerate(BLOCKS):
                act.wait_ge(turned, b + 1)
                if b >= 2:
                    act.wait_ge(hidden, b - 1)
                act.activation(agg_t[:, b % 2, 0:n * P], p_t[b % 2][:, 0:n * P], ACT.Copy).then_inc(kept, 1)
                act.wait_ge(hidden, b + 1)
                if b >= 2:
                    act.wait_ge(made, b - 1)
                act.activation(hid[:, b % 2, 0:n * P], p_h[b % 2][:, 0:n * P], ACT.Silu, bias=b1[:, 0:1]).then_inc(acted, 1)

        @block.vector
        def _(dve):
            then = Chain(dve, chain)
            dve.memset(one[:, :], 1.0).then_inc(set_up, 1)
            then(dve.tensor_tensor(T.X[:, :, :], T.X[:, :, :], T.H[:, :, :], ALU.add))
            for b, (t0, n) in enumerate(BLOCKS):
                dve.wait_ge(made, b + 1)
                dve.tensor_tensor(T.X[:, t0:t0 + n, :], T.X[:, t0:t0 + n, :], p_o[b % 2][:, 0:n, :], ALU.add).then_inc(taken, 1)


BANK = 512
PARTS = 3


class AggInPsum:

    def __init__(self, sb, ps, sem, weights=False):
        banks = TBANKS + 1 if weights else TBANKS
        self.all = ps("sums", [P, banks, BANK])
        flat = self.all[:, :, :].rearrange("p b c -> p (b c)")
        self.sums = flat[:, 0:TILES * D].rearrange("p (t f) -> p t f", f=D)
        if weights:
            per_tile = PARTS * HEADS
            self.in_first = (TBANKS * BANK - TILES * D) // per_tile
            assert (TBANKS * BANK - TILES * D) % per_tile == 0
            self.weights = flat[:, TILES * D:TILES * (D + per_tile)].rearrange("p (t c) -> p t c", c=per_tile)
        self.nil = sb("nil", [P, BANK], BF16)
        self.banks, self.has_weights = banks, weights
        self.nil_ready, self.closed = sem("nil_ready"), sem("sums_closed")

    def clear(self, dve):
        dve.memset(self.nil[:, :], 0.0).then_inc(self.nil_ready, 1)

    def sweep(self, pe, first):
        if first:
            pe.wait_ge(self.nil_ready, 1)
        for b in range(self.banks):
            mm = pe.matmul(self.all[:, b, :], self.nil[:, 0:P], self.nil[:, :], start=first, stop=not first, skip_group_check=True)
        if not first:
            mm.then_inc(self.closed, 1)

    def add(self, pe, tile, onehot, rows):
        return pe.matmul(self.sums[:, bass.ds(tile, 1), :].rearrange("p t f -> p (t f)"), onehot, rows,
                         start=False, stop=False, skip_group_check=True)

    def add_weights(self, pe, tile, onehot, parts):
        return pe.matmul(self.weights[:, bass.ds(tile, 1), :].rearrange("p t c -> p (t c)"), onehot, parts,
                         start=False, stop=False, skip_group_check=True)

    def store(self, dve, T):
        dve.wait_ge(self.closed, 1)
        for b, (t0, n) in enumerate(BLOCKS):
            dve.tensor_copy(T.agg[:, t0:t0 + n, 0:D], self.sums[:, t0:t0 + n, :])
        if self.has_weights:
            for these in (slice(0, self.in_first), slice(self.in_first, TILES)):
                dve.tensor_reduce(T.agg[:, these, D:AW], self.weights[:, these, :].rearrange("p t (c h) -> p t h c", h=HEADS), AX.X, ALU.add)


def sum_pass(nc, A, T):
    with ExitStack() as ctx:
        sb, ps, sem = stack(nc, ctx, "sum_pass_")
        idx = sb("idx1", [P, 4, G], I32)
        hx = sb("hx1", [P, 4, G, D])
        oh = sb("oh1", [P, 2, G, P])
        agg = AggInPsum(sb, ps, sem)
        summed, idx_ready, onehots = sem("l1_summed"), sem("l1_idx_ready"), sem("l1_onehots")
        opened = sem("l1_opened")
        block = ctx.enter_context(nc.Block())

        @block.gpsimd
        def _(pool):
            bound = pool.to_reg(NP - 1)

            def step(g, s, r):
                pool.wait_ge(idx_ready, g + 3)
                if past(g, 2):
                    pool.wait_ge(summed, g - 1)
                pool.sem_inc(opened, 1)
                for k in range(G):
                    pool.indirect_dma_start(out=hx[:, r, k, :], out_offset=None, in_=T.h_table,
                                            in_offset=bass.IndirectOffsetOnAxis(ap=idx[:, r, k:k + 1].bitcast(U32), axis=0),
                                            bounds_check=bound).then_inc(T.gathered[r], 16)

            pipeline(pool, step)

        @block.scalar
        def _(act):
            act.sem_inc(idx_ready, 2)

            def step(g, s, r):
                if past(g, 2):
                    act.wait_ge(summed, g - 1)
                act.activation(idx[:, r, :], T.src[:, bass.ds(g * G, G)], ACT.Copy).then_inc(idx_ready, 1)

            pipeline(act, step)

        @block.tensor
        def _(pe):
            pe.sem_inc(summed, 2)
            agg.sweep(pe, True)

            def step(g, s, r):
                tiles = load_tiles(nc, pe, T, g)
                pe.wait_ge(onehots, g + 3)
                wait_gathers(pe, T, 1, g, r)
                for k in range(G):
                    mm = agg.add(pe, tiles[k], oh[:, s, k, :], hx[:, r, k, :])
                mm.then_inc(summed, 1)

            pipeline(pe, step)
            agg.sweep(pe, False)

        @block.vector
        def _(dve):
            dve.sem_inc(onehots, 2)
            agg.clear(dve)

            def step(g, s, r):
                dve.wait_ge(summed, g + 1)
                dve.tensor_tensor(oh[:, s, :, :], T.iota[:, :].unsqueeze(1).to_broadcast([P, G, P]),
                                  T.rel[:, bass.ds(g * G, G)].unsqueeze(2).to_broadcast([P, G, P]),
                                  ALU.is_equal).then_inc(onehots, 1)

            pipeline(dve, step)
            agg.store(dve, T)


class Batchnorm:

    def __init__(self, sb, sem, name, Y):
        self.Y, self.sq = Y, sb(name + "_sq", [P, N])
        self.st, self.gb = sb(name + "_st", [P, 6]), sb(name + "_gb", [P, 2])
        self.centred, self.squared, self.var_ready, self.root, self.scaled, self.done, self.params = (
            sem(name + n) for n in ("_centred", "_squared", "_var", "_root", "_scaled", "_done", "_gb_in"))

    def load(self, sp, gamma, beta):
        sp.dma_start(self.gb[:, 0:1], gamma.rearrange("(p o) -> p o", o=1)).then_inc(self.params, 16)
        sp.dma_start(self.gb[:, 1:2], beta.rearrange("(p o) -> p o", o=1)).then_inc(self.params, 16)

    def on_vector(self, dve, then):
        st, Y = self.st, self.Y
        then(dve.tensor_reduce(st[:, 0:1], Y[:, 0:N], AX.X, ALU.add))
        then(dve.tensor_scalar(st[:, 0:1], st[:, 0:1], 1.0 / N, None, ALU.mult))
        dve.tensor_scalar(Y[:, :], Y[:, :], st[:, 0:1], None, ALU.subtract).then_inc(self.centred, 1)
        dve.wait_ge(self.squared, 1)
        then(dve.tensor_reduce(st[:, 1:2], self.sq[:, :], AX.X, ALU.add))
        dve.tensor_scalar(st[:, 1:2], st[:, 1:2], 1.0 / N, EPS, ALU.mult, ALU.add).then_inc(self.var_ready, 1)
        dve.wait_ge(self.root, 1)
        then(dve.reciprocal(st[:, 3:4], st[:, 2:3]))
        dve.wait_ge(self.params, 32)
        dve.tensor_tensor(st[:, 4:5], st[:, 3:4], self.gb[:, 0:1], ALU.mult).then_inc(self.scaled, 1)

    def on_scalar(self, act, func):
        st, Y = self.st, self.Y
        act.wait_ge(self.centred, 1)
        act.activation(self.sq[:, :], Y[:, 0:N], ACT.Square).then_inc(self.squared, 1)
        act.wait_ge(self.var_ready, 1)
        act.activation(st[:, 2:3], st[:, 1:2], ACT.Sqrt).then_inc(self.root, 1)
        act.wait_ge(self.scaled, 1)
        act.activation(Y[:, :], Y[:, :], func, bias=self.gb[:, 1:2], scale=st[:, 4:5]).then_inc(self.done, 1)


def node_gin(nc, A, T):
    with ExitStack() as ctx:
        sb, ps, sem = stack(nc, ctx, "node_gin_")
        w1, w2 = sb("w1", [D, D]), sb("w2", [D, D])
        bias = sb("bias_n1", [P, 3])
        Z, Y = sb("Z", [P, TILES, D]), sb("Y", [P, NP])
        in_t, hid = sb("in_t", [P, 2, 512]), sb("hid_n1", [P, 2, 512])
        p_t = [ps(f"p_t{i}", [P, 512]) for i in range(2)]
        p_h = [ps(f"p_h{i}", [P, 512]) for i in range(2)]
        p_y = [ps(f"p_y{i}", [P, 512]) for i in range(2)]
        p_b = [ps(f"p_b{i}", [P, 4, D]) for i in range(2)]
        params, chain, z_ready = sem("n1_params"), sem("n1_chain"), sem("n1_z_ready")
        turned, kept, hidden, acted, made, y_ready, back, taken = (
            sem("n1_" + n) for n in ("turned", "kept", "hidden", "acted", "made", "y_ready", "back", "taken"))
        bn = Batchnorm(sb, sem, "bn1_", Y)
        block = ctx.enter_context(nc.Block())
        NB = len(BLOCKS)

        @block.sync
        def _(sp):
            sp.dma_start(bias[:, 2:3], A["L1_gnn_eps"].partition_broadcast(P)).then_inc(params, 16)
            sp.dma_start(w1[:, :], A["L1_gnn_W1"]).then_inc(params, 16)
            sp.dma_start(w2[:, :], A["L1_gnn_W2"]).then_inc(params, 16)
            sp.dma_start(bias[:, 0:1], A["L1_gnn_b1"].rearrange("(p o) -> p o", o=1)).then_inc(params, 16)
            sp.dma_start(bias[:, 1:2], A["L1_gnn_b2"].rearrange("(p o) -> p o", o=1)).then_inc(params, 16)
            bn.load(sp, A["L1_gnn_gamma"], A["L1_gnn_beta"])

        @block.tensor
        def _(pe):
            pe.wait_ge(z_ready, 1)
            pe.wait_ge(params, 80)
            for b, (t0, n) in enumerate(BLOCKS):
                if b >= 2:
                    pe.wait_ge(kept, b - 1)
                for k in range(n):
                    tr = pe.transpose(p_t[b % 2][:, k * P:(k + 1) * P], Z[:, t0 + k, :], T.ident[:, :])
                tr.then_inc(turned, 1)
                pe.wait_ge(kept, b + 1)
                if b >= 2:
                    pe.wait_ge(acted, b - 1)
                pe.matmul(p_h[b % 2][:, 0:n * P], w1[:, :], in_t[:, b % 2, 0:n * P], start=True, stop=True).then_inc(hidden, 1)
                pe.wait_ge(acted, b + 1)
                if b >= 2:
                    pe.wait_ge(y_ready, b - 1)
                pe.matmul(p_y[b % 2][:, 0:n * P], w2[:, :], hid[:, b % 2, 0:n * P], start=True, stop=True).then_inc(made, 1)
            pe.wait_ge(bn.done, 1)
            for b, (t0, n) in enumerate(BLOCKS):
                if b >= 2:
                    pe.wait_ge(taken, b - 1)
                for k in range(n):
                    tr = pe.transpose(p_b[b % 2][:, k, :], Y[:, (t0 + k) * P:(t0 + k + 1) * P], T.ident[:, :])
                tr.then_inc(back, 1)

        @block.scalar
        def _(act):
            act.wait_ge(params, 80)
            for b, (t0, n) in enumerate(BLOCKS):
                act.wait_ge(turned, b + 1)
                if b >= 2:
                    act.wait_ge(hidden, b - 1)
                act.activation(in_t[:, b % 2, 0:n * P], p_t[b % 2][:, 0:n * P], ACT.Copy).then_inc(kept, 1)
                act.wait_ge(hidden, b + 1)
                if b >= 2:
                    act.wait_ge(made, b - 1)
                act.activation(hid[:, b % 2, 0:n * P], p_h[b % 2][:, 0:n * P], ACT.Relu, bias=bias[:, 0:1]).then_inc(acted, 1)
                act.wait_ge(made, b + 1)
                act.activation(Y[:, t0 * P:(t0 + n) * P], p_y[b % 2][:, 0:n * P], ACT.Identity, bias=bias[:, 1:2]).then_inc(y_ready, 1)
            bn.on_scalar(act, ACT.Relu)

        @block.vector
        def _(dve):
            then = Chain(dve, chain)
            dve.wait_ge(params, 80)
            then(dve.tensor_scalar(bias[:, 2:3], bias[:, 2:3], 1.0, None, ALU.add))
            dve.scalar_tensor_tensor(out=Z[:, :, :], in0=T.H[:, :, :], scalar=bias[:, 2:3], in1=T.agg[:, :, 0:D],
                                     op0=ALU.mult, op1=ALU.add).then_inc(z_ready, 1)
            dve.wait_ge(y_ready, NB)
            bn.on_vector(dve, then)
            for b, (t0, n) in enumerate(BLOCKS):
                dve.wait_ge(back, b + 1)
                dve.tensor_tensor(T.X[:, t0:t0 + n, :], T.X[:, t0:t0 + n, :], p_b[b % 2][:, 0:n, :], ALU.add).then_inc(taken, 1)


def scan_flags(nc, A, T):
    with ExitStack() as ctx:
        sb, ps, sem = stack(nc, ctx, "scan_flags_")
        keys = sb("keys", [P, LE + 2])
        shift = sb("shift", [P, 2, P])
        whole = sb("whole", [P, 2])
        nti, nbi = sb("nti", [TILES, P], I32), sb("nbi", [P, NP], I32)
        ntf = sb("ntf", [TILES, P])
        typed = sem("typed")
        p_k = [ps(f"p_k{i}", [P, 4, P]) for i in range(2)]
        p_e, p_r = ps("p_e", [P, 512]), ps("p_r", [P, 512])
        chain, turned, taken, shifts, edges, set_up = (sem("fl_" + n) for n in ("chain", "turned", "taken", "shifts", "edges", "set_up"))
        wholes, rows, types_in = sem("fl_wholes"), sem("fl_rows"), sem("fl_types_in")
        block = ctx.enter_context(nc.Block())
        spread = sem("spread")
        lanes = T.att[:, :, :].rearrange("p v h -> p (v h)").rearrange("p (j l h) -> p j l h", l=LANES, h=HEADS)
        quads = [(j, min(4, LV - j)) for j in range(0, LV, 4)]

        @block.sync
        def _(sp):
            full = N // P
            sp.wait_ge(set_up, 2)
            nt = A["node_type_8"]
            sp.dma_start(nti[0:full, :], nt[0:full * P].rearrange("(t p) -> t p", p=P)).then_inc(types_in, 16)
            sp.dma_start(nti[full:full + 1, 0:N - full * P], nt[full * P:N].rearrange("(o p) -> o p", o=1)).then_inc(types_in, 16)
            sp.dma_start(nbi[:, 0:N], nt.partition_broadcast(P)).then_inc(types_in, 16)

        @block.gpsimd
        def _(pool):
            pool.memset(shift[:, :, :], 0.0).then_inc(shifts, 1)
            pool.wait_ge(shifts, 1)
            pool.affine_select(out=shift[:, 0, :], in_=shift[:, 0, :], compare_op=ALU.not_equal, fill=1.0, base=HEADS,
                               pattern=[[-1, P]], channel_multiplier=1).then_inc(shifts, 1)
            pool.affine_select(out=shift[:, 1, :], in_=shift[:, 1, :], compare_op=ALU.not_equal, fill=1.0, base=-HEADS,
                               pattern=[[-1, P]], channel_multiplier=1).then_inc(shifts, 1)

        @block.tensor
        def _(pe):
            pe.wait_ge(spread, 1)
            for b, (j, n) in enumerate(quads):
                if b >= 2:
                    pe.wait_ge(taken, b - 1)
                for k in range(n):
                    tr = pe.transpose(p_k[b % 2][:, k, :], lanes[:, j + k].rearrange("p l h -> p (l h)"), T.ident[:, :])
                tr.then_inc(turned, 1)
            pe.wait_ge(taken, len(quads))
            pe.wait_ge(shifts, 3)
            pe.matmul(p_e[:, 0:1], shift[:, 0, :], keys[:, LE:LE + 1], start=True, stop=True)
            pe.matmul(p_e[:, 1:2], shift[:, 1, :], keys[:, 1:2], start=True, stop=True).then_inc(edges, 1)
            pe.wait_ge(wholes, 1)
            pe.transpose(p_r[0:1, 0:P], whole[:, 0:1], T.ident[:, :])
            pe.transpose(p_r[0:1, P:2 * P], whole[:, 1:2], T.ident[:, :]).then_inc(rows, 1)
            pe.wait_ge(typed, 1)
            pe.transpose(p_e[:, 2:2 + TILES], ntf[:, :], T.ident[0:TILES, 0:TILES]).then_inc(rows, 1)

        @block.vector
        def _(dve):
            then = Chain(dve, chain)
            dve.memset(nti[:, :], -1).then_inc(set_up, 1)
            dve.memset(nbi[:, :], -1).then_inc(set_up, 1)
            dve.tensor_copy(lanes, T.key[:, 0:SV].rearrange("p (l j) -> p j l", j=LV).unsqueeze(3).to_broadcast([P, LV, LANES, HEADS])).then_inc(spread, 1)
            for b, (j, n) in enumerate(quads):
                dve.wait_ge(turned, b + 1)
                dve.tensor_copy(keys[:, 1 + j * P:1 + (j + n) * P], p_k[b % 2][:, 0:n, :].rearrange("p k e -> p (k e)")).then_inc(taken, 1)
            dve.wait_ge(edges, 1)
            then(dve.tensor_copy(keys[:, 0:1], p_e[:, 0:1]))
            then(dve.tensor_copy(keys[:, LE + 1:LE + 2], p_e[:, 1:2]))
            then(dve.tensor_tensor(T.flag[:, :], keys[:, 1:LE + 2], keys[:, 0:LE + 1], ALU.not_equal))
            then(dve.tensor_scalar(T.flag[:, :], T.flag[:, :], -BIG, None, ALU.mult))
            then(dve.tensor_reduce(whole[:, 0:1], T.flag[:, 0:LE], AX.X, ALU.min))
            then(dve.tensor_reduce(whole[:, 1:2], T.flag[:, 1:LE + 1], AX.X, ALU.min))
            dve.sem_inc(wholes, 1)
            dve.wait_ge(rows, 1)
            dve.tensor_copy(T.whole[:, :, :], p_r[0:1, 0:2 * P].rearrange("o (k p) -> o k p", k=2))
            dve.wait_ge(types_in, 48)
            dve.tensor_copy(ntf[:, :], nti[:, :]).then_inc(typed, 1)
            dve.wait_ge(rows, 2)
            dve.tensor_copy(T.type_of[:, :], p_e[:, 2:2 + TILES])
            dve.tensor_copy(T.type_row[:, :], nbi[:, :])
            dve.memset(T.att[:, VISITS:SV, :], 0.0)


def typed_qkv(nc, A, T, l):
    with ExitStack() as ctx:
        sb, ps, sem = stack(nc, ctx)
        nm = f"qkv{l}_"
        w = [sb(f"{nm}w{k}", [D, TYPES, D]) for k in range(3)]
        bd = [sb(f"{nm}bd{k}", [D, REL, D]) for k in range(2)]
        pri = sb(nm + "pri", [P, REL])
        e_t = sb(nm + "e_t", [P, 512])
        xm = sb(nm + "xm", [P, TYPES, 512])
        kv_t = sb(nm + "kv_t", [P, 2, 512])
        rows = sb(nm + "rows", [P, 2, REL, 2, D])
        p_t, p_q = ps(nm + "p_t", [P, 512]), ps(nm + "p_q", [P, 4, D])
        p_kv = [ps(f"{nm}p_kv{k}", [P, 512]) for k in range(2)]
        p_r = [ps(f"{nm}p_r{k}", [P, 4, D]) for k in range(4)]
        params, zeroed, chain, bd_ready = (sem(nm + n) for n in ("params", "zeroed", "chain", "bd_ready"))
        turned, kept, masked, projected, cast, q_made, q_kept = (
            sem(nm + n) for n in ("turned", "kept", "masked", "projected", "cast", "q_made", "q_kept"))
        related = sem(nm + "related")
        by_act, by_dve = sem(nm + "by_act"), sem(nm + "by_dve")
        stored = [sem(f"{nm}stored{i}") for i in range(2)]
        block = ctx.enter_context(nc.Block())
        table = T.kv_table.rearrange("(n r) (c f) -> n r c f", r=REL, f=D)

        @block.sync
        def _(sp):
            for k, name in enumerate(("Wk", "Wv", "Wq")):
                sp.dma_start(w[k][:, :, :], A["L2_gnn_" + name][l].rearrange("t i o -> i t o")).then_inc(params, 16)
            sp.wait_ge(zeroed, 2)
            for h in range(HEADS):
                of = slice(h * HS, (h + 1) * HS)
                sp.dma_start(bd[0][of, :, of], A["L2_gnn_Watt"][l, h].rearrange("r i o -> i r o")).then_inc(params, 16)
                sp.dma_start(bd[1][of, :, of], A["L2_gnn_Wmsg"][l, h].rearrange("r i o -> i r o")).then_inc(params, 16)
                sp.dma_start(pri[of, :], A["L2_gnn_pri"][l, h].partition_broadcast(HS)).then_inc(params, 16)
            for t in range(TILES):
                sp.wait_ge(by_act, 2 * (t + 1))
                sp.wait_ge(by_dve, 2 * (t + 1))
                sp.dma_start(table[t * P:(t + 1) * P], rows[:, t % 2]).then_inc(stored[t % 2], 16)
            sp.wait_ge(stored[0], 16 * ((TILES + 1) // 2))
            sp.wait_ge(stored[1], 16 * (TILES // 2))

        @block.tensor
        def _(pe):
            pe.wait_ge(params, 16 * (3 + 3 * HEADS))
            for b, (t0, n) in enumerate(BLOCKS):
                if b >= 1:
                    pe.wait_ge(kept, b)
                for k in range(n):
                    tr = pe.transpose(p_t[:, k * P:(k + 1) * P], T.H[:, t0 + k, :], T.ident[:, :])
                tr.then_inc(turned, 1)
                pe.wait_ge(masked, b + 1)
                for c in range(2):
                    if b >= 1:
                        pe.wait_ge(cast, 2 * b - 1 + c)
                    for t in range(TYPES):
                        mm = pe.matmul(p_kv[c][:, 0:n * P], w[c][:, t, :], xm[:, t, 0:n * P], start=(t == 0), stop=(t == TYPES - 1))
                    mm.then_inc(projected, 1)
                if b >= 1:
                    pe.wait_ge(q_kept, b)
                for k in range(n):
                    for t in range(TYPES):
                        mm = pe.matmul(p_q[:, k, :], xm[:, t, k * P:(k + 1) * P], w[2][:, t, :], start=(t == 0), stop=(t == TYPES - 1))
                mm.then_inc(q_made, 1)
                pe.wait_ge(cast, 2 * (b + 1))
                pe.wait_ge(bd_ready, 1)
                for k in range(n):
                    t = t0 + k
                    for c in range(2):
                        for half in range(2):
                            if t >= 1:
                                pe.wait_ge(by_dve if c else by_act, 2 * t - 1 + half)
                            pe.matmul(p_r[2 * c + half][:, :, :], kv_t[:, c, k * P:(k + 1) * P],
                                      bd[c][:, 4 * half:4 * half + 4, :], start=True, stop=True).then_inc(related, 1)

        @block.scalar
        def _(act):
            for b, (t0, n) in enumerate(BLOCKS):
                act.wait_ge(turned, b + 1)
                if b >= 1:
                    act.wait_ge(masked, b)
                act.activation(e_t[:, 0:n * P], p_t[:, 0:n * P], ACT.Copy).then_inc(kept, 1)
                for c in range(2):
                    act.wait_ge(projected, 2 * b + c + 1)
                    if b >= 1:
                        act.wait_ge(related, 4 * t0)
                    act.activation(kv_t[:, c, 0:n * P], p_kv[c][:, 0:n * P], ACT.Copy).then_inc(cast, 1)
                act.wait_ge(q_made, b + 1)
                act.activation(T.Q[:, t0:t0 + n, :], p_q[:, 0:n, :], ACT.Copy).then_inc(q_kept, 1)
                for k in range(n):
                    t = t0 + k
                    if t >= 2:
                        act.wait_ge(stored[t % 2], 16 * (t // 2))
                    for half in range(2):
                        act.wait_ge(related, 4 * t + half + 1)
                        act.activation(rows[:, t % 2, 4 * half:4 * half + 4, 0, :], p_r[half][:, :, :], ACT.Copy).then_inc(by_act, 1)

        @block.vector
        def _(dve):
            then = Chain(dve, chain)
            for c in range(2):
                dve.memset(bd[c][:, :, :], 0.0).then_inc(zeroed, 1)
            dve.wait_ge(params, 16 * (3 + 3 * HEADS))
            then(dve.tensor_scalar(pri[:, :], pri[:, :], 1.0 / float(HS) ** 0.5, None, ALU.mult))
            dve.tensor_tensor(bd[0][:, :, :], bd[0][:, :, :], pri[:, :].unsqueeze(2).to_broadcast([P, REL, D]), ALU.mult).then_inc(bd_ready, 1)
            for b, (t0, n) in enumerate(BLOCKS):
                dve.wait_ge(kept, b + 1)
                if b >= 1:
                    dve.wait_ge(q_made, b)
                for t in range(TYPES):
                    ins = dve.scalar_tensor_tensor(out=xm[:, t, 0:n * P], in0=T.type_row[:, t0 * P:(t0 + n) * P], scalar=float(t),
                                                   in1=e_t[:, 0:n * P], op0=ALU.is_equal, op1=ALU.mult)
                ins.then_inc(masked, 1)
                for k in range(n):
                    t = t0 + k
                    if t >= 2:
                        dve.wait_ge(stored[t % 2], 16 * (t // 2))
                    for half in range(2):
                        dve.wait_ge(related, 4 * t + half + 3)
                        dve.tensor_copy(rows[:, t % 2, 4 * half:4 * half + 4, 1, :], p_r[2 + half][:, :, :]).then_inc(by_dve, 1)


def score_pass(nc, A, T, l):
    with ExitStack() as ctx:
        sb, ps, sem = stack(nc, ctx)
        nm = f"sc{l}_"
        idx = sb(nm + "idx", [P, 4, G], I32)
        kv = sb(nm + "kv", [P, 4, G, 2 * D])
        oh = sb(nm + "oh", [P, 2, G, P])
        oh_t = sb(nm + "oh_t", [P, 2, G, P])
        prod = sb(nm + "prod", [P, G, D])
        p_t = [ps(f"{nm}p_t{i}", [P, G, P]) for i in range(2)]
        p_q = [ps(f"{nm}p_q{i}", [P, G, D]) for i in range(2)]
        m_out = [sem(f"{nm}m_out{i}") for i in range(4)]
        idx_ready, onehots, turned, kept, spread, scored = (sem(nm + n) for n in ("idx_ready", "onehots", "turned", "kept", "spread", "scored"))
        opened, multiplied = sem(nm + "opened"), sem(nm + "multiplied")
        block = ctx.enter_context(nc.Block())
        m_slots = T.m_table.rearrange("(v p) f -> p v f", p=P)

        @block.sync
        def _(sp):
            def step(g, s, r):
                wait_gathers(sp, T, 2 + l, g, r)
                sp.dma_start(m_slots[:, bass.ds(g * G, G), :], kv[:, r, :, D:2 * D]).then_inc(m_out[r], 16)

            pipeline(sp, step)
            for r in range(4):
                sp.wait_ge(m_out[r], 16 * (len(range(r, GROUPS, 4)) + 1))

        @block.gpsimd
        def _(pool):
            bound = pool.to_reg(NP * REL - 1)
            for r in range(4):
                pool.sem_inc(m_out[r], 16)

            def step(g, s, r):
                pool.wait_ge(idx_ready, g + 3)
                if past(g, 2):
                    pool.wait_ge(scored, g - 1)
                pool.wait_ge(m_out[r], turns(g, r, 16))
                pool.sem_inc(opened, 1)
                for k in range(G):
                    pool.indirect_dma_start(out=kv[:, r, k, :], out_offset=None, in_=T.kv_table,
                                            in_offset=bass.IndirectOffsetOnAxis(ap=idx[:, r, k:k + 1].bitcast(U32), axis=0),
                                            bounds_check=bound).then_inc(T.gathered[r], 16)

            pipeline(pool, step)

        @block.scalar
        def _(act):
            act.sem_inc(idx_ready, 2)
            act.sem_inc(kept, 2)

            def step(g, s, r):
                if past(g, 2):
                    act.wait_ge(scored, g - 1)
                act.activation(idx[:, r, :], T.srcrel[:, bass.ds(g * G, G)], ACT.Copy).then_inc(idx_ready, 1)
                act.wait_ge(turned, g + 3)
                act.wait_ge(spread, g + 1)
                act.activation(oh_t[:, s, :, :], p_t[s][:, :, :], ACT.Copy).then_inc(kept, 1)

            pipeline(act, step)

        @block.tensor
        def _(pe):
            pe.sem_inc(turned, 2)
            pe.sem_inc(spread, 2)

            def step(g, s, r):
                pe.wait_ge(onehots, g + 3)
                pe.wait_ge(kept, g + 1)
                tiles = load_tiles(nc, pe, T, g)
                for k in range(G):
                    tr = pe.transpose(p_t[s][:, k, :], oh[:, s, k, :], T.ident[:, :])
                tr.then_inc(turned, 1)
                pe.wait_ge(kept, g + 3)
                pe.wait_ge(scored, g + 1)
                for k in range(G):
                    q = T.Q[:, bass.ds(tiles[k], 1), :].rearrange("p t f -> p (t f)")
                    mm = pe.matmul(p_q[s][:, k, :], oh_t[:, s, k, :], q, start=True, stop=True)
                mm.then_inc(spread, 1)

            pipeline(pe, step)

        @block.vector
        def _(dve):
            dve.sem_inc(onehots, 2)
            dve.sem_inc(scored, 2)

            def step(g, s, r):
                if within(g):
                    dve.wait_ge(turned, g + 1)
                    dve.tensor_tensor(oh[:, s, :, :], T.iota[:, :].unsqueeze(1).to_broadcast([P, G, P]),
                                      T.rel[:, bass.ds(g * G, G)].unsqueeze(2).to_broadcast([P, G, P]),
                                      ALU.is_equal).then_inc(onehots, 1)
                if past(g, 1):
                    h, q = g - 1, 1 - s
                    wait_gathers(dve, T, 2 + l, h, (r - 1) % 4)
                    dve.wait_ge(spread, h + 3)
                    if past(h, 1):
                        dve.wait_ge(scored, h + 2)
                    dve.tensor_tensor(prod[:, :, :], kv[:, (r - 1) % 4, :, 0:D], p_q[q][:, :, :], ALU.mult).then_inc(multiplied, 1)
                    dve.wait_ge(multiplied, h + 1)
                    dve.tensor_reduce(T.att[:, bass.ds(h * G, G), :].rearrange("p v h -> p (v h)"),
                                      prod[:, :, :].rearrange("p k (h o) -> p (k h) o", o=HS), AX.X, ALU.add).then_inc(scored, 1)

            pipeline(dve, step, drain=(GROUPS,))


def softmax_shift(nc, A, T, l):
    with ExitStack() as ctx:
        sb, ps, sem = stack(nc, ctx)
        nm = f"mx{l}_"
        a_t, top = sb(nm + "a_t", [P, LE]), sb(nm + "top", [P, LE])
        whole_max = T.att[:, :, :].rearrange("p v h -> p (v h)")
        ends, into = sb(nm + "ends", [1, 2, P]), sb(nm + "into", [1, 2, P])
        start = sb(nm + "start", [P, 2])
        p_l = [ps(f"{nm}p_l{i}", [P, 4, P]) for i in range(3)]
        p_e, p_s = ps(nm + "p_e", [P, 512]), ps(nm + "p_s", [P, 512])
        chain, turned, by_act, by_dve, ended, row_made, carried, started = (
            sem(nm + n) for n in ("chain", "turned", "by_act", "by_dve", "ended", "row_made", "carried", "started"))
        shifted, exped, back, placed = (sem(nm + n) for n in ("shifted", "exped", "back", "placed"))
        block = ctx.enter_context(nc.Block())
        lanes = top[:, :].rearrange("p (j l h) -> p j l h", l=LANES, h=HEADS)
        ordered = sem(nm + "ordered")
        quads = [(j, min(4, LV - j)) for j in range(0, LV, 4)]
        NQ = len(quads)

        @block.tensor
        def _(pe):
            pe.wait_ge(ordered, 1)
            for b, (j, n) in enumerate(quads):
                if b >= 3:
                    pe.wait_ge(by_act, b - 2)
                for k in range(n):
                    tr = pe.transpose(p_l[b % 3][:, k, :], lanes[:, j + k].rearrange("p l h -> p (l h)"), T.ident[:, :])
                tr.then_inc(turned, 1)
            for d in range(2):
                pe.wait_ge(ended, d + 1)
                last = top[:, LE - 1:LE] if d == 0 else whole_max[:, 0:1]
                pe.transpose(p_e[0:1, d * P:(d + 1) * P], last, T.ident[:, :]).then_inc(row_made, 1)
                pe.wait_ge(carried, d + 1)
                pe.transpose(p_s[:, d:d + 1], into[0:1, d, :], T.ident[0:1, 0:1]).then_inc(started, 1)
            for b, (j, n) in enumerate(quads):
                pe.wait_ge(exped, b + 1)
                if b >= 3:
                    pe.wait_ge(placed, b - 2)
                else:
                    pe.wait_ge(by_act, NQ)
                for k in range(n):
                    tr = pe.transpose(p_l[b % 3][:, k, :], a_t[:, (j + k) * P:(j + k + 1) * P], T.ident[:, :])
                tr.then_inc(back, 1)

        @block.scalar
        def _(act):
            for b, (j, n) in enumerate(quads):
                act.wait_ge(turned, b + 1)
                act.activation(a_t[:, j * P:(j + n) * P], p_l[b % 3][:, 0:n, :].rearrange("p k e -> p (k e)"), ACT.Copy).then_inc(by_act, 1)
            act.wait_ge(shifted, 1)
            for b, (j, n) in enumerate(quads):
                act.activation(a_t[:, j * P:(j + n) * P], a_t[:, j * P:(j + n) * P], ACT.Exp).then_inc(exped, 1)

        @block.vector
        def _(dve):
            then = Chain(dve, chain)
            dve.tensor_copy(lanes, T.att[:, :, :].rearrange("p (l j) h -> p j l h", j=LV)).then_inc(ordered, 1)
            dve.wait_ge(by_act, NQ)

            def forwards(initial):
                return dve.tensor_tensor_scan(top[:, :], T.flag[:, 0:LE], a_t[:, :], initial, ALU.add, ALU.max)

            def backwards(initial):
                return dve.tensor_tensor_scan(whole_max[:, ::-1], T.flag[:, 1:LE + 1][:, ::-1], top[:, ::-1], initial, ALU.add, ALU.max)

            for d, scan in enumerate((forwards, backwards)):
                scan(-BIG).then_inc(ended, 1)
                dve.wait_ge(row_made, d + 1)
                then(dve.tensor_copy(ends[:, d, :], p_e[0:1, d * P:(d + 1) * P]))
                for h in range(HEADS):
                    def along(row):
                        v = row.rearrange("o (l h) -> o l h", h=HEADS)[:, :, h]
                        return v[:, ::-1] if d else v
                    ins = dve.tensor_tensor_scan(along(ends[:, d, :]), along(T.whole[:, d, :]), along(ends[:, d, :]), -BIG, ALU.add, ALU.max)
                    then(ins)
                then(dve.memset(into[:, d, :], -BIG))
                if d == 0:
                    dve.tensor_copy(into[:, 0, HEADS:P], ends[:, 0, 0:P - HEADS]).then_inc(carried, 1)
                else:
                    dve.tensor_copy(into[:, 1, 0:P - HEADS], ends[:, 1, HEADS:P]).then_inc(carried, 1)
                dve.wait_ge(started, d + 1)
                then(dve.tensor_copy(start[:, d:d + 1], p_s[:, d:d + 1]))
                then(scan(start[:, d:d + 1]))
            dve.tensor_tensor(a_t[:, :], a_t[:, :], whole_max, ALU.subtract).then_inc(shifted, 1)
            for b, (j, n) in enumerate(quads):
                dve.wait_ge(back, b + 1)
                if b == 0:
                    dve.wait_ge(shifted, 1)
                dve.tensor_copy(T.att[:, :, :].rearrange("p (l j) h -> p j l h", j=LV)[:, j:j + n],
                                p_l[b % 3][:, 0:n, :].rearrange("p k (l h) -> p k l h", h=HEADS)).then_inc(placed, 1)


def message_pass(nc, A, T, l):
    with ExitStack() as ctx:
        sb, ps, sem = stack(nc, ctx, f"ms{l}_")
        m = sb("m", [P, 4, G, D])
        oh = sb("oh", [P, 2, G, P])
        msg = sb("msg", [P, 2, G, D])
        narrow = sb("narrow", [P, 2, G, P], BF16)
        parts = sb("parts", [P, 2, G, PARTS, HEADS], BF16)
        rest = sb("rest", [P, 2, G, HEADS])
        agg = AggInPsum(sb, ps, sem, weights=True)
        m_in = [sem(f"m_in{i}") for i in range(4)]
        onehots, narrowed, messages, split, summed = (sem(n) for n in ("onehots", "narrowed", "messages", "split", "summed"))
        high, rests, middle = (sem(n) for n in ("high", "rests", "middle"))
        block = ctx.enter_context(nc.Block())
        m_slots = T.m_table.rearrange("(v p) f -> p v f", p=P)

        @block.sync
        def _(sp):
            def step(g, s, r):
                if past(g, 2):
                    sp.wait_ge(messages, g - 1)
                sp.dma_start(m[:, r, :, :], m_slots[:, bass.ds(g * G, G), :]).then_inc(m_in[r], 16)

            pipeline(sp, step)

        @block.scalar
        def _(act):
            for q in (high, middle, narrowed):
                act.sem_inc(q, 2)

            def step(g, s, r):
                act.wait_ge(summed, g + 1)
                act.activation(parts[:, s, :, 0, :], T.att[:, bass.ds(g * G, G), :], ACT.Copy).then_inc(high, 1)
                act.wait_ge(rests, g + 3)
                act.activation(parts[:, s, :, 1, :], rest[:, s, :, :], ACT.Copy).then_inc(middle, 1)
                act.wait_ge(onehots, g + 3)
                act.activation(narrow[:, s, :, :], oh[:, s, :, :], ACT.Copy).then_inc(narrowed, 1)

            pipeline(act, step)

        @block.tensor
        def _(pe):
            pe.sem_inc(summed, 2)
            agg.sweep(pe, True)

            def step(g, s, r):
                tiles = load_tiles(nc, pe, T, g)
                pe.wait_ge(onehots, g + 3)
                pe.wait_ge(messages, g + 3)
                for k in range(G):
                    agg.add(pe, tiles[k], oh[:, s, k, :], msg[:, s, k, :])
                pe.wait_ge(narrowed, g + 3)
                pe.wait_ge(split, g + 3)
                for k in range(G):
                    mm = agg.add_weights(pe, tiles[k], narrow[:, s, k, :], parts[:, s, k, :, :].rearrange("p c h -> p (c h)"))
                mm.then_inc(summed, 1)

            pipeline(pe, step)
            agg.sweep(pe, False)

        @block.vector
        def _(dve):
            dve.sem_inc(onehots, 2)
            for q in (messages, rests, split):
                dve.sem_inc(q, 2)
            agg.clear(dve)

            def step(g, s, r):
                dve.wait_ge(summed, g + 1)
                dve.tensor_tensor(oh[:, s, :, :], T.iota[:, :].unsqueeze(1).to_broadcast([P, G, P]),
                                  T.rel[:, bass.ds(g * G, G)].unsqueeze(2).to_broadcast([P, G, P]),
                                  ALU.is_equal).then_inc(onehots, 1)
                dve.wait_ge(high, g + 3)
                dve.tensor_tensor(rest[:, s, :, :], T.att[:, bass.ds(g * G, G), :], parts[:, s, :, 0, :], ALU.subtract).then_inc(rests, 1)
                dve.wait_ge(m_in[r], turns(g, r, 16))
                dve.tensor_tensor(msg[:, s, :, :].rearrange("p k (h o) -> p k h o", o=HS),
                                  m[:, r, :, :].rearrange("p k (h o) -> p k h o", o=HS),
                                  T.att[:, bass.ds(g * G, G), :].unsqueeze(3).to_broadcast([P, G, HEADS, HS]), ALU.mult).then_inc(messages, 1)
                dve.wait_ge(middle, g + 3)
                dve.tensor_tensor(parts[:, s, :, 2, :], rest[:, s, :, :], parts[:, s, :, 1, :], ALU.subtract).then_inc(split, 1)

            pipeline(dve, step)
            agg.store(dve, T)


def node_update(nc, A, T, l):
    with ExitStack() as ctx:
        sb, ps, sem = stack(nc, ctx)
        nm = f"up{l}_"
        wa = sb(nm + "wa", [D, TYPES, D])
        par = sb(nm + "par", [P, 2, D])
        skip = sb(nm + "skip", [P, TYPES])
        den = sb(nm + "den", [P, TILES, HEADS])
        al = sb(nm + "al", [P, 2, TILES])
        Z, O = sb(nm + "Z", [P, TILES, D]), sb(nm + "O", [P, TILES, D])
        st = sb(nm + "st", [P, 4, TILES])
        z_t, xm = sb(nm + "z_t", [P, 512]), sb(nm + "xm", [P, TYPES, 512])
        p_t, p_o = ps(nm + "p_t", [P, 512]), [ps(f"{nm}p_o{i}", [P, 4, D]) for i in range(2)]
        params, chain, z_ready, turned, kept, masked, made, silued, al_sum, al_ready = (
            sem(nm + n) for n in ("params", "chain", "z_ready", "turned", "kept", "masked", "made", "silued", "al_sum", "al_ready"))
        centred, squared, var_ready, root = (sem(nm + n) for n in ("centred", "squared", "var_ready", "root"))
        block = ctx.enter_context(nc.Block())
        NB = len(BLOCKS)

        @block.sync
        def _(sp):
            sp.dma_start(skip[:, :], A["L2_gnn_skip"][l].partition_broadcast(P)).then_inc(params, 16)
            sp.dma_start(wa[:, :, :], A["L2_gnn_Wa"][l].rearrange("t i o -> i t o")).then_inc(params, 16)
            sp.dma_start(par[:, 0, :], A["L2_gnn_ln_g"][l].partition_broadcast(P)).then_inc(params, 16)
            sp.dma_start(par[:, 1, :], A["L2_gnn_ln_b"][l].partition_broadcast(P)).then_inc(params, 16)

        @block.tensor
        def _(pe):
            pe.wait_ge(z_ready, 1)
            pe.wait_ge(params, 64)
            for b, (t0, n) in enumerate(BLOCKS):
                if b >= 1:
                    pe.wait_ge(kept, b)
                for k in range(n):
                    tr = pe.transpose(p_t[:, k * P:(k + 1) * P], Z[:, t0 + k, :], T.ident[:, :])
                tr.then_inc(turned, 1)
                pe.wait_ge(masked, b + 1)
                if b >= 2:
                    pe.wait_ge(silued, b - 1)
                for k in range(n):
                    for t in range(TYPES):
                        mm = pe.matmul(p_o[b % 2][:, k, :], xm[:, t, k * P:(k + 1) * P], wa[:, t, :], start=(t == 0), stop=(t == TYPES - 1))
                mm.then_inc(made, 1)

        @block.scalar
        def _(act):
            for b, (t0, n) in enumerate(BLOCKS):
                act.wait_ge(turned, b + 1)
                if b >= 1:
                    act.wait_ge(masked, b)
                act.activation(z_t[:, 0:n * P], p_t[:, 0:n * P], ACT.Copy).then_inc(kept, 1)
                act.wait_ge(made, b + 1)
                act.activation(O[:, t0:t0 + n, :], p_o[b % 2][:, 0:n, :], ACT.Silu).then_inc(silued, 1)
            act.wait_ge(al_sum, 1)
            act.activation(al[:, 1, :], al[:, 0, :], ACT.Sigmoid).then_inc(al_ready, 1)
            act.wait_ge(centred, 1)
            act.activation(Z[:, :, :], O[:, :, :], ACT.Square).then_inc(squared, 1)
            act.wait_ge(var_ready, 1)
            act.activation(st[:, 2, :], st[:, 1, :], ACT.Sqrt).then_inc(root, 1)

        @block.vector
        def _(dve):
            then = Chain(dve, chain)

            def wide(a):
                return a.unsqueeze(2).to_broadcast([P, TILES, D])

            then(dve.tensor_scalar(den[:, :, :], T.agg[:, :, D:AW], 1e-16, None, ALU.add))
            then(dve.reciprocal(den[:, :, :], den[:, :, :]))
            for h in range(HEADS):
                of = slice(h * HS, (h + 1) * HS)
                ins = dve.tensor_tensor(Z[:, :, of], T.agg[:, :, of], den[:, :, h].unsqueeze(2).to_broadcast([P, TILES, HS]), ALU.mult)
            ins.then_inc(z_ready, 1)
            for b, (t0, n) in enumerate(BLOCKS):
                dve.wait_ge(kept, b + 1)
                if b >= 1:
                    dve.wait_ge(made, b)
                for t in range(TYPES):
                    ins = dve.scalar_tensor_tensor(out=xm[:, t, 0:n * P], in0=T.type_row[:, t0 * P:(t0 + n) * P], scalar=float(t),
                                                   in1=z_t[:, 0:n * P], op0=ALU.is_equal, op1=ALU.mult)
                ins.then_inc(masked, 1)
            dve.wait_ge(params, 64)
            then(dve.tensor_scalar(al[:, 0, :], T.type_of[:, :], 0.0, skip[:, 0:1], ALU.is_equal, ALU.mult))
            for t in range(1, TYPES):
                then(dve.tensor_scalar(al[:, 1, :], T.type_of[:, :], float(t), skip[:, t:t + 1], ALU.is_equal, ALU.mult))
                then(dve.tensor_tensor(al[:, 0, :], al[:, 0, :], al[:, 1, :], ALU.add))
            dve.sem_inc(al_sum, 1)
            dve.wait_ge(silued, NB)
            dve.wait_ge(al_ready, 1)
            then(dve.tensor_tensor(O[:, :, :], O[:, :, :], T.H[:, :, :], ALU.subtract))
            then(dve.tensor_tensor(O[:, :, :], O[:, :, :], wide(al[:, 1, :]), ALU.mult))
            then(dve.tensor_tensor(O[:, :, :], O[:, :, :], T.H[:, :, :], ALU.add))
            then(dve.tensor_reduce(st[:, 0, :], O[:, :, :], AX.X, ALU.add))
            then(dve.tensor_scalar(st[:, 0, :], st[:, 0, :], 1.0 / D, None, ALU.mult))
            dve.tensor_tensor(O[:, :, :], O[:, :, :], wide(st[:, 0, :]), ALU.subtract).then_inc(centred, 1)
            dve.wait_ge(squared, 1)
            then(dve.tensor_reduce(st[:, 1, :], Z[:, :, :], AX.X, ALU.add))
            dve.tensor_scalar(st[:, 1, :], st[:, 1, :], 1.0 / D, EPS, ALU.mult, ALU.add).then_inc(var_ready, 1)
            dve.wait_ge(root, 1)
            then(dve.reciprocal(st[:, 3, :], st[:, 2, :]))
            then(dve.tensor_tensor(O[:, :, :], O[:, :, :], wide(st[:, 3, :]), ALU.mult))
            then(dve.tensor_tensor(O[:, :, :], O[:, :, :], par[:, 0, :].unsqueeze(1).to_broadcast([P, TILES, D]), ALU.mult))
            then(dve.tensor_tensor(T.H[:, :, :], O[:, :, :], par[:, 1, :].unsqueeze(1).to_broadcast([P, TILES, D]), ALU.add))


def feed_out(nc, A, T):
    with ExitStack() as ctx:
        sb, ps, sem = stack(nc, ctx, "feed_out_")
        w, b0, one = sb("wff", [D, D]), sb("bff", [1, D]), sb("one_ff", [1, P])
        h_t = sb("ff_h_t", [P, 2, 512])
        p_t = [ps(f"ff_p_t{i}", [P, 512]) for i in range(2)]
        p_o = [ps(f"ff_p_o{i}", [P, 4, D]) for i in range(2)]
        params, set_up, turned, kept, made, taken = (sem("ff_" + n) for n in ("params", "set_up", "turned", "kept", "made", "taken"))
        block = ctx.enter_context(nc.Block())

        @block.sync
        def _(sp):
            sp.dma_start(w[:, :], A["L2_gnn_Wff"]).then_inc(params, 16)
            sp.dma_start(b0[:, :], A["L2_gnn_bff"].rearrange("(o f) -> o f", o=1)).then_inc(params, 16)

        @block.tensor
        def _(pe):
            pe.wait_ge(set_up, 1)
            pe.wait_ge(params, 32)
            for b, (t0, n) in enumerate(BLOCKS):
                if b >= 2:
                    pe.wait_ge(kept, b - 1)
                for k in range(n):
                    tr = pe.transpose(p_t[b % 2][:, k * P:(k + 1) * P], T.H[:, t0 + k, :], T.ident[:, :])
                tr.then_inc(turned, 1)
                pe.wait_ge(kept, b + 1)
                if b >= 2:
                    pe.wait_ge(taken, b - 1)
                for k in range(n):
                    pe.matmul(p_o[b % 2][:, k, :], h_t[:, b % 2, k * P:(k + 1) * P], w[:, :], start=True, stop=False)
                    mm = pe.matmul(p_o[b % 2][:, k, :], one[:, :], b0[:, :], start=False, stop=True)
                mm.then_inc(made, 1)

        @block.scalar
        def _(act):
            for b, (t0, n) in enumerate(BLOCKS):
                act.wait_ge(turned, b + 1)
                if b >= 2:
                    act.wait_ge(made, b - 1)
                act.activation(h_t[:, b % 2, 0:n * P], p_t[b % 2][:, 0:n * P], ACT.Copy).then_inc(kept, 1)

        @block.vector
        def _(dve):
            dve.memset(one[:, :], 1.0).then_inc(set_up, 1)
            for b, (t0, n) in enumerate(BLOCKS):
                dve.wait_ge(made, b + 1)
                dve.tensor_tensor(T.X[:, t0:t0 + n, :], T.X[:, t0:t0 + n, :], p_o[b % 2][:, 0:n, :], ALU.add).then_inc(taken, 1)


def gate_tables(nc, A, T):
    with ExitStack() as ctx:
        sb, ps, sem = stack(nc, ctx, "gate_tables_")
        w = sb("gt_w", [D, ROW3])
        row_b, one = sb("gt_row_b", [1, ROW3]), sb("gt_one", [1, P])
        w_dst, w_dst_wide, b_att = sb("gt_w_dst", [D, 1]), sb("gt_w_dst_wide", [D, P]), sb("gt_b_att", [P, 1])
        rows = sb("gt_rows", [P, TILES, ROW3])
        p_t = [ps(f"gt_p_t{i}", [P, 512]) for i in range(2)]
        p_o = [[ps(f"gt_p_o{i}{j}", [P, 2, 256]) for j in range(2)] for i in range(2)]
        p_d = [ps(f"gt_p_d{i}", [P, 512]) for i in range(2)]
        params, set_up, turned, kept, made, taken, dsts, dst_kept, stored, widened = (
            sem("gt_" + n) for n in ("params", "set_up", "turned", "kept", "made", "taken", "dsts", "dst_kept", "stored", "widened"))
        block = ctx.enter_context(nc.Block())
        W_att = A["L3_gnn_W_att"]

        @block.sync
        def _(sp):
            sp.wait_ge(set_up, 3)
            sp.dma_start(w[:, 0:D], A["L3_gnn_W_msg"]).then_inc(params, 16)
            sp.dma_start(w[:, D:D + 1], W_att[0:D, :]).then_inc(params, 16)
            sp.dma_start(w_dst[:, :], W_att[D:2 * D, :]).then_inc(params, 16)
            sp.dma_start(row_b[:, 0:D], A["L3_gnn_b_msg"].rearrange("(o f) -> o f", o=1)).then_inc(params, 16)
            sp.dma_start(b_att[:, :], A["L3_gnn_b_att"].partition_broadcast(P)).then_inc(params, 16)
            sp.wait_ge(taken, 2 * len(BLOCKS) - 1)
            sp.dma_start(T.gate_table.rearrange("(t p) f -> p t f", p=P), rows[:, :, :]).then_inc(stored, 16)
            sp.wait_ge(stored, 16)

        @block.tensor
        def _(pe):
            pe.wait_ge(widened, 1)
            done = 0
            for b, (t0, n) in enumerate(BLOCKS):
                if b >= 2:
                    pe.wait_ge(kept, b - 1)
                for k in range(n):
                    tr = pe.transpose(p_t[b % 2][:, k * P:(k + 1) * P], T.H[:, t0 + k, :], T.ident[:, :])
                tr.then_inc(turned, 1)
                pe.wait_ge(kept, b + 1)
                if b >= 2:
                    pe.wait_ge(taken, 2 * (b - 1))
                    pe.wait_ge(dst_kept, b - 1)
                for k in range(n):
                    at = p_o[b % 2][k // 2][:, k % 2, 0:ROW3]
                    pe.matmul(at, T.H_t[:, (t0 + k) * P:(t0 + k + 1) * P], w[:, :], start=True, stop=False)
                    mm = pe.matmul(at, one[:, :], row_b[:, :], start=False, stop=True)
                mm.then_inc(made, 1)
                pe.matmul(p_d[b % 2][:, 0:n * P], w_dst_wide[:, :], T.H_t[:, t0 * P:(t0 + n) * P], start=True, stop=True).then_inc(dsts, 1)

        @block.scalar
        def _(act):
            act.wait_ge(params, 80)
            for b, (t0, n) in enumerate(BLOCKS):
                act.wait_ge(turned, b + 1)
                act.activation(T.H_t[:, t0 * P:(t0 + n) * P], p_t[b % 2][:, 0:n * P], ACT.Copy).then_inc(kept, 1)
                act.wait_ge(dsts, b + 1)
                act.activation(T.dst_row[:, t0 * P:(t0 + n) * P], p_d[b % 2][:, 0:n * P], ACT.Identity, bias=b_att[:, 0:1]).then_inc(dst_kept, 1)

        @block.vector
        def _(dve):
            dve.memset(w[:, :], 0.0).then_inc(set_up, 1)
            dve.memset(row_b[:, :], 0.0).then_inc(set_up, 1)
            dve.memset(one[:, :], 1.0).then_inc(set_up, 1)
            dve.wait_ge(params, 80)
            dve.tensor_copy(w_dst_wide[:, :], w_dst[:, 0:1].to_broadcast([D, P])).then_inc(widened, 1)
            for b, (t0, n) in enumerate(BLOCKS):
                dve.wait_ge(made, b + 1)
                for j in range((n + 1) // 2):
                    m = min(2, n - 2 * j)
                    dve.tensor_copy(rows[:, t0 + 2 * j:t0 + 2 * j + m, :], p_o[b % 2][j][:, 0:m, 0:ROW3]).then_inc(taken, 1)


def gate_pass(nc, A, T):
    with ExitStack() as ctx:
        sb, ps, sem = stack(nc, ctx, "gate_pass_")
        idx = sb("idx", [P, 4, G], I32)
        hx = sb("hx", [P, 4, G, ROW3])
        oh = sb("oh", [P, 4, G, P])
        dst_rows = sb("dst_rows", [P, 2, G, P])
        pick = sb("pick", [P, 2, G, P])
        dst_term = sb("dst_term", [P, 2, G])
        z, gate = sb("z", [P, 2, G]), sb("gate", [P, 2, G])
        msg = sb("msg", [P, 2, G, D])
        agg = AggInPsum(sb, ps, sem)
        idx_ready, onehots, rows_ready, messages, summed, gates, terms, dst_terms = (
            sem(n) for n in ("idx_ready", "onehots", "rows_ready", "messages", "summed", "gates", "terms", "dst_terms"))
        picked, opened = sem("picked"), sem("opened")
        block = ctx.enter_context(nc.Block())

        @block.gpsimd
        def _(pool):
            bound = pool.to_reg(NP - 1)

            def step(g, s, r):
                pool.wait_ge(idx_ready, g + 3)
                if past(g, 2):
                    pool.wait_ge(messages, g - 1)
                pool.sem_inc(opened, 1)
                for k in range(G):
                    pool.indirect_dma_start(out=hx[:, r, k, :], out_offset=None, in_=T.gate_table,
                                            in_offset=bass.IndirectOffsetOnAxis(ap=idx[:, r, k:k + 1].bitcast(U32), axis=0),
                                            bounds_check=bound).then_inc(T.gathered[r], 16)

            pipeline(pool, step)

        @block.scalar
        def _(act):
            act.sem_inc(idx_ready, 2)
            act.sem_inc(rows_ready, 2)
            act.sem_inc(gates, 2)

            def step(g, s, r):
                if within(g):
                    if past(g, 2):
                        act.wait_ge(messages, g - 1)
                    act.activation(idx[:, r, :], T.src[:, bass.ds(g * G, G)], ACT.Copy).then_inc(idx_ready, 1)
                    act.wait_ge(dst_terms, g + 1)
                    for k, t in enumerate(load_tiles(nc, act, T, g)):
                        ins = act.activation(dst_rows[:, s, k, :], T.dst_row[:, bass.ds(t * P, P)], ACT.Copy)
                    ins.then_inc(rows_ready, 1)
                if past(g, 1):
                    h, q = g - 1, 1 - s
                    act.wait_ge(terms, h + 3)
                    act.activation(gate[:, q, :], z[:, q, :], ACT.Sigmoid).then_inc(gates, 1)

            pipeline(act, step, drain=(GROUPS,))

        @block.tensor
        def _(pe):
            pe.sem_inc(summed, 2)
            agg.sweep(pe, True)

            def step(g, s, r):
                tiles = load_tiles(nc, pe, T, g)
                pe.wait_ge(messages, g + 3)
                pe.wait_ge(onehots, g + 3)
                for k in range(G):
                    mm = agg.add(pe, tiles[k], oh[:, r, k, :], msg[:, s, k, :])
                mm.then_inc(summed, 1)

            pipeline(pe, step)
            agg.sweep(pe, False)

        @block.vector
        def _(dve):
            for q in (onehots, messages, terms, dst_terms):
                dve.sem_inc(q, 2)
            agg.clear(dve)

            def step(g, s, r):
                h, q = g - 1, 1 - s
                if past(g, 1):
                    wait_gathers(dve, T, 4, h, (r - 1) % 4)
                    dve.wait_ge(dst_terms, h + 3)
                    dve.wait_ge(gates, h + 1)
                    dve.tensor_tensor(z[:, q, :], hx[:, (r - 1) % 4, :, D], dst_term[:, q, :], ALU.add).then_inc(terms, 1)
                if within(g):
                    if past(g, 2):
                        dve.wait_ge(summed, g - 1)
                    dve.tensor_tensor(oh[:, r, :, :], T.iota[:, :].unsqueeze(1).to_broadcast([P, G, P]),
                                      T.rel[:, bass.ds(g * G, G)].unsqueeze(2).to_broadcast([P, G, P]),
                                      ALU.is_equal).then_inc(onehots, 1)
                    dve.wait_ge(onehots, g + 3)
                    dve.wait_ge(rows_ready, g + 3)
                    dve.wait_ge(dst_terms, g + 1)
                    dve.tensor_tensor(pick[:, s, :, :], oh[:, r, :, :], dst_rows[:, s, :, :], ALU.mult).then_inc(picked, 1)
                    dve.wait_ge(picked, g + 1)
                    dve.wait_ge(terms, g + 1)
                    dve.tensor_reduce(dst_term[:, s, :], pick[:, s, :, :], AX.X, ALU.add).then_inc(dst_terms, 1)
                if past(g, 1):
                    dve.wait_ge(gates, h + 3)
                    dve.wait_ge(summed, h + 1)
                    dve.tensor_tensor(msg[:, q, :, :], hx[:, (r - 1) % 4, :, 0:D], gate[:, q, :].unsqueeze(2).to_broadcast([P, G, D]), ALU.mult).then_inc(messages, 1)

            pipeline(dve, step, drain=(GROUPS,))
            agg.store(dve, T)


def node_gru(nc, A, T, out):
    with ExitStack() as ctx:
        sb, ps, sem = stack(nc, ctx, "node_gru_")
        raw = sb("gru_raw", [P, 2, 3, D])
        w_t = sb("gru_w_t", [P, 2, 3, D])
        bias = sb("gru_bias", [P, 2, 3])
        both = sb("gru_both", [P, 2])
        agg_t = sb("gru_agg_t", [P, 2, 512])
        r, z, nn, hn = (sb("gru_" + n, [P, 2, 512]) for n in ("r", "z", "nn", "hn"))
        Y = sb("gru_Y", [P, NP])
        p_t = [ps(f"gru_p_t{i}", [P, 512]) for i in range(2)]
        p_r, p_z, p_i, p_h = (ps("gru_p_" + n, [P, 512]) for n in "rzih")
        p_b = [ps(f"gru_p_b{i}", [P, 4, D]) for i in range(2)]
        params, chain, w_turned, w_kept, turned, kept, gated, sig, steps, tanhed, biased = (
            sem("gru_" + n) for n in ("params", "chain", "w_turned", "w_kept", "turned", "kept", "gated", "sig", "steps", "tanhed", "biased"))
        back, taken, n_read, i_summed, done = (sem("gru_" + n) for n in ("back", "taken", "n_read", "i_summed", "done"))
        bn = Batchnorm(sb, sem, "bn3_", Y)
        block = ctx.enter_context(nc.Block())
        NB = len(BLOCKS)

        @block.sync
        def _(sp):
            for k, name in enumerate(("ih", "hh")):
                sp.dma_start(raw[:, k, :, :], A["L3_gnn_W_" + name].rearrange("(g p) f -> p g f", p=P)).then_inc(params, 16)
                for g in range(3):
                    sp.dma_start(bias[:, k, g:g + 1], A["L3_gnn_b_" + name][g * P:(g + 1) * P].rearrange("(p o) -> p o", o=1)).then_inc(params, 16)
            bn.load(sp, A["L3_gnn_gamma"], A["L3_gnn_beta"])
            full = N // P
            sp.wait_ge(taken, NB)
            sp.dma_start(out[0:full * P, :].rearrange("(t p) f -> p t f", p=P), T.X[:, 0:full, :]).then_inc(done, 16)
            sp.dma_start(out[full * P:N, :], T.X[0:N - full * P, full, :]).then_inc(done, 16)
            sp.wait_ge(done, 32)

        @block.tensor
        def _(pe):
            pe.wait_ge(params, 128)
            for k in range(2):
                for g in range(3):
                    tr = pe.transpose(p_t[k][:, g * P:(g + 1) * P], raw[:, k, g, :], T.ident[:, :])
                tr.then_inc(w_turned, 1)
            pe.wait_ge(w_kept, 2)
            for b, (t0, n) in enumerate(BLOCKS):
                if b >= 2:
                    pe.wait_ge(kept, b - 1)
                for k in range(n):
                    tr = pe.transpose(p_t[b % 2][:, k * P:(k + 1) * P], T.agg[:, t0 + k, 0:D], T.ident[:, :])
                tr.then_inc(turned, 1)
                pe.wait_ge(kept, b + 1)
                w = n * P
                a, h = agg_t[:, b % 2, 0:w], T.H_t[:, t0 * P:t0 * P + w]
                if b >= 1:
                    pe.wait_ge(sig, 2 * b)
                for g, bank in enumerate((p_r, p_z)):
                    pe.matmul(bank[:, 0:w], w_t[:, 0, g, :], a, start=True, stop=False)
                    pe.matmul(bank[:, 0:w], w_t[:, 1, g, :], h, start=False, stop=True).then_inc(gated, 1)
                if b >= 1:
                    pe.wait_ge(n_read, b)
                    pe.wait_ge(i_summed, b)
                pe.matmul(p_h[:, 0:w], w_t[:, 1, 2, :], h, start=True, stop=True).then_inc(gated, 1)
                pe.matmul(p_i[:, 0:w], w_t[:, 0, 2, :], a, start=True, stop=True).then_inc(gated, 1)
            pe.wait_ge(bn.done, 1)
            for b, (t0, n) in enumerate(BLOCKS):
                if b >= 2:
                    pe.wait_ge(taken, b - 1)
                for k in range(n):
                    tr = pe.transpose(p_b[b % 2][:, k, :], Y[:, (t0 + k) * P:(t0 + k + 1) * P], T.ident[:, :])
                tr.then_inc(back, 1)

        @block.scalar
        def _(act):
            act.wait_ge(params, 128)
            for k in range(2):
                act.wait_ge(w_turned, k + 1)
                act.activation(w_t[:, k, :, :], p_t[k][:, 0:3 * P].rearrange("p (g o) -> p g o", g=3), ACT.Copy).then_inc(w_kept, 1)
            act.wait_ge(biased, 1)
            for b, (t0, n) in enumerate(BLOCKS):
                w, s = n * P, b % 2
                act.wait_ge(turned, b + 1)
                if b >= 2:
                    act.wait_ge(gated, 4 * (b - 1))
                act.activation(agg_t[:, s, 0:w], p_t[s][:, 0:w], ACT.Copy).then_inc(kept, 1)
                if b >= 2:
                    act.wait_ge(steps, 4 * (b - 1))
                act.wait_ge(gated, 4 * b + 1)
                act.activation(r[:, s, 0:w], p_r[:, 0:w], ACT.Sigmoid, bias=both[:, 0:1]).then_inc(sig, 1)
                act.wait_ge(gated, 4 * b + 2)
                act.activation(z[:, s, 0:w], p_z[:, 0:w], ACT.Sigmoid, bias=both[:, 1:2]).then_inc(sig, 1)
                act.wait_ge(gated, 4 * b + 3)
                act.activation(hn[:, s, 0:w], p_h[:, 0:w], ACT.Identity, bias=bias[:, 1, 2:3]).then_inc(n_read, 1)
                act.wait_ge(i_summed, b + 1)
                act.activation(nn[:, s, 0:w], nn[:, s, 0:w], ACT.Tanh, bias=bias[:, 0, 2:3]).then_inc(tanhed, 1)
            bn.on_scalar(act, ACT.Identity)

        @block.vector
        def _(dve):
            then = Chain(dve, chain)
            dve.wait_ge(params, 128)
            dve.tensor_tensor(both[:, :], bias[:, 0, 0:2], bias[:, 1, 0:2], ALU.add).then_inc(biased, 1)
            for b, (t0, n) in enumerate(BLOCKS):
                w, s = n * P, b % 2
                h, y = T.H_t[:, t0 * P:t0 * P + w], Y[:, t0 * P:t0 * P + w]
                dve.wait_ge(n_read, b + 1)
                dve.tensor_tensor(nn[:, s, 0:w], r[:, s, 0:w], hn[:, s, 0:w], ALU.mult).then_inc(steps, 1)
                dve.wait_ge(steps, 4 * b + 1)
                dve.wait_ge(gated, 4 * b + 4)
                dve.tensor_tensor(nn[:, s, 0:w], nn[:, s, 0:w], p_i[:, 0:w], ALU.add).then_inc(i_summed, 1)
                dve.wait_ge(tanhed, b + 1)
                dve.tensor_tensor(y, h, nn[:, s, 0:w], ALU.subtract).then_inc(steps, 1)
                dve.wait_ge(steps, 4 * b + 2)
                dve.tensor_tensor(y, y, z[:, s, 0:w], ALU.mult).then_inc(steps, 1)
                dve.wait_ge(steps, 4 * b + 3)
                dve.tensor_tensor(y, y, nn[:, s, 0:w], ALU.add).then_inc(steps, 1)
            dve.wait_ge(steps, 4 * NB)
            bn.on_vector(dve, then)
            for b, (t0, n) in enumerate(BLOCKS):
                dve.wait_ge(back, b + 1)
                dve.tensor_tensor(T.X[:, t0:t0 + n, :], T.X[:, t0:t0 + n, :], p_b[b % 2][:, 0:n, :], ALU.add).then_inc(taken, 1)


def clear_semaphores(nc):
    free = sorted(nc.free_semaphores)
    assert free == list(range(free[0], free[-1] + 1))
    with nc.Block() as block:
        @block.gpsimd
        def _(pool):
            pool.sem_clear(range(free[0], free[-1] + 1))


def program(nc, A, out):
    T = Tensors()
    with ExitStack() as ctx:
        sb, ps, sem = stack(nc, ctx)
        T.chunk_table = nc.dram_tensor("chunk_table", (CT * P, 3 * P), I32).ap()
        T.attr = nc.dram_tensor("attr_padded", ((VISITS - TILES + 1) * P, EF), F32).ap()
        T.h_table = nc.dram_tensor("h_table", (NP, D), F32).ap()
        T.kv_table = nc.dram_tensor("kv_table", (NP * REL, 2 * D), F32).ap()
        T.m_table = nc.dram_tensor("m_table", (VISITS * P, D), F32).ap()
        T.gate_table = nc.dram_tensor("gate_table", (NP, ROW3), F32).ap()
        T.X = sb("X", [P, TILES, D])
        T.H = sb("H", [P, TILES, D])
        T.agg = sb("agg", [P, TILES, AW])
        T.ident = sb("ident", [P, P])
        T.iota = sb("iota", [P, P])
        T.rel = sb("rel", [P, CT * P])
        T.key = sb("key", [P, CT * P])
        T.src = sb("src", [P, CT * P], I32)
        T.srcrel = sb("srcrel", [P, CT * P], I32)
        T.tile_codes = sb("tile_codes", [1, GROUPS], I32)
        T.gathered = [sem(f"gathered{i}") for i in range(4)]
        T.rows_in = sem("visit_rows_in")
        setup(nc, A, T)
        layernorm_relu(nc, T, "ln0", True)
        edge_mlp_pass(nc, A, T)
        node_mlp(nc, A, T)
        layernorm_relu(nc, T, "ln1", True)
        sum_pass(nc, A, T)
        node_gin(nc, A, T)
        clear_semaphores(nc)
        layernorm_relu(nc, T, "ln2", False)
        with ExitStack() as layer2:
            sb, ps, sem = stack(nc, layer2)
            T.type_row = sb("type_row", [P, NP])
            T.type_of = sb("type_of", [P, TILES])
            T.Q = sb("Q", [P, TILES, D])
            T.whole = sb("whole_lane", [1, 2, P])
            T.att = sb("att", [P, SV, HEADS])
            T.flag = sb("flag", [P, LE + 1])
            scan_flags(nc, A, T)
            for l in range(LAYERS):
                typed_qkv(nc, A, T, l)
                score_pass(nc, A, T, l)
                softmax_shift(nc, A, T, l)
                message_pass(nc, A, T, l)
                node_update(nc, A, T, l)
                clear_semaphores(nc)
        feed_out(nc, A, T)
        layernorm_relu(nc, T, "ln3", False)
        T.H_t = sb_outer(nc, ctx, "H_t", [P, NP])
        T.dst_row = sb_outer(nc, ctx, "dst_row", [P, NP])
        gate_tables(nc, A, T)
        gate_pass(nc, A, T)
        node_gru(nc, A, T, out)


def sb_outer(nc, ctx, name, shape):
    return ctx.enter_context(nc.sbuf_tensor(name, shape, F32))




def kernel(**inputs):
    import numpy as _np
    import concourse.bacc as _bacc
    from concourse.bass_utils import run_bass_kernel_spmd as _run

    nc = _bacc.Bacc("TRN2", target_bir_lowering=False, num_devices=1)
    arrays, args = {}, {}
    for name, value in inputs.items():
        a = _np.ascontiguousarray(value)
        arrays[f"in_{name}_dram"] = a
        args[name] = nc.dram_tensor(f"in_{name}_dram", a.shape, mybir.dt.from_np(a.dtype), kind="ExternalInput").ap()
    out = nc.dram_tensor("out_dram", (N, D), F32, kind="ExternalOutput").ap()
    program(nc, args, out)
    r = _run(nc, [arrays], core_ids=[0])
    return r.results[0]["out_dram"]
```

```python
from contextlib import ExitStack

import concourse.bass as bass
from concourse import mybir

P = 128
N = 3125
E = 100000
D = 128
EF = 50
TILES = -(-N // P)
NP = TILES * P
CHUNKS = -(-E // P)
G = 4
GROUPS = -(-(CHUNKS + TILES - 1) // G)
VISITS = GROUPS * G
CT = -(-VISITS // P)
HEADS, HS, REL, TYPES, LAYERS = 8, 16, 8, 8, 2
LANES = P // HEADS
LV = -(-VISITS // LANES)
SV = LV * LANES
LE = LV * P
PAD_DST = 30000
BIG = 1.0e38
EPS = 1e-5
ROW3 = 132
AW = D + HEADS

F32 = mybir.dt.float32
BF16 = mybir.dt.bfloat16
I32 = mybir.dt.int32
U32 = mybir.dt.uint32
ALU = mybir.AluOpType
ACT = mybir.ActivationFunctionType
AX = mybir.AxisListType

TBANKS = -(-TILES // 4)
CODE = (TILES - 1).bit_length()
STEPS = 4 * G - 1
BLOCKS = [(b, min(4, TILES - b)) for b in range(0, TILES, 4)]


class Tensors:
    pass


class Chain:

    def __init__(self, eng, sem):
        self.eng, self.sem, self.n = eng, sem, 0

    def __call__(self, ins):
        self.n += 1
        ins.then_inc(self.sem, 1)
        self.eng.wait_ge(self.sem, self.n)


def stack(nc, ctx, stage=""):
    def sb(name, shape, dt=F32):
        return ctx.enter_context(nc.sbuf_tensor(stage + name, shape, dt))

    def ps(name, shape, dt=F32):
        return ctx.enter_context(nc.psum_tensor(stage + name, shape, dt))

    def sem(name):
        return ctx.enter_context(nc.semaphore(stage + name))

    return sb, ps, sem


def setup(nc, A, T):
    with ExitStack() as ctx:
        sb, ps, sem = stack(nc, ctx, "setup_")
        ctab = sb("ctab", [P, CT, 3, P], I32)
        last = sb("last", [P, CT])
        thr = sb("thr", [P, TILES - 1, CT])
        cmp1 = sb("cmp1", [P, TILES - 1, CT])
        cnt = sb("cnt", [P, TILES - 1])
        tio = sb("tio", [P, TILES - 1])
        ends = sb("ends", [P, TILES - 1])
        vio = sb("vio", [P, CT])
        cmp2 = sb("cmp2", [P, CT, TILES - 1])
        tvp = sb("tvp", [P, CT])
        cvp = sb("cvp", [P, CT])
        cvi = sb("cvi", [P, CT], I32)
        base = sb("base", [P, CT])
        tvrow = sb("tvrow", [1, CT * P])
        moves = sb("moves", [1, VISITS + STEPS])
        codes = sb("codes", [1, GROUPS])
        ones = sb("ones", [P, P])
        vt = sb("vt", [P, CT, 3 * P], I32)
        fld = sb("fld", [P, 4, CT, P])
        vtf = sb("vtf", [P, 2, CT, P])
        pc = ps("pc", [P, 512])
        pt = [ps(f"pt{i}", [P, 4, P]) for i in range(2)]
        loaded, stored, padded = sem("ctab_loaded"), sem("ctab_stored"), sem("ctab_padded")
        copied, x_in, zeroed = T.attr_copied, sem("x_in"), sem("zeroed")
        consts, chain, counted = sem("consts"), sem("setup_chain"), sem("counted")
        ends_ready, cvi_ready, rows_in = sem("ends_ready"), sem("cvi_ready"), T.rows_in
        fields, turned, taken, tile_rows = sem("fields"), sem("turned"), sem("taken"), sem("tile_rows")
        block = ctx.enter_context(nc.Block())
        chunked = T.chunk_table.rearrange("(j p) (k e) -> p j k e", p=P, e=P)
        full = (CT - 1) * P
        more = E // P - full
        tail = E - (full + more) * P

        @block.sync
        def _(sp):
            sp.wait_ge(padded, 3)
            for k, a in enumerate((A["dst"], A["src"], A["edge_type_8"])):
                sp.dma_start(ctab[:, 0:CT - 1, k, :], a[0:full * P].rearrange("(j p e) -> p j e", p=P, e=P)).then_inc(loaded, 16)
                sp.dma_start(ctab[0:more, CT - 1, k, :], a[full * P:(full + more) * P].rearrange("(p e) -> p e", e=P)).then_inc(loaded, 16)
                sp.dma_start(ctab[more:more + 1, CT - 1, k, 0:tail], a[(full + more) * P:E].rearrange("(p e) -> p e", p=1)).then_inc(loaded, 16)
            sp.wait_ge(loaded, 9 * 16)
            for j in range(CT):
                sp.dma_start(chunked[:, j], ctab[:, j]).then_inc(stored, 16)
            full_tiles = N // P
            sp.wait_ge(zeroed, 2)
            sp.dma_start(T.X[:, 0:full_tiles, :], A["x"][0:full_tiles * P, :].rearrange("(t p) f -> p t f", p=P)).then_inc(x_in, 16)
            sp.dma_start(T.X[0:N - full_tiles * P, full_tiles, :], A["x"][full_tiles * P:N, :]).then_inc(x_in, 16)
            sp.wait_ge(x_in, 32)
            sp.wait_ge(stored, 16 * CT)

        @block.scalar
        def _(act):
            act.wait_ge(rows_in, 16 * CT)
            rows = E // 4
            for q in range(4):
                act.dma_start(T.attr[q * rows:(q + 1) * rows, :].rearrange("(a b) f -> a (b f)", b=50),
                              A["edge_attr_50"][q * rows:(q + 1) * rows, :].rearrange("(a b) f -> a (b f)", b=50)).then_inc(copied, 16)
            act.wait_ge(zeroed, 1)
            pad = T.attr.shape[0] - E
            act.dma_start(T.attr[E:E + pad, :].rearrange("(q r) f -> q (r f)", r=16),
                          T.zeros[0:pad // 16, 0:16 * EF]).then_inc(copied, 16)

        @block.gpsimd
        def _(pool):
            pool.memset(ctab[:, CT - 1, 0, :], PAD_DST).then_inc(padded, 1)
            pool.memset(ctab[:, CT - 1, 1, :], 0).then_inc(padded, 1)
            pool.memset(ctab[:, CT - 1, 2, :], 0).then_inc(padded, 1)
            pool.memset(T.ident[:, :], 0.0).then_inc(consts, 1)
            pool.wait_ge(consts, 1)
            pool.affine_select(out=T.ident[:, :], in_=T.ident[:, :], compare_op=ALU.not_equal, fill=1.0, base=0,
                               pattern=[[-1, P]], channel_multiplier=1).then_inc(consts, 1)
            pool.iota(thr[:, :, :], [[P, TILES - 1], [0, CT]], base=P, channel_multiplier=0,
                      allow_small_or_imprecise_dtypes=True).then_inc(consts, 1)
            pool.iota(tio[:, :], [[1, TILES - 1]], base=0, channel_multiplier=0,
                      allow_small_or_imprecise_dtypes=True).then_inc(consts, 1)
            pool.iota(vio[:, :], [[P, CT]], base=0, channel_multiplier=1,
                      allow_small_or_imprecise_dtypes=True).then_inc(consts, 1)
            pool.iota(T.iota[:, :], [[1, P]], base=0, channel_multiplier=0,
                      allow_small_or_imprecise_dtypes=True).then_inc(consts, 1)
            pool.memset(ones[:, :], 1.0).then_inc(consts, 1)
            pool.wait_ge(cvi_ready, 1)
            pool.wait_ge(stored, 16 * CT)
            for j in range(CT):
                pool.indirect_dma_start(out=vt[:, j, :], out_offset=None, in_=T.chunk_table,
                                        in_offset=bass.IndirectOffsetOnAxis(ap=cvi[:, j:j + 1].bitcast(U32), axis=0),
                                        bounds_check=CT * P - 1).then_inc(rows_in, 16)

        @block.tensor
        def _(pe):
            pe.wait_ge(counted, 1)
            pe.wait_ge(consts, 7)
            pe.matmul(pc[:, 0:TILES - 1], ones[:, :], cnt[:, :], start=True, stop=True).then_inc(ends_ready, 1)
            pe.wait_ge(cvi_ready, 1)
            for j in range(CT):
                tr = pe.transpose(pt[j // 4][0:1, j % 4, :], tvp[:, j:j + 1], T.ident[:, :])
            tr.then_inc(tile_rows, 1)
            pe.wait_ge(fields, 1)
            for b in range(CT):
                if b >= 2:
                    pe.wait_ge(taken, b - 1)
                for k in range(4):
                    tr = pe.transpose(pt[b % 2][:, k, :], fld[:, k, b, :], T.ident[:, :])
                tr.then_inc(turned, 1)

        @block.vector
        def _(dve):
            then = Chain(dve, chain)
            dve.memset(T.zeros[:, :], 0.0).then_inc(zeroed, 1)
            dve.memset(T.X[:, TILES - 1, :], 0.0).then_inc(zeroed, 1)
            dve.wait_ge(loaded, 9 * 16)
            dve.wait_ge(consts, 7)
            then(dve.tensor_copy(last[:, :], ctab[:, :, 0, P - 1]))
            then(dve.tensor_tensor(cmp1[:, :, :], last[:, :].unsqueeze(1).to_broadcast([P, TILES - 1, CT]), thr[:, :, :], ALU.is_lt))
            dve.tensor_reduce(cnt[:, :], cmp1[:, :, :], AX.X, ALU.add).then_inc(counted, 1)
            dve.wait_ge(ends_ready, 1)
            then(dve.tensor_tensor(ends[:, :], pc[:, 0:TILES - 1], tio[:, :], ALU.add))
            then(dve.tensor_tensor(cmp2[:, :, :], ends[:, :].unsqueeze(1).to_broadcast([P, CT, TILES - 1]),
                                   vio[:, :].unsqueeze(2).to_broadcast([P, CT, TILES - 1]), ALU.is_lt))
            then(dve.tensor_reduce(tvp[:, :], cmp2[:, :, :], AX.X, ALU.add))
            then(dve.tensor_tensor(cvp[:, :], vio[:, :], tvp[:, :], ALU.subtract))
            dve.tensor_copy(cvi[:, :], cvp[:, :]).then_inc(cvi_ready, 1)
            then(dve.tensor_scalar(base[:, :], tvp[:, :], float(P), None, ALU.mult))
            dve.wait_ge(tile_rows, 1)
            then(dve.tensor_copy(tvrow[:, 0:4 * P], pt[0][0:1, :, :].rearrange("o k p -> o (k p)")))
            then(dve.tensor_copy(tvrow[:, 4 * P:], pt[1][0:1, 0:CT - 4, :].rearrange("o k p -> o (k p)")))
            then(dve.tensor_tensor(moves[:, :], tvrow[:, 1:VISITS + STEPS + 1], tvrow[:, 0:VISITS + STEPS], ALU.subtract))
            then(dve.tensor_copy(codes[:, :], tvrow[0:1, 0:VISITS:G]))
            for k in range(STEPS):
                then(dve.scalar_tensor_tensor(out=codes[:, :], in0=moves[:, k:k + VISITS:G][:, 0:GROUPS], scalar=float(1 << CODE + k),
                                              in1=codes[:, :], op0=ALU.mult, op1=ALU.add))
            then(dve.tensor_copy(T.tile_codes[:, :], codes[:, :]))
            dve.wait_ge(rows_in, 16 * CT)
            rows = vt[:, :, :].rearrange("p j (k e) -> p j k e", e=P)
            then(dve.tensor_copy(vtf[:, 0, :, :], rows[:, :, 0, :]))
            then(dve.tensor_copy(fld[:, 2, :, :], rows[:, :, 1, :]))
            then(dve.tensor_copy(vtf[:, 1, :, :], rows[:, :, 2, :]))
            for j in range(CT):
                then(dve.tensor_scalar(fld[:, 0, j, :], vtf[:, 0, j, :], base[:, j:j + 1], None, ALU.subtract))
            then(dve.scalar_tensor_tensor(out=fld[:, 3, :, :], in0=fld[:, 2, :, :], scalar=float(REL),
                                          in1=vtf[:, 1, :, :], op0=ALU.mult, op1=ALU.add))
            then(dve.tensor_scalar(vtf[:, 1, :, :], fld[:, 0, :, :], 0.0, None, ALU.is_ge))
            then(dve.scalar_tensor_tensor(out=vtf[:, 1, :, :], in0=fld[:, 0, :, :], scalar=float(P),
                                          in1=vtf[:, 1, :, :], op0=ALU.is_lt, op1=ALU.mult))
            dve.scalar_tensor_tensor(out=fld[:, 1, :, :], in0=vtf[:, 0, :, :], scalar=1.0,
                                     in1=vtf[:, 1, :, :], op0=ALU.add, op1=ALU.mult).then_inc(fields, 1)
            for b in range(CT):
                dve.wait_ge(turned, b + 1)
                to = slice(b * P, (b + 1) * P)
                dve.tensor_copy(T.rel[:, to], pt[b % 2][:, 0, :])
                dve.tensor_copy(T.key[:, to], pt[b % 2][:, 1, :])
                dve.tensor_copy(T.src[:, to], pt[b % 2][:, 2, :])
                dve.tensor_copy(T.srcrel[:, to], pt[b % 2][:, 3, :]).then_inc(taken, 1)


def staggered(*stages):
    for b in range(len(BLOCKS) + len(stages) - 1):
        for k, stage in enumerate(stages):
            if 0 <= b - k < len(BLOCKS):
                stage(b - k)


def layernorm_relu(nc, T, name, store):
    with ExitStack() as ctx:
        sb, ps, sem = stack(nc, ctx)
        sq = sb(name + "_sq", [P, TILES, D])
        st = sb(name + "_st", [P, 4, TILES])
        chain, centred, squared = sem(name + "_chain"), sem(name + "_centred"), sem(name + "_squared")
        var_ready, root, h_ready, stored = sem(name + "_var"), sem(name + "_root"), sem(name + "_h"), sem(name + "_stored")
        block = ctx.enter_context(nc.Block())
        halves = ((0, TILES // 2), (TILES // 2, TILES))
        rows = T.h_table.rearrange("(t p) f -> p t f", p=P)

        def wide(k, a, b):
            return st[:, k, a:b].unsqueeze(2).to_broadcast([P, b - a, D])

        @block.vector
        def _(dve):
            then = Chain(dve, chain)
            for a, b in halves:
                then(dve.tensor_reduce(st[:, 0, a:b], T.X[:, a:b, :], AX.X, ALU.add))
                then(dve.tensor_scalar(st[:, 0, a:b], st[:, 0, a:b], 1.0 / D, None, ALU.mult))
                dve.tensor_tensor(T.H[:, a:b, :], T.X[:, a:b, :], wide(0, a, b), ALU.subtract).then_inc(centred, 1)
            for k, (a, b) in enumerate(halves):
                dve.wait_ge(squared, k + 1)
                then(dve.tensor_reduce(st[:, 1, a:b], sq[:, a:b, :], AX.X, ALU.add))
                dve.tensor_scalar(st[:, 1, a:b], st[:, 1, a:b], 1.0 / D, EPS, ALU.mult, ALU.add).then_inc(var_ready, 1)
            for k, (a, b) in enumerate(halves):
                dve.wait_ge(root, k + 1)
                then(dve.reciprocal(st[:, 3, a:b], st[:, 2, a:b]))
                dve.scalar_tensor_tensor(out=T.H[:, a:b, :], in0=T.H[:, a:b, :], scalar=0.0, in1=wide(3, a, b),
                                         op0=ALU.max, op1=ALU.mult).then_inc(h_ready, 1)

        @block.scalar
        def _(act):
            for k, (a, b) in enumerate(halves):
                act.wait_ge(centred, k + 1)
                act.activation(sq[:, a:b, :], T.H[:, a:b, :], ACT.Square).then_inc(squared, 1)
            for k, (a, b) in enumerate(halves):
                act.wait_ge(var_ready, k + 1)
                act.activation(st[:, 2, a:b], st[:, 1, a:b], ACT.Sqrt).then_inc(root, 1)

        @block.sync
        def _(sp):
            if store:
                for k, (a, b) in enumerate(halves):
                    sp.wait_ge(h_ready, k + 1)
                    sp.dma_start(rows[:, a:b, :], T.H[:, a:b, :]).then_inc(stored, 16)
                sp.wait_ge(stored, 32)


def pipeline(eng, step, drain=(), turn=4):
    step(0, 0, 0)
    step(1, 1, 1)
    assert turn % 4 == 0 and (GROUPS - 2) % turn == 0
    with eng.Fori(0, (GROUPS - 2) // turn) as i:
        for k in range(2, turn + 2):
            step(turn * i + k, k % 2, k % 4)
    for g in drain:
        step(g, g % 2, g % 4)


assert GROUPS % 4 == 2


def gathered_before(n, r):
    return n * 16 * G * len(range(r, GROUPS, 4))


def turns(g, r, each):
    return each * (g // 4 + 1) if isinstance(g, int) else (g - r) * (each // 4) + each


def wait_gathers(eng, T, n, g, r):
    eng.wait_ge(T.gathered[r], turns(g, r, 16 * G) + gathered_before(n, r))


def load_code(nc, eng, T, g):
    return nc.s_assert_within(eng.value_load(T.tile_codes[0:1, bass.ds(g, 1)]), 0, (1 << CODE + STEPS) - 1,
                              skip_runtime_bounds_check_because="setup packs a tile and STEPS bits")


def decode_tiles(nc, eng, code, tile, at):
    tiles = []
    for k in range(at, at + G):
        tile = code & ((1 << CODE) - 1) if k == 0 else tile + ((code >> (CODE + k - 1)) & 1)
        tile = nc.s_assert_within(eng.snap(tile), 0, TILES - 1,
                                  skip_runtime_bounds_check_because="it is the number of a tile")
        tiles.append(tile)
    return tiles


def load_tiles(nc, eng, T, g):
    return decode_tiles(nc, eng, load_code(nc, eng, T, g), None, 0)


class TurnTiles:

    def __init__(self, nc, eng, T):
        self.nc, self.eng, self.T = nc, eng, T

    def __call__(self, g, r):
        nth = g if isinstance(g, int) else (r - 2) % 4
        if nth == 0:
            self.code, self.last = load_code(self.nc, self.eng, self.T, g), None
        tiles = decode_tiles(self.nc, self.eng, self.code, self.last, nth * G)
        self.last = tiles[-1]
        return tiles


def past(g, k):
    return not isinstance(g, int) or g >= k


def within(g):
    return not isinstance(g, int) or g < GROUPS


def edge_mlp_pass(nc, A, T):
    with ExitStack() as ctx:
        sb, ps, sem = stack(nc, ctx, "edge_mlp_pass_")
        we1 = sb("we1", [EF, D])
        be1 = sb("be1", [D, 1])
        we2 = sb("we2", [D, D])
        be2 = sb("be2", [1, D])
        one = sb("one", [1, P])
        attr = sb("attr_sb", [P, 2, G, P])
        attr_t = sb("attr_t", [EF, 2, G * P])
        hid = sb("hid", [P, 2, G * P])
        idx = sb("idx", [P, 4, G], I32)
        hx = sb("hx", [P, 4, G, D])
        oh = sb("oh", [P, 2, G, P])
        msg = sb("msg", [P, 2, G, D])
        p_at = [ps(f"p_at{i}", [P, 512]) for i in range(2)]
        p_h = [ps(f"p_h{i}", [P, 512]) for i in range(2)]
        p_w = [ps(f"p_w{i}", [P, G, D]) for i in range(2)]
        p_a = [ps(f"p_a{i}", [P, G, D]) for i in range(2)]
        params, set_up, attr_zero = sem("l0_params"), sem("l0_set_up"), sem("l0_attr_zero")
        attr_in = [sem(f"l0_attr_in{i}") for i in range(2)]
        attr_turned, attr_kept, hidden, acted = sem("l0_attr_turned"), sem("l0_attr_kept"), sem("l0_hidden"), sem("l0_acted")
        weighed, messages, summed = sem("l0_weighed"), sem("l0_messages"), sem("l0_summed")
        idx_ready, onehots, opened = sem("l0_idx_ready"), sem("l0_onehots"), sem("l0_opened")
        added = sem("l0_added")
        block = ctx.enter_context(nc.Block())
        chunks = T.attr.rearrange("(c p) f -> c p f", p=P)

        @block.sync
        def _(sp):
            sp.dma_start(we1[:, :], A["L0_gnn_We1"]).then_inc(params, 16)
            sp.dma_start(be1[:, :], A["L0_gnn_be1"].rearrange("(p o) -> p o", o=1)).then_inc(params, 16)
            sp.dma_start(we2[:, :], A["L0_gnn_We2"]).then_inc(params, 16)
            sp.dma_start(be2[:, :], A["L0_gnn_be2"].rearrange("(o f) -> o f", o=1)).then_inc(params, 16)
            sp.wait_ge(attr_zero, 1)
            sp.wait_ge(T.attr_copied, 5 * 16)

            tiles_of = TurnTiles(nc, sp, T)

            def step(g, s, r):
                sp.wait_ge(attr_turned, g + 1)
                for k, tile in enumerate(tiles_of(g, r)):
                    chunk = nc.s_assert_within(sp.snap(g * G + k - tile), 0, VISITS - TILES,
                                               skip_runtime_bounds_check_because="a visit's number is its chunk plus its tile")
                    sp.dma_start(attr[:, s, k, 0:EF], chunks[bass.ds(chunk, 1)].rearrange("c p f -> (c p) f")).then_inc(attr_in[s], 16)

            pipeline(sp, step)

        @block.gpsimd
        def _(pool):
            bound = pool.to_reg(NP - 1)

            def step(g, s, r):
                pool.wait_ge(idx_ready, g + 3)
                if past(g, 2):
                    pool.wait_ge(messages, g - 1)
                pool.sem_inc(opened, 1)
                for k in range(G):
                    pool.indirect_dma_start(out=hx[:, r, k, :], out_offset=None, in_=T.h_table,
                                            in_offset=bass.IndirectOffsetOnAxis(ap=idx[:, r, k:k + 1].bitcast(U32), axis=0),
                                            bounds_check=bound).then_inc(T.gathered[r], 16)

            pipeline(pool, step)

        @block.scalar
        def _(act):
            act.sem_inc(idx_ready, 2)
            act.sem_inc(attr_kept, 2)
            act.sem_inc(acted, 2)
            act.wait_ge(params, 64)

            def step(g, s, r):
                if past(g, 2):
                    act.wait_ge(messages, g - 1)
                act.activation(idx[:, r, :], T.src[:, bass.ds(g * G, G)], ACT.Copy).then_inc(idx_ready, 1)
                act.wait_ge(attr_turned, g + 3)
                act.wait_ge(hidden, g + 1)
                act.activation(attr_t[:, s, :], p_at[s][0:EF, :], ACT.Copy).then_inc(attr_kept, 1)
                act.wait_ge(hidden, g + 3)
                act.wait_ge(weighed, g + 1)
                act.activation(hid[:, s, :], p_h[s][:, :], ACT.Silu, bias=be1[:, 0:1]).then_inc(acted, 1)

            pipeline(act, step)

        @block.tensor
        def _(pe):
            for q in (attr_turned, hidden, weighed, summed):
                pe.sem_inc(q, 2)
            pe.wait_ge(params, 64)
            pe.wait_ge(set_up, 2)

            def weigh(g, s):
                pe.wait_ge(acted, g + 3)
                pe.wait_ge(messages, g + 1)
                for k in range(G):
                    pe.matmul(p_w[s][:, k, :], hid[:, s, k * P:(k + 1) * P], we2[:, :], start=True, stop=False)
                    mm = pe.matmul(p_w[s][:, k, :], one[:, :], be2[:, :], start=False, stop=True)
                mm.then_inc(weighed, 1)

            def scatter(g, s):
                pe.wait_ge(messages, g + 3)
                pe.wait_ge(onehots, g + 3)
                if past(g, 2):
                    pe.wait_ge(added, (g - 1) * G + 1)
                for k in range(G):
                    mm = pe.matmul(p_a[s][:, k, :], oh[:, s, k, :], msg[:, s, k, :], start=True, stop=True)
                mm.then_inc(summed, 1)

            def step(g, s, r):
                if within(g):
                    if isinstance(g, int):
                        pe.wait_ge(attr_in[s], 16 * G * (g // 2 + 1))
                    else:
                        pe.wait_ge(attr_in[s], (g - s) * (8 * G) + 16 * G)
                    pe.wait_ge(attr_kept, g + 1)
                    for k in range(G):
                        tr = pe.transpose(p_at[s][:, k * P:(k + 1) * P], attr[:, s, k, :], T.ident[:, :])
                    tr.then_inc(attr_turned, 1)
                if past(g, 1):
                    weigh(g - 1, 1 - s)
                if within(g):
                    pe.wait_ge(attr_kept, g + 3)
                    pe.wait_ge(acted, g + 1)
                    pe.matmul(p_h[s][:, :], we1[:, :], attr_t[:, s, :], start=True, stop=True).then_inc(hidden, 1)
                if past(g, 1):
                    scatter(g - 1, 1 - s)

            pipeline(pe, step, drain=(GROUPS,))

        @block.vector
        def _(dve):
            dve.sem_inc(messages, 2)
            dve.sem_inc(onehots, 2)
            dve.sem_inc(added, 1)
            dve.memset(attr[:, :, :, :], 0.0).then_inc(attr_zero, 1)
            dve.memset(one[:, :], 1.0).then_inc(set_up, 1)
            dve.memset(T.agg[:, :, :], 0.0).then_inc(set_up, 1)
            dve.wait_ge(set_up, 2)

            def step(g, s, r):
                if within(g):
                    dve.wait_ge(summed, g + 1)
                    dve.tensor_tensor(oh[:, s, :, :], T.iota[:, :].unsqueeze(1).to_broadcast([P, G, P]),
                                      T.rel[:, bass.ds(g * G, G)].unsqueeze(2).to_broadcast([P, G, P]),
                                      ALU.is_equal).then_inc(onehots, 1)
                if past(g, 1) and within(g - 1):
                    h, q = g - 1, 1 - s
                    wait_gathers(dve, T, 0, h, (r - 1) % 4)
                    dve.wait_ge(weighed, h + 3)
                    dve.wait_ge(summed, h + 1)
                    dve.tensor_tensor(msg[:, q, :, :], hx[:, (r - 1) % 4, :, :], p_w[q][:, :, :], ALU.mult).then_inc(messages, 1)
                if past(g, 2):
                    h = g - 2
                    dve.wait_ge(summed, h + 3)
                    for k, t in enumerate(load_tiles(nc, dve, T, h)):
                        into = T.agg[:, bass.ds(t, 1), 0:D].rearrange("p t f -> p (t f)")
                        dve.wait_ge(added, h * G + k + 1)
                        dve.tensor_tensor(into, into, p_a[s][:, k, :], ALU.add).then_inc(added, 1)

            pipeline(dve, step, drain=(GROUPS, GROUPS + 1))


def node_mlp(nc, A, T):
    with ExitStack() as ctx:
        sb, ps, sem = stack(nc, ctx, "node_mlp_")
        w1, b1, w2, b2 = sb("wn1", [D, D]), sb("bn1", [D, 1]), sb("wn2", [D, D]), sb("bn2", [1, D])
        one = sb("one_n0", [1, P])
        agg_t, hid = sb("agg_t", [P, 2, 512]), sb("hid_n0", [P, 2, 512])
        p_t = [ps(f"p_t{i}", [P, 512]) for i in range(2)]
        p_h = [ps(f"p_h{i}", [P, 512]) for i in range(2)]
        p_o = [ps(f"p_o{i}", [P, 4, D]) for i in range(2)]
        params, set_up, chain = sem("n0_params"), sem("n0_set_up"), sem("n0_chain")
        turned, kept, hidden, acted, made, taken = (sem("n0_" + n) for n in ("turned", "kept", "hidden", "acted", "made", "taken"))
        block = ctx.enter_context(nc.Block())

        @block.sync
        def _(sp):
            sp.dma_start(w1[:, :], A["L0_gnn_Wn1"]).then_inc(params, 16)
            sp.dma_start(b1[:, :], A["L0_gnn_bn1"].rearrange("(p o) -> p o", o=1)).then_inc(params, 16)
            sp.dma_start(w2[:, :], A["L0_gnn_Wn2"]).then_inc(params, 16)
            sp.dma_start(b2[:, :], A["L0_gnn_bn2"].rearrange("(o f) -> o f", o=1)).then_inc(params, 16)

        @block.tensor
        def _(pe):
            def turn(b):
                t0, n = BLOCKS[b]
                if b >= 2:
                    pe.wait_ge(kept, b - 1)
                for k in range(n):
                    tr = pe.transpose(p_t[b % 2][:, k * P:(k + 1) * P], T.agg[:, t0 + k, 0:D], T.ident[:, :])
                tr.then_inc(turned, 1)

            def first(b):
                t0, n = BLOCKS[b]
                if b == 0:
                    pe.wait_ge(params, 64)
                pe.wait_ge(kept, b + 1)
                if b >= 2:
                    pe.wait_ge(acted, b - 1)
                pe.matmul(p_h[b % 2][:, 0:n * P], w1[:, :], agg_t[:, b % 2, 0:n * P], start=True, stop=True).then_inc(hidden, 1)

            def second(b):
                t0, n = BLOCKS[b]
                pe.wait_ge(acted, b + 1)
                if b >= 2:
                    pe.wait_ge(taken, b - 1)
                for k in range(n):
                    pe.matmul(p_o[b % 2][:, k, :], hid[:, b % 2, k * P:(k + 1) * P], w2[:, :], start=True, stop=False)
                    mm = pe.matmul(p_o[b % 2][:, k, :], one[:, :], b2[:, :], start=False, stop=True)
                mm.then_inc(made, 1)

            pe.wait_ge(set_up, 1)
            staggered(turn, first, second)

        @block.scalar
        def _(act):
            act.wait_ge(params, 64)

            def keep(b):
                t0, n = BLOCKS[b]
                act.wait_ge(turned, b + 1)
                if b >= 2:
                    act.wait_ge(hidden, b - 1)
                act.activation(agg_t[:, b % 2, 0:n * P], p_t[b % 2][:, 0:n * P], ACT.Copy).then_inc(kept, 1)

            def act_hidden(b):
                t0, n = BLOCKS[b]
                act.wait_ge(hidden, b + 1)
                if b >= 2:
                    act.wait_ge(made, b - 1)
                act.activation(hid[:, b % 2, 0:n * P], p_h[b % 2][:, 0:n * P], ACT.Silu, bias=b1[:, 0:1]).then_inc(acted, 1)

            staggered(keep, act_hidden)

        @block.vector
        def _(dve):
            then = Chain(dve, chain)
            dve.memset(one[:, :], 1.0).then_inc(set_up, 1)
            then(dve.tensor_tensor(T.X[:, :, :], T.X[:, :, :], T.H[:, :, :], ALU.add))
            for b, (t0, n) in enumerate(BLOCKS):
                dve.wait_ge(made, b + 1)
                dve.tensor_tensor(T.X[:, t0:t0 + n, :], T.X[:, t0:t0 + n, :], p_o[b % 2][:, 0:n, :], ALU.add).then_inc(taken, 1)


BANK = 512
PARTS = 3


class AggInPsum:

    def __init__(self, sb, ps, sem, weights=False):
        banks = TBANKS + 1 if weights else TBANKS
        self.all = ps("sums", [P, banks, BANK])
        flat = self.all[:, :, :].rearrange("p b c -> p (b c)")
        self.sums = flat[:, 0:TILES * D].rearrange("p (t f) -> p t f", f=D)
        if weights:
            per_tile = PARTS * HEADS
            self.in_first = (TBANKS * BANK - TILES * D) // per_tile
            assert (TBANKS * BANK - TILES * D) % per_tile == 0
            self.weights = flat[:, TILES * D:TILES * (D + per_tile)].rearrange("p (t c) -> p t c", c=per_tile)
        self.nil = sb("nil", [P, BANK], BF16)
        self.banks, self.has_weights = banks, weights
        self.nil_ready, self.closed = sem("nil_ready"), sem("sums_closed")

    def clear(self, dve):
        dve.memset(self.nil[:, :], 0.0).then_inc(self.nil_ready, 1)

    def sweep(self, pe, first):
        if first:
            pe.wait_ge(self.nil_ready, 1)
        for b in range(self.banks):
            mm = pe.matmul(self.all[:, b, :], self.nil[:, 0:P], self.nil[:, :], start=first, stop=not first, skip_group_check=True)
        if not first:
            mm.then_inc(self.closed, 1)

    def add(self, pe, tile, onehot, rows):
        return pe.matmul(self.sums[:, bass.ds(tile, 1), :].rearrange("p t f -> p (t f)"), onehot, rows,
                         start=False, stop=False, skip_group_check=True)

    def add_weights(self, pe, tile, onehot, parts):
        return pe.matmul(self.weights[:, bass.ds(tile, 1), :].rearrange("p t c -> p (t c)"), onehot, parts,
                         start=False, stop=False, skip_group_check=True)

    def store(self, dve, T):
        dve.wait_ge(self.closed, 1)
        for b, (t0, n) in enumerate(BLOCKS):
            dve.tensor_copy(T.agg[:, t0:t0 + n, 0:D], self.sums[:, t0:t0 + n, :])
        if self.has_weights:
            for these in (slice(0, self.in_first), slice(self.in_first, TILES)):
                dve.tensor_reduce(T.agg[:, these, D:AW], self.weights[:, these, :].rearrange("p t (c h) -> p t h c", h=HEADS), AX.X, ALU.add)


def sum_pass(nc, A, T):
    with ExitStack() as ctx:
        sb, ps, sem = stack(nc, ctx, "sum_pass_")
        idx = sb("idx1", [P, 4, G], I32)
        hx = sb("hx1", [P, 4, G, D])
        oh = sb("oh1", [P, 2, G, P])
        agg = AggInPsum(sb, ps, sem)
        summed, idx_ready, onehots = sem("l1_summed"), sem("l1_idx_ready"), sem("l1_onehots")
        opened = sem("l1_opened")
        block = ctx.enter_context(nc.Block())

        @block.gpsimd
        def _(pool):
            bound = pool.to_reg(NP - 1)

            def step(g, s, r):
                pool.wait_ge(idx_ready, g + 3)
                if past(g, 2):
                    pool.wait_ge(summed, g - 1)
                pool.sem_inc(opened, 1)
                for k in range(G):
                    pool.indirect_dma_start(out=hx[:, r, k, :], out_offset=None, in_=T.h_table,
                                            in_offset=bass.IndirectOffsetOnAxis(ap=idx[:, r, k:k + 1].bitcast(U32), axis=0),
                                            bounds_check=bound).then_inc(T.gathered[r], 16)

            pipeline(pool, step)

        @block.scalar
        def _(act):
            act.sem_inc(idx_ready, 2)

            def step(g, s, r):
                if past(g, 2):
                    act.wait_ge(summed, g - 1)
                act.activation(idx[:, r, :], T.src[:, bass.ds(g * G, G)], ACT.Copy).then_inc(idx_ready, 1)

            pipeline(act, step)

        @block.tensor
        def _(pe):
            pe.sem_inc(summed, 2)
            agg.sweep(pe, True)
            tiles_of = TurnTiles(nc, pe, T)

            def step(g, s, r):
                tiles = tiles_of(g, r)
                pe.wait_ge(onehots, g + 3)
                wait_gathers(pe, T, 1, g, r)
                for k in range(G):
                    mm = agg.add(pe, tiles[k], oh[:, s, k, :], hx[:, r, k, :])
                mm.then_inc(summed, 1)

            pipeline(pe, step)
            agg.sweep(pe, False)

        @block.vector
        def _(dve):
            dve.sem_inc(onehots, 2)
            agg.clear(dve)

            def step(g, s, r):
                dve.wait_ge(summed, g + 1)
                dve.tensor_tensor(oh[:, s, :, :], T.iota[:, :].unsqueeze(1).to_broadcast([P, G, P]),
                                  T.rel[:, bass.ds(g * G, G)].unsqueeze(2).to_broadcast([P, G, P]),
                                  ALU.is_equal).then_inc(onehots, 1)

            pipeline(dve, step)
            agg.store(dve, T)


class Batchnorm:

    def __init__(self, sb, sem, name, Y):
        self.Y, self.sq = Y, sb(name + "_sq", [P, N])
        self.st, self.gb = sb(name + "_st", [P, 6]), sb(name + "_gb", [P, 2])
        self.centred, self.squared, self.var_ready, self.root, self.scaled, self.done, self.params = (
            sem(name + n) for n in ("_centred", "_squared", "_var", "_root", "_scaled", "_done", "_gb_in"))

    def load(self, sp, gamma, beta):
        sp.dma_start(self.gb[:, 0:1], gamma.rearrange("(p o) -> p o", o=1)).then_inc(self.params, 16)
        sp.dma_start(self.gb[:, 1:2], beta.rearrange("(p o) -> p o", o=1)).then_inc(self.params, 16)

    def on_vector(self, dve, then):
        st, Y = self.st, self.Y
        then(dve.tensor_reduce(st[:, 0:1], Y[:, 0:N], AX.X, ALU.add))
        then(dve.tensor_scalar(st[:, 0:1], st[:, 0:1], 1.0 / N, None, ALU.mult))
        dve.tensor_scalar(Y[:, :], Y[:, :], st[:, 0:1], None, ALU.subtract).then_inc(self.centred, 1)
        dve.wait_ge(self.squared, 1)
        then(dve.tensor_reduce(st[:, 1:2], self.sq[:, :], AX.X, ALU.add))
        dve.tensor_scalar(st[:, 1:2], st[:, 1:2], 1.0 / N, EPS, ALU.mult, ALU.add).then_inc(self.var_ready, 1)
        dve.wait_ge(self.root, 1)
        then(dve.reciprocal(st[:, 3:4], st[:, 2:3]))
        dve.wait_ge(self.params, 32)
        dve.tensor_tensor(st[:, 4:5], st[:, 3:4], self.gb[:, 0:1], ALU.mult).then_inc(self.scaled, 1)

    def on_scalar(self, act, func):
        st, Y = self.st, self.Y
        act.wait_ge(self.centred, 1)
        act.activation(self.sq[:, :], Y[:, 0:N], ACT.Square).then_inc(self.squared, 1)
        act.wait_ge(self.var_ready, 1)
        act.activation(st[:, 2:3], st[:, 1:2], ACT.Sqrt).then_inc(self.root, 1)
        act.wait_ge(self.scaled, 1)
        act.activation(Y[:, :], Y[:, :], func, bias=self.gb[:, 1:2], scale=st[:, 4:5]).then_inc(self.done, 1)


def node_gin(nc, A, T):
    with ExitStack() as ctx:
        sb, ps, sem = stack(nc, ctx, "node_gin_")
        w1, w2 = sb("w1", [D, D]), sb("w2", [D, D])
        bias = sb("bias_n1", [P, 3])
        Z, Y = sb("Z", [P, TILES, D]), sb("Y", [P, NP])
        in_t, hid = sb("in_t", [P, 2, 512]), sb("hid_n1", [P, 2, 512])
        p_t = [ps(f"p_t{i}", [P, 512]) for i in range(2)]
        p_h = [ps(f"p_h{i}", [P, 512]) for i in range(2)]
        p_y = [ps(f"p_y{i}", [P, 512]) for i in range(2)]
        p_b = [ps(f"p_b{i}", [P, 4, D]) for i in range(2)]
        params, eps_in, chain, z_ready = sem("n1_params"), sem("eps_in"), sem("n1_chain"), sem("n1_z_ready")
        turned, kept, hidden, acted, made, y_ready, back, taken = (
            sem("n1_" + n) for n in ("turned", "kept", "hidden", "acted", "made", "y_ready", "back", "taken"))
        bn = Batchnorm(sb, sem, "bn1_", Y)
        block = ctx.enter_context(nc.Block())
        NB = len(BLOCKS)

        @block.sync
        def _(sp):
            sp.dma_start(bias[:, 2:3], A["L1_gnn_eps"].partition_broadcast(P)).then_inc(eps_in, 16)
            sp.dma_start(w1[:, :], A["L1_gnn_W1"]).then_inc(params, 16)
            sp.dma_start(w2[:, :], A["L1_gnn_W2"]).then_inc(params, 16)
            sp.dma_start(bias[:, 0:1], A["L1_gnn_b1"].rearrange("(p o) -> p o", o=1)).then_inc(params, 16)
            sp.dma_start(bias[:, 1:2], A["L1_gnn_b2"].rearrange("(p o) -> p o", o=1)).then_inc(params, 16)
            bn.load(sp, A["L1_gnn_gamma"], A["L1_gnn_beta"])

        @block.tensor
        def _(pe):
            pe.wait_ge(z_ready, 1)

            def turn(b):
                t0, n = BLOCKS[b]
                if b >= 2:
                    pe.wait_ge(kept, b - 1)
                for k in range(n):
                    tr = pe.transpose(p_t[b % 2][:, k * P:(k + 1) * P], Z[:, t0 + k, :], T.ident[:, :])
                tr.then_inc(turned, 1)

            def first(b):
                t0, n = BLOCKS[b]
                if b == 0:
                    pe.wait_ge(params, 64)
                pe.wait_ge(kept, b + 1)
                if b >= 2:
                    pe.wait_ge(acted, b - 1)
                pe.matmul(p_h[b % 2][:, 0:n * P], w1[:, :], in_t[:, b % 2, 0:n * P], start=True, stop=True).then_inc(hidden, 1)

            def second(b):
                t0, n = BLOCKS[b]
                pe.wait_ge(acted, b + 1)
                if b >= 2:
                    pe.wait_ge(y_ready, b - 1)
                pe.matmul(p_y[b % 2][:, 0:n * P], w2[:, :], hid[:, b % 2, 0:n * P], start=True, stop=True).then_inc(made, 1)

            staggered(turn, first, second)
            pe.wait_ge(bn.done, 1)
            for b, (t0, n) in enumerate(BLOCKS):
                if b >= 2:
                    pe.wait_ge(taken, b - 1)
                for k in range(n):
                    tr = pe.transpose(p_b[b % 2][:, k, :], Y[:, (t0 + k) * P:(t0 + k + 1) * P], T.ident[:, :])
                tr.then_inc(back, 1)

        @block.scalar
        def _(act):
            act.wait_ge(params, 64)

            def keep(b):
                t0, n = BLOCKS[b]
                act.wait_ge(turned, b + 1)
                if b >= 2:
                    act.wait_ge(hidden, b - 1)
                act.activation(in_t[:, b % 2, 0:n * P], p_t[b % 2][:, 0:n * P], ACT.Copy).then_inc(kept, 1)

            def act_first(b):
                t0, n = BLOCKS[b]
                act.wait_ge(hidden, b + 1)
                if b >= 2:
                    act.wait_ge(made, b - 1)
                act.activation(hid[:, b % 2, 0:n * P], p_h[b % 2][:, 0:n * P], ACT.Relu, bias=bias[:, 0:1]).then_inc(acted, 1)

            def act_second(b):
                t0, n = BLOCKS[b]
                act.wait_ge(made, b + 1)
                act.activation(Y[:, t0 * P:(t0 + n) * P], p_y[b % 2][:, 0:n * P], ACT.Identity, bias=bias[:, 1:2]).then_inc(y_ready, 1)

            staggered(keep, act_first, act_second)
            bn.on_scalar(act, ACT.Relu)

        @block.vector
        def _(dve):
            then = Chain(dve, chain)
            dve.wait_ge(eps_in, 16)
            then(dve.tensor_scalar(bias[:, 2:3], bias[:, 2:3], 1.0, None, ALU.add))
            dve.scalar_tensor_tensor(out=Z[:, :, :], in0=T.H[:, :, :], scalar=bias[:, 2:3], in1=T.agg[:, :, 0:D],
                                     op0=ALU.mult, op1=ALU.add).then_inc(z_ready, 1)
            dve.wait_ge(y_ready, NB)
            bn.on_vector(dve, then)
            for b, (t0, n) in enumerate(BLOCKS):
                dve.wait_ge(back, b + 1)
                dve.tensor_tensor(T.X[:, t0:t0 + n, :], T.X[:, t0:t0 + n, :], p_b[b % 2][:, 0:n, :], ALU.add).then_inc(taken, 1)


def scan_flags(nc, A, T):
    with ExitStack() as ctx:
        sb, ps, sem = stack(nc, ctx, "scan_flags_")
        keys = sb("keys", [P, LE + 2])
        shift = sb("shift", [P, 2, P])
        whole, inner = sb("whole", [P, 2]), sb("inner", [P, 1])
        differs = sb("differs", [P, LE + 1])
        nti, nbi = sb("nti", [TILES, P], I32), sb("nbi", [P, NP], I32)
        ntf = sb("ntf", [TILES, P])
        typed = sem("typed")
        p_k = [ps(f"p_k{i}", [P, 4, P]) for i in range(2)]
        p_e, p_r = ps("p_e", [P, 512]), ps("p_r", [P, 512])
        chain, turned, taken, shifts, edges, set_up = (sem("fl_" + n) for n in ("chain", "turned", "taken", "shifts", "edges", "set_up"))
        wholes, rows, types_in = sem("fl_wholes"), sem("fl_rows"), sem("fl_types_in")
        block = ctx.enter_context(nc.Block())
        spread, compared = sem("spread"), sem("compared")
        lanes = T.att[:, :, :].rearrange("p v h -> p (v h)").rearrange("p (j l h) -> p j l h", l=LANES, h=HEADS)
        quads = [(j, min(4, LV - j)) for j in range(0, LV, 4)]

        @block.sync
        def _(sp):
            full = N // P
            sp.wait_ge(set_up, 2)
            nt = A["node_type_8"]
            sp.dma_start(nti[0:full, :], nt[0:full * P].rearrange("(t p) -> t p", p=P)).then_inc(types_in, 16)
            sp.dma_start(nti[full:full + 1, 0:N - full * P], nt[full * P:N].rearrange("(o p) -> o p", o=1)).then_inc(types_in, 16)
            sp.dma_start(nbi[:, 0:N], nt.partition_broadcast(P)).then_inc(types_in, 16)

        @block.scalar
        def _(act):
            act.wait_ge(types_in, 48)
            act.activation(T.type_row[:, :], nbi[:, :], ACT.Copy)
            act.wait_ge(compared, 1)
            act.activation(T.flag[:, :], differs[:, :], ACT.Copy, scale=-BIG)

        @block.gpsimd
        def _(pool):
            pool.memset(shift[:, :, :], 0.0).then_inc(shifts, 1)
            pool.wait_ge(shifts, 1)
            pool.affine_select(out=shift[:, 0, :], in_=shift[:, 0, :], compare_op=ALU.not_equal, fill=1.0, base=HEADS,
                               pattern=[[-1, P]], channel_multiplier=1).then_inc(shifts, 1)
            pool.affine_select(out=shift[:, 1, :], in_=shift[:, 1, :], compare_op=ALU.not_equal, fill=1.0, base=-HEADS,
                               pattern=[[-1, P]], channel_multiplier=1).then_inc(shifts, 1)

        @block.tensor
        def _(pe):
            pe.wait_ge(spread, 1)
            for b, (j, n) in enumerate(quads):
                if b >= 2:
                    pe.wait_ge(taken, b - 1)
                for k in range(n):
                    tr = pe.transpose(p_k[b % 2][:, k, :], lanes[:, j + k].rearrange("p l h -> p (l h)"), T.ident[:, :])
                tr.then_inc(turned, 1)
            pe.wait_ge(taken, len(quads))
            pe.wait_ge(shifts, 3)
            pe.matmul(p_e[:, 0:1], shift[:, 0, :], keys[:, LE:LE + 1], start=True, stop=True)
            pe.matmul(p_e[:, 1:2], shift[:, 1, :], keys[:, 1:2], start=True, stop=True).then_inc(edges, 1)
            pe.wait_ge(wholes, 1)
            pe.transpose(p_r[0:1, 0:P], whole[:, 0:1], T.ident[:, :])
            pe.transpose(p_r[0:1, P:2 * P], whole[:, 1:2], T.ident[:, :]).then_inc(rows, 1)
            pe.wait_ge(typed, 1)
            pe.transpose(p_e[:, 2:2 + TILES], ntf[:, :], T.ident[0:TILES, 0:TILES]).then_inc(rows, 1)

        @block.vector
        def _(dve):
            then = Chain(dve, chain)
            dve.memset(nti[:, :], -1).then_inc(set_up, 1)
            dve.memset(nbi[:, :], -1).then_inc(set_up, 1)
            dve.tensor_copy(lanes, T.key[:, 0:SV].rearrange("p (l j) -> p j l", j=LV).unsqueeze(3).to_broadcast([P, LV, LANES, HEADS])).then_inc(spread, 1)
            for b, (j, n) in enumerate(quads):
                dve.wait_ge(turned, b + 1)
                dve.tensor_copy(keys[:, 1 + j * P:1 + (j + n) * P], p_k[b % 2][:, 0:n, :].rearrange("p k e -> p (k e)")).then_inc(taken, 1)
            dve.wait_ge(edges, 1)
            then(dve.tensor_copy(keys[:, 0:1], p_e[:, 0:1]))
            then(dve.tensor_copy(keys[:, LE + 1:LE + 2], p_e[:, 1:2]))
            dve.tensor_tensor(differs[:, :], keys[:, 1:LE + 2], keys[:, 0:LE + 1], ALU.not_equal).then_inc(compared, 1)
            dve.wait_ge(compared, 1)
            then(dve.tensor_reduce(inner[:, :], differs[:, 1:LE], AX.X, ALU.max))
            then(dve.tensor_tensor(whole[:, 0:1], differs[:, 0:1], inner[:, :], ALU.max))
            then(dve.tensor_tensor(whole[:, 1:2], differs[:, LE:LE + 1], inner[:, :], ALU.max))
            dve.tensor_scalar(whole[:, :], whole[:, :], -BIG, None, ALU.mult).then_inc(wholes, 1)
            dve.wait_ge(rows, 1)
            dve.tensor_copy(T.whole[:, :, :], p_r[0:1, 0:2 * P].rearrange("o (k p) -> o k p", k=2))
            dve.wait_ge(types_in, 48)
            dve.tensor_copy(ntf[:, :], nti[:, :]).then_inc(typed, 1)
            dve.wait_ge(rows, 2)
            dve.tensor_copy(T.type_of[:, :], p_e[:, 2:2 + TILES])
            dve.memset(T.att[:, VISITS:SV, :], 0.0)


def typed_qkv(nc, A, T, l):
    with ExitStack() as ctx:
        sb, ps, sem = stack(nc, ctx)
        nm = f"qkv{l}_"
        w = [sb(f"{nm}w{k}", [D, TYPES, D]) for k in range(3)]
        bd = [sb(f"{nm}bd{k}", [D, REL, D]) for k in range(2)]
        pri = sb(nm + "pri", [P, REL])
        e_t = sb(nm + "e_t", [P, 512])
        xm = sb(nm + "xm", [P, 2, TYPES, 512])
        kv_t = sb(nm + "kv_t", [P, 2, 512])
        rows = sb(nm + "rows", [P, 2, REL, 2, D])
        p_t, p_q = ps(nm + "p_t", [P, 512]), ps(nm + "p_q", [P, 4, D])
        p_kv = [ps(f"{nm}p_kv{k}", [P, 512]) for k in range(2)]
        p_r = [ps(f"{nm}p_r{k}", [P, 4, D]) for k in range(4)]
        params, zeroed, chain, bd_ready = (sem(nm + n) for n in ("params", "zeroed", "chain", "bd_ready"))
        turned, kept, masked, projected, cast, q_made, q_kept = (
            sem(nm + n) for n in ("turned", "kept", "masked", "projected", "cast", "q_made", "q_kept"))
        w_in = sem(nm + "w_in")
        related = sem(nm + "related")
        by_act, by_dve = sem(nm + "by_act"), sem(nm + "by_dve")
        stored = [sem(f"{nm}stored{i}") for i in range(2)]
        block = ctx.enter_context(nc.Block())
        table = T.kv_table.rearrange("(n r) (c f) -> n r c f", r=REL, f=D)

        @block.sync
        def _(sp):
            for k, name in enumerate(("Wk", "Wv", "Wq")):
                sp.dma_start(w[k][:, :, :], A["L2_gnn_" + name][l].rearrange("t i o -> i t o")).then_inc(w_in, 16)
            sp.wait_ge(zeroed, 2)
            for h in range(HEADS):
                of = slice(h * HS, (h + 1) * HS)
                sp.dma_start(bd[0][of, :, of], A["L2_gnn_Watt"][l, h].rearrange("r i o -> i r o")).then_inc(params, 16)
                sp.dma_start(bd[1][of, :, of], A["L2_gnn_Wmsg"][l, h].rearrange("r i o -> i r o")).then_inc(params, 16)
                sp.dma_start(pri[of, :], A["L2_gnn_pri"][l, h].partition_broadcast(HS)).then_inc(params, 16)
            for t in range(TILES):
                sp.wait_ge(by_act, 2 * (t + 1))
                sp.wait_ge(by_dve, 2 * (t + 1))
                sp.dma_start(table[t * P:(t + 1) * P], rows[:, t % 2]).then_inc(stored[t % 2], 16)
            sp.wait_ge(stored[0], 16 * ((TILES + 1) // 2))
            sp.wait_ge(stored[1], 16 * (TILES // 2))

        @block.tensor
        def _(pe):

            def turn(b):
                t0, n = BLOCKS[b]
                if b >= 1:
                    pe.wait_ge(kept, b)
                for k in range(n):
                    tr = pe.transpose(p_t[:, k * P:(k + 1) * P], T.H[:, t0 + k, :], T.ident[:, :])
                tr.then_inc(turned, 1)

            turn(0)
            for b, (t0, n) in enumerate(BLOCKS):
                if b + 1 < len(BLOCKS):
                    turn(b + 1)
                pe.wait_ge(masked, b + 1)
                if b == 0:
                    pe.wait_ge(w_in, 48)
                for c in range(2):
                    if b >= 1:
                        pe.wait_ge(cast, 2 * b - 1 + c)
                    for t in range(TYPES):
                        mm = pe.matmul(p_kv[c][:, 0:n * P], w[c][:, t, :], xm[:, b % 2, t, 0:n * P], start=(t == 0), stop=(t == TYPES - 1))
                    mm.then_inc(projected, 1)
                if b >= 1:
                    pe.wait_ge(q_kept, b)
                for k in range(n):
                    for t in range(TYPES):
                        mm = pe.matmul(p_q[:, k, :], xm[:, b % 2, t, k * P:(k + 1) * P], w[2][:, t, :], start=(t == 0), stop=(t == TYPES - 1))
                mm.then_inc(q_made, 1)
                pe.wait_ge(cast, 2 * (b + 1))
                pe.wait_ge(bd_ready, 1)
                for k in range(n):
                    t = t0 + k
                    for c in range(2):
                        for half in range(2):
                            if t >= 1:
                                pe.wait_ge(by_dve if c else by_act, 2 * t - 1 + half)
                            pe.matmul(p_r[2 * c + half][:, :, :], kv_t[:, c, k * P:(k + 1) * P],
                                      bd[c][:, 4 * half:4 * half + 4, :], start=True, stop=True).then_inc(related, 1)

        @block.scalar
        def _(act):

            def keep(b):
                w = BLOCKS[b][1] * P
                act.wait_ge(turned, b + 1)
                if b >= 1:
                    act.wait_ge(masked, b)
                act.activation(e_t[:, 0:w], p_t[:, 0:w], ACT.Copy).then_inc(kept, 1)

            keep(0)
            for b, (t0, n) in enumerate(BLOCKS):
                if b + 1 < len(BLOCKS):
                    keep(b + 1)
                for c in range(2):
                    act.wait_ge(projected, 2 * b + c + 1)
                    if b >= 1:
                        act.wait_ge(related, 4 * t0)
                    act.activation(kv_t[:, c, 0:n * P], p_kv[c][:, 0:n * P], ACT.Copy).then_inc(cast, 1)
                act.wait_ge(q_made, b + 1)
                act.activation(T.Q[:, t0:t0 + n, :], p_q[:, 0:n, :], ACT.Copy).then_inc(q_kept, 1)
                for k in range(n):
                    t = t0 + k
                    if t >= 2:
                        act.wait_ge(stored[t % 2], 16 * (t // 2))
                    for half in range(2):
                        act.wait_ge(related, 4 * t + half + 1)
                        act.activation(rows[:, t % 2, 4 * half:4 * half + 4, 0, :], p_r[half][:, :, :], ACT.Copy).then_inc(by_act, 1)

        @block.vector
        def _(dve):
            then = Chain(dve, chain)
            for c in range(2):
                dve.memset(bd[c][:, :, :], 0.0).then_inc(zeroed, 1)

            def mask(b):
                t0, n = BLOCKS[b]
                dve.wait_ge(kept, b + 1)
                if b >= 2:
                    dve.wait_ge(q_made, b - 1)
                for t in range(TYPES):
                    ins = dve.scalar_tensor_tensor(out=xm[:, b % 2, t, 0:n * P], in0=T.type_row[:, t0 * P:(t0 + n) * P], scalar=float(t),
                                                   in1=e_t[:, 0:n * P], op0=ALU.is_equal, op1=ALU.mult)
                ins.then_inc(masked, 1)

            mask(0)
            dve.wait_ge(params, 16 * 3 * HEADS)
            then(dve.tensor_scalar(pri[:, :], pri[:, :], 1.0 / float(HS) ** 0.5, None, ALU.mult))
            dve.tensor_tensor(bd[0][:, :, :], bd[0][:, :, :], pri[:, :].unsqueeze(2).to_broadcast([P, REL, D]), ALU.mult).then_inc(bd_ready, 1)
            for b, (t0, n) in enumerate(BLOCKS):
                if b + 1 < len(BLOCKS):
                    mask(b + 1)
                for k in range(n):
                    t = t0 + k
                    if t >= 2:
                        dve.wait_ge(stored[t % 2], 16 * (t // 2))
                    for half in range(2):
                        dve.wait_ge(related, 4 * t + half + 3)
                        dve.tensor_copy(rows[:, t % 2, 4 * half:4 * half + 4, 1, :], p_r[2 + half][:, :, :]).then_inc(by_dve, 1)


def score_pass(nc, A, T, l):
    with ExitStack() as ctx:
        sb, ps, sem = stack(nc, ctx)
        nm = f"sc{l}_"
        idx = sb(nm + "idx", [P, 4, G], I32)
        kv = sb(nm + "kv", [P, 4, G, 2 * D])
        oh = sb(nm + "oh", [P, 2, G, P])
        oh_t = sb(nm + "oh_t", [P, 2, G, P])
        prod = sb(nm + "prod", [P, G, D])
        p_t = [ps(f"{nm}p_t{i}", [P, G, P]) for i in range(2)]
        p_q = [ps(f"{nm}p_q{i}", [P, G, D]) for i in range(2)]
        m_out = [sem(f"{nm}m_out{i}") for i in range(4)]
        idx_ready, onehots, turned, kept, spread, scored = (sem(nm + n) for n in ("idx_ready", "onehots", "turned", "kept", "spread", "scored"))
        opened, multiplied = sem(nm + "opened"), sem(nm + "multiplied")
        block = ctx.enter_context(nc.Block())
        m_slots = T.m_table.rearrange("(v p) f -> p v f", p=P)

        @block.sync
        def _(sp):
            def step(g, s, r):
                wait_gathers(sp, T, 2 + l, g, r)
                sp.dma_start(m_slots[:, bass.ds(g * G, G), :], kv[:, r, :, D:2 * D]).then_inc(m_out[r], 16)

            pipeline(sp, step)
            for r in range(4):
                sp.wait_ge(m_out[r], 16 * (len(range(r, GROUPS, 4)) + 1))

        @block.gpsimd
        def _(pool):
            bound = pool.to_reg(NP * REL - 1)
            for r in range(4):
                pool.sem_inc(m_out[r], 16)

            def step(g, s, r):
                pool.wait_ge(idx_ready, g + 3)
                if past(g, 2):
                    pool.wait_ge(scored, g - 1)
                pool.wait_ge(m_out[r], turns(g, r, 16))
                pool.sem_inc(opened, 1)
                for k in range(G):
                    pool.indirect_dma_start(out=kv[:, r, k, :], out_offset=None, in_=T.kv_table,
                                            in_offset=bass.IndirectOffsetOnAxis(ap=idx[:, r, k:k + 1].bitcast(U32), axis=0),
                                            bounds_check=bound).then_inc(T.gathered[r], 16)

            pipeline(pool, step)

        @block.scalar
        def _(act):
            act.sem_inc(idx_ready, 2)
            act.sem_inc(kept, 2)

            def step(g, s, r):
                if past(g, 2):
                    act.wait_ge(scored, g - 1)
                act.activation(idx[:, r, :], T.srcrel[:, bass.ds(g * G, G)], ACT.Copy).then_inc(idx_ready, 1)
                act.wait_ge(turned, g + 3)
                act.wait_ge(spread, g + 1)
                act.activation(oh_t[:, s, :, :], p_t[s][:, :, :], ACT.Copy).then_inc(kept, 1)

            pipeline(act, step)

        @block.tensor
        def _(pe):
            pe.sem_inc(turned, 2)
            pe.sem_inc(spread, 2)

            tiles_of = TurnTiles(nc, pe, T)

            def step(g, s, r):
                pe.wait_ge(onehots, g + 3)
                pe.wait_ge(kept, g + 1)
                tiles = tiles_of(g, r)
                for k in range(G):
                    tr = pe.transpose(p_t[s][:, k, :], oh[:, s, k, :], T.ident[:, :])
                tr.then_inc(turned, 1)
                pe.wait_ge(kept, g + 3)
                pe.wait_ge(scored, g + 1)
                for k in range(G):
                    q = T.Q[:, bass.ds(tiles[k], 1), :].rearrange("p t f -> p (t f)")
                    mm = pe.matmul(p_q[s][:, k, :], oh_t[:, s, k, :], q, start=True, stop=True)
                mm.then_inc(spread, 1)

            pipeline(pe, step)

        @block.vector
        def _(dve):
            dve.sem_inc(onehots, 2)
            dve.sem_inc(scored, 2)

            def step(g, s, r):
                if within(g):
                    dve.wait_ge(turned, g + 1)
                    dve.tensor_tensor(oh[:, s, :, :], T.iota[:, :].unsqueeze(1).to_broadcast([P, G, P]),
                                      T.rel[:, bass.ds(g * G, G)].unsqueeze(2).to_broadcast([P, G, P]),
                                      ALU.is_equal).then_inc(onehots, 1)
                if past(g, 1):
                    h, q = g - 1, 1 - s
                    wait_gathers(dve, T, 2 + l, h, (r - 1) % 4)
                    dve.wait_ge(spread, h + 3)
                    if past(h, 1):
                        dve.wait_ge(scored, h + 2)
                    dve.tensor_tensor(prod[:, :, :], kv[:, (r - 1) % 4, :, 0:D], p_q[q][:, :, :], ALU.mult).then_inc(multiplied, 1)
                    dve.wait_ge(multiplied, h + 1)
                    dve.tensor_reduce(T.att[:, bass.ds(h * G, G), :].rearrange("p v h -> p (v h)"),
                                      prod[:, :, :].rearrange("p k (h o) -> p (k h) o", o=HS), AX.X, ALU.add).then_inc(scored, 1)

            pipeline(dve, step, drain=(GROUPS,))


def softmax_shift(nc, A, T, l):
    with ExitStack() as ctx:
        sb, ps, sem = stack(nc, ctx)
        nm = f"mx{l}_"
        a_t, top = sb(nm + "a_t", [P, LE]), sb(nm + "top", [P, LE])
        whole_max = T.att[:, :, :].rearrange("p v h -> p (v h)")
        ends, into = sb(nm + "ends", [1, 2, P]), sb(nm + "into", [1, 2, P])
        start = sb(nm + "start", [P, 2])
        p_l = [ps(f"{nm}p_l{i}", [P, 4, P]) for i in range(3)]
        p_e, p_s = ps(nm + "p_e", [P, 512]), ps(nm + "p_s", [P, 512])
        chain, turned, by_act, by_dve, ended, row_made, carried, started = (
            sem(nm + n) for n in ("chain", "turned", "by_act", "by_dve", "ended", "row_made", "carried", "started"))
        shifted, exped, back, placed = (sem(nm + n) for n in ("shifted", "exped", "back", "placed"))
        block = ctx.enter_context(nc.Block())
        lanes = top[:, :].rearrange("p (j l h) -> p j l h", l=LANES, h=HEADS)
        ordered = sem(nm + "ordered")
        quads = [(j, min(4, LV - j)) for j in range(0, LV, 4)]
        NQ = len(quads)

        @block.tensor
        def _(pe):
            for b, (j, n) in enumerate(quads):
                pe.wait_ge(ordered, b + 1)
                if b >= 3:
                    pe.wait_ge(by_act, b - 2)
                for k in range(n):
                    tr = pe.transpose(p_l[b % 3][:, k, :], lanes[:, j + k].rearrange("p l h -> p (l h)"), T.ident[:, :])
                tr.then_inc(turned, 1)
            for d in range(2):
                pe.wait_ge(ended, d + 1)
                last = top[:, LE - 1:LE] if d == 0 else whole_max[:, 0:1]
                pe.transpose(p_e[0:1, d * P:(d + 1) * P], last, T.ident[:, :]).then_inc(row_made, 1)
                pe.wait_ge(carried, d + 1)
                pe.transpose(p_s[:, d:d + 1], into[0:1, d, :], T.ident[0:1, 0:1]).then_inc(started, 1)
            for b, (j, n) in enumerate(quads):
                pe.wait_ge(exped, b + 1)
                if b >= 3:
                    pe.wait_ge(placed, b - 2)
                else:
                    pe.wait_ge(by_act, NQ)
                for k in range(n):
                    tr = pe.transpose(p_l[b % 3][:, k, :], a_t[:, (j + k) * P:(j + k + 1) * P], T.ident[:, :])
                tr.then_inc(back, 1)

        @block.scalar
        def _(act):
            for b, (j, n) in enumerate(quads):
                act.wait_ge(turned, b + 1)
                act.activation(a_t[:, j * P:(j + n) * P], p_l[b % 3][:, 0:n, :].rearrange("p k e -> p (k e)"), ACT.Copy).then_inc(by_act, 1)
            act.wait_ge(shifted, 1)
            for b, (j, n) in enumerate(quads):
                act.activation(a_t[:, j * P:(j + n) * P], a_t[:, j * P:(j + n) * P], ACT.Exp).then_inc(exped, 1)

        @block.vector
        def _(dve):
            then = Chain(dve, chain)
            for j, n in quads:
                dve.tensor_copy(lanes[:, j:j + n], T.att[:, :, :].rearrange("p (l j) h -> p j l h", j=LV)[:, j:j + n]).then_inc(ordered, 1)
            dve.wait_ge(by_act, NQ)

            def forwards(initial):
                return dve.tensor_tensor_scan(top[:, :], T.flag[:, 0:LE], a_t[:, :], initial, ALU.add, ALU.max)

            def backwards(initial):
                return dve.tensor_tensor_scan(whole_max[:, ::-1], T.flag[:, 1:LE + 1][:, ::-1], top[:, ::-1], initial, ALU.add, ALU.max)

            for d, scan in enumerate((forwards, backwards)):
                scan(-BIG).then_inc(ended, 1)
                dve.wait_ge(row_made, d + 1)
                then(dve.tensor_copy(ends[:, d, :], p_e[0:1, d * P:(d + 1) * P]))
                for h in range(HEADS):
                    def along(row):
                        v = row.rearrange("o (l h) -> o l h", h=HEADS)[:, :, h]
                        return v[:, ::-1] if d else v
                    ins = dve.tensor_tensor_scan(along(ends[:, d, :]), along(T.whole[:, d, :]), along(ends[:, d, :]), -BIG, ALU.add, ALU.max)
                    then(ins)
                then(dve.memset(into[:, d, :], -BIG))
                if d == 0:
                    dve.tensor_copy(into[:, 0, HEADS:P], ends[:, 0, 0:P - HEADS]).then_inc(carried, 1)
                else:
                    dve.tensor_copy(into[:, 1, 0:P - HEADS], ends[:, 1, HEADS:P]).then_inc(carried, 1)
                dve.wait_ge(started, d + 1)
                then(dve.tensor_copy(start[:, d:d + 1], p_s[:, d:d + 1]))
                then(scan(start[:, d:d + 1]))
            dve.tensor_tensor(a_t[:, :], a_t[:, :], whole_max, ALU.subtract).then_inc(shifted, 1)
            for b, (j, n) in enumerate(quads):
                dve.wait_ge(back, b + 1)
                if b == 0:
                    dve.wait_ge(shifted, 1)
                dve.tensor_copy(T.att[:, :, :].rearrange("p (l j) h -> p j l h", j=LV)[:, j:j + n],
                                p_l[b % 3][:, 0:n, :].rearrange("p k (l h) -> p k l h", h=HEADS)).then_inc(placed, 1)


def message_pass(nc, A, T, l):
    with ExitStack() as ctx:
        sb, ps, sem = stack(nc, ctx, f"ms{l}_")
        m = sb("m", [P, 4, G, D])
        oh = sb("oh", [P, 4, G, P])
        msg = sb("msg", [P, 4, G, D])
        narrow = sb("narrow", [P, 4, G, P], BF16)
        parts = sb("parts", [P, 4, G, PARTS, HEADS], BF16)
        rest = sb("rest", [P, 4, G, HEADS])
        agg = AggInPsum(sb, ps, sem, weights=True)
        m_in = [sem(f"m_in{i}") for i in range(4)]
        messages, split, summed = (sem(n) for n in ("messages", "split", "summed"))
        high, rests, middle = (sem(n) for n in ("high", "rests", "middle"))
        block = ctx.enter_context(nc.Block())
        m_slots = T.m_table.rearrange("(v p) f -> p v f", p=P)

        @block.sync
        def _(sp):
            def step(g, s, r):
                if past(g, 2):
                    sp.wait_ge(messages, g - 1)
                sp.dma_start(m[:, r, :, :], m_slots[:, bass.ds(g * G, G), :]).then_inc(m_in[r], 16)

            pipeline(sp, step)

        @block.scalar
        def _(act):
            for q in (high, middle):
                act.sem_inc(q, 2)

            def step(g, s, r):
                if past(g, 2):
                    act.wait_ge(summed, g - 1)
                act.activation(parts[:, r, :, 0, :], T.att[:, bass.ds(g * G, G), :], ACT.Copy).then_inc(high, 1)
                act.wait_ge(rests, g + 3)
                act.activation(narrow[:, r, :, :], oh[:, r, :, :], ACT.Copy)
                act.activation(parts[:, r, :, 1, :], rest[:, r, :, :], ACT.Copy).then_inc(middle, 1)

            pipeline(act, step)

        @block.tensor
        def _(pe):
            pe.sem_inc(summed, 2)
            agg.sweep(pe, True)
            tiles_of = TurnTiles(nc, pe, T)

            def step(g, s, r):
                if s == 0:
                    return
                pe.wait_ge(split, g + 3)
                for h, q in ((g - 1, r - 1), (g, r)):
                    tiles = tiles_of(h, q)
                    for k in range(G):
                        agg.add(pe, tiles[k], oh[:, q, k, :], msg[:, q, k, :])
                    for k in range(G):
                        mm = agg.add_weights(pe, tiles[k], narrow[:, q, k, :], parts[:, q, k, :, :].rearrange("p c h -> p (c h)"))
                mm.then_inc(summed, 2)

            pipeline(pe, step, turn=8)
            agg.sweep(pe, False)

        @block.vector
        def _(dve):
            for q in (messages, rests, split):
                dve.sem_inc(q, 2)
            agg.clear(dve)

            def step(g, s, r):
                if past(g, 2):
                    dve.wait_ge(summed, g - 1)
                dve.tensor_tensor(oh[:, r, :, :], T.iota[:, :].unsqueeze(1).to_broadcast([P, G, P]),
                                  T.rel[:, bass.ds(g * G, G)].unsqueeze(2).to_broadcast([P, G, P]),
                                  ALU.is_equal)
                dve.wait_ge(high, g + 3)
                dve.tensor_tensor(rest[:, r, :, :], T.att[:, bass.ds(g * G, G), :], parts[:, r, :, 0, :], ALU.subtract).then_inc(rests, 1)
                dve.wait_ge(m_in[r], turns(g, r, 16))
                dve.tensor_tensor(msg[:, r, :, :].rearrange("p k (h o) -> p k h o", o=HS),
                                  m[:, r, :, :].rearrange("p k (h o) -> p k h o", o=HS),
                                  T.att[:, bass.ds(g * G, G), :].unsqueeze(3).to_broadcast([P, G, HEADS, HS]), ALU.mult).then_inc(messages, 1)
                dve.wait_ge(middle, g + 3)
                dve.tensor_tensor(parts[:, r, :, 2, :], rest[:, r, :, :], parts[:, r, :, 1, :], ALU.subtract).then_inc(split, 1)

            pipeline(dve, step)
            agg.store(dve, T)


def node_update(nc, A, T, l):
    with ExitStack() as ctx:
        sb, ps, sem = stack(nc, ctx)
        nm = f"up{l}_"
        wa = sb(nm + "wa", [D, TYPES, D])
        par = sb(nm + "par", [P, 2, D])
        skip = sb(nm + "skip", [P, TYPES])
        den = sb(nm + "den", [P, TILES, HEADS])
        al = sb(nm + "al", [P, 2, TILES])
        Z, O = sb(nm + "Z", [P, TILES, D]), sb(nm + "O", [P, TILES, D])
        st = sb(nm + "st", [P, 4, TILES])
        z_t, xm = sb(nm + "z_t", [P, 512]), sb(nm + "xm", [P, 2, TYPES, 512])
        p_t, p_o = ps(nm + "p_t", [P, 512]), [ps(f"{nm}p_o{i}", [P, 4, D]) for i in range(2)]
        params, chain, z_ready, turned, kept, masked, made, silued, al_sum, al_ready = (
            sem(nm + n) for n in ("params", "chain", "z_ready", "turned", "kept", "masked", "made", "silued", "al_sum", "al_ready"))
        centred, squared, var_ready, root = (sem(nm + n) for n in ("centred", "squared", "var_ready", "root"))
        block = ctx.enter_context(nc.Block())
        NB = len(BLOCKS)

        @block.sync
        def _(sp):
            sp.dma_start(skip[:, :], A["L2_gnn_skip"][l].partition_broadcast(P)).then_inc(params, 16)
            sp.dma_start(wa[:, :, :], A["L2_gnn_Wa"][l].rearrange("t i o -> i t o")).then_inc(params, 16)
            sp.dma_start(par[:, 0, :], A["L2_gnn_ln_g"][l].partition_broadcast(P)).then_inc(params, 16)
            sp.dma_start(par[:, 1, :], A["L2_gnn_ln_b"][l].partition_broadcast(P)).then_inc(params, 16)

        @block.tensor
        def _(pe):
            pe.wait_ge(z_ready, 1)
            pe.wait_ge(params, 64)

            def turn(b):
                t0, n = BLOCKS[b]
                if b >= 1:
                    pe.wait_ge(kept, b)
                for k in range(n):
                    tr = pe.transpose(p_t[:, k * P:(k + 1) * P], Z[:, t0 + k, :], T.ident[:, :])
                tr.then_inc(turned, 1)

            turn(0)
            for b, (t0, n) in enumerate(BLOCKS):
                if b + 1 < NB:
                    turn(b + 1)
                pe.wait_ge(masked, b + 1)
                if b >= 2:
                    pe.wait_ge(silued, b - 1)
                for k in range(n):
                    for t in range(TYPES):
                        mm = pe.matmul(p_o[b % 2][:, k, :], xm[:, b % 2, t, k * P:(k + 1) * P], wa[:, t, :], start=(t == 0), stop=(t == TYPES - 1))
                mm.then_inc(made, 1)

        @block.scalar
        def _(act):

            def keep(b):
                w = BLOCKS[b][1] * P
                act.wait_ge(turned, b + 1)
                if b >= 1:
                    act.wait_ge(masked, b)
                act.activation(z_t[:, 0:w], p_t[:, 0:w], ACT.Copy).then_inc(kept, 1)

            def square(b):
                t0, n = BLOCKS[b]
                act.wait_ge(centred, b + 1)
                act.activation(Z[:, t0:t0 + n, :], O[:, t0:t0 + n, :], ACT.Square).then_inc(squared, 1)

            act.wait_ge(al_sum, 1)
            act.activation(al[:, 1, :], al[:, 0, :], ACT.Sigmoid).then_inc(al_ready, 1)
            keep(0)
            for b, (t0, n) in enumerate(BLOCKS):
                if b + 1 < NB:
                    keep(b + 1)
                act.wait_ge(made, b + 1)
                act.activation(O[:, t0:t0 + n, :], p_o[b % 2][:, 0:n, :], ACT.Silu).then_inc(silued, 1)
                if b >= 1:
                    square(b - 1)
            square(NB - 1)
            act.wait_ge(var_ready, 1)
            act.activation(st[:, 2, :], st[:, 1, :], ACT.Sqrt).then_inc(root, 1)

        @block.vector
        def _(dve):
            then = Chain(dve, chain)

            def wide(a):
                return a.unsqueeze(2).to_broadcast([P, TILES, D])

            then(dve.tensor_scalar(den[:, :, :], T.agg[:, :, D:AW], 1e-16, None, ALU.add))
            then(dve.reciprocal(den[:, :, :], den[:, :, :]))
            for h in range(HEADS):
                of = slice(h * HS, (h + 1) * HS)
                ins = dve.tensor_tensor(Z[:, :, of], T.agg[:, :, of], den[:, :, h].unsqueeze(2).to_broadcast([P, TILES, HS]), ALU.mult)
            ins.then_inc(z_ready, 1)
            dve.wait_ge(params, 64)
            then(dve.tensor_scalar(al[:, 0, :], T.type_of[:, :], 0.0, skip[:, 0:1], ALU.is_equal, ALU.mult))
            for t in range(1, TYPES):
                then(dve.tensor_scalar(al[:, 1, :], T.type_of[:, :], float(t), skip[:, t:t + 1], ALU.is_equal, ALU.mult))
                then(dve.tensor_tensor(al[:, 0, :], al[:, 0, :], al[:, 1, :], ALU.add))
            dve.sem_inc(al_sum, 1)

            def mask(b):
                t0, n = BLOCKS[b]
                dve.wait_ge(kept, b + 1)
                if b >= 2:
                    dve.wait_ge(made, b - 1)
                for t in range(TYPES):
                    ins = dve.scalar_tensor_tensor(out=xm[:, b % 2, t, 0:n * P], in0=T.type_row[:, t0 * P:(t0 + n) * P], scalar=float(t),
                                                   in1=z_t[:, 0:n * P], op0=ALU.is_equal, op1=ALU.mult)
                ins.then_inc(masked, 1)

            def centre(b):
                t0, n = BLOCKS[b]
                these = slice(t0, t0 + n)
                o, h, mean = O[:, these, :], T.H[:, these, :], st[:, 0, these]

                def wide(a):
                    return a.unsqueeze(2).to_broadcast([P, n, D])

                dve.wait_ge(silued, b + 1)
                then(dve.tensor_tensor(o, o, h, ALU.subtract))
                then(dve.tensor_tensor(o, o, wide(al[:, 1, these]), ALU.mult))
                then(dve.tensor_tensor(o, o, h, ALU.add))
                then(dve.tensor_reduce(mean, o, AX.X, ALU.add))
                then(dve.tensor_scalar(mean, mean, 1.0 / D, None, ALU.mult))
                dve.tensor_tensor(o, o, wide(mean), ALU.subtract).then_inc(centred, 1)

            def spread(b):
                t0, n = BLOCKS[b]
                dve.wait_ge(squared, b + 1)
                then(dve.tensor_reduce(st[:, 1, t0:t0 + n], Z[:, t0:t0 + n, :], AX.X, ALU.add))

            mask(0)
            dve.wait_ge(al_ready, 1)
            for b in range(NB):
                if b + 1 < NB:
                    mask(b + 1)
                centre(b)
                if b >= 1:
                    spread(b - 1)
            spread(NB - 1)
            dve.tensor_scalar(st[:, 1, :], st[:, 1, :], 1.0 / D, EPS, ALU.mult, ALU.add).then_inc(var_ready, 1)
            dve.wait_ge(root, 1)
            then(dve.reciprocal(st[:, 3, :], st[:, 2, :]))
            dve.wait_ge(centred, NB)
            for k, (op, by) in enumerate(((ALU.mult, wide(st[:, 3, :])),
                                          (ALU.mult, par[:, 0, :].unsqueeze(1).to_broadcast([P, TILES, D])),
                                          (ALU.add, par[:, 1, :].unsqueeze(1).to_broadcast([P, TILES, D])))):
                then(dve.tensor_tensor(T.H[:, :, :] if k == 2 else O[:, :, :], O[:, :, :], by, op))


def feed_out(nc, A, T):
    with ExitStack() as ctx:
        sb, ps, sem = stack(nc, ctx, "feed_out_")
        w, b0, one = sb("wff", [D, D]), sb("bff", [1, D]), sb("one_ff", [1, P])
        h_t = sb("ff_h_t", [P, 2, 512])
        p_t = [ps(f"ff_p_t{i}", [P, 512]) for i in range(2)]
        p_o = [ps(f"ff_p_o{i}", [P, 4, D]) for i in range(2)]
        params, set_up, turned, kept, made, taken = (sem("ff_" + n) for n in ("params", "set_up", "turned", "kept", "made", "taken"))
        block = ctx.enter_context(nc.Block())

        @block.sync
        def _(sp):
            sp.dma_start(w[:, :], A["L2_gnn_Wff"]).then_inc(params, 16)
            sp.dma_start(b0[:, :], A["L2_gnn_bff"].rearrange("(o f) -> o f", o=1)).then_inc(params, 16)

        @block.tensor
        def _(pe):

            def turn(b):
                t0, n = BLOCKS[b]
                if b >= 2:
                    pe.wait_ge(kept, b - 1)
                for k in range(n):
                    tr = pe.transpose(p_t[b % 2][:, k * P:(k + 1) * P], T.H[:, t0 + k, :], T.ident[:, :])
                tr.then_inc(turned, 1)

            def multiply(b):
                t0, n = BLOCKS[b]
                if b == 0:
                    pe.wait_ge(set_up, 1)
                    pe.wait_ge(params, 32)
                pe.wait_ge(kept, b + 1)
                if b >= 2:
                    pe.wait_ge(taken, b - 1)
                for k in range(n):
                    pe.matmul(p_o[b % 2][:, k, :], h_t[:, b % 2, k * P:(k + 1) * P], w[:, :], start=True, stop=False)
                    mm = pe.matmul(p_o[b % 2][:, k, :], one[:, :], b0[:, :], start=False, stop=True)
                mm.then_inc(made, 1)

            staggered(turn, multiply)

        @block.scalar
        def _(act):
            for b, (t0, n) in enumerate(BLOCKS):
                act.wait_ge(turned, b + 1)
                if b >= 2:
                    act.wait_ge(made, b - 1)
                act.activation(h_t[:, b % 2, 0:n * P], p_t[b % 2][:, 0:n * P], ACT.Copy).then_inc(kept, 1)

        @block.vector
        def _(dve):
            dve.memset(one[:, :], 1.0).then_inc(set_up, 1)
            for b, (t0, n) in enumerate(BLOCKS):
                dve.wait_ge(made, b + 1)
                dve.tensor_tensor(T.X[:, t0:t0 + n, :], T.X[:, t0:t0 + n, :], p_o[b % 2][:, 0:n, :], ALU.add).then_inc(taken, 1)


def gate_tables(nc, A, T):
    with ExitStack() as ctx:
        sb, ps, sem = stack(nc, ctx, "gate_tables_")
        w = sb("gt_w", [D, ROW3])
        row_b, one = sb("gt_row_b", [1, ROW3]), sb("gt_one", [1, P])
        w_dst, w_dst_wide, b_att = sb("gt_w_dst", [D, 1]), sb("gt_w_dst_wide", [D, P]), sb("gt_b_att", [P, 1])
        rows = sb("gt_rows", [P, TILES, ROW3])
        p_t = [ps(f"gt_p_t{i}", [P, 512]) for i in range(2)]
        p_o = [[ps(f"gt_p_o{i}{j}", [P, 2, 256]) for j in range(2)] for i in range(2)]
        p_d = [ps(f"gt_p_d{i}", [P, 512]) for i in range(2)]
        params, set_up, turned, kept, made, taken, dsts, dst_kept, stored, widened = (
            sem("gt_" + n) for n in ("params", "set_up", "turned", "kept", "made", "taken", "dsts", "dst_kept", "stored", "widened"))
        block = ctx.enter_context(nc.Block())
        W_att = A["L3_gnn_W_att"]

        @block.sync
        def _(sp):
            sp.wait_ge(set_up, 3)
            sp.dma_start(w[:, 0:D], A["L3_gnn_W_msg"]).then_inc(params, 16)
            sp.dma_start(w[:, D:D + 1], W_att[0:D, :]).then_inc(params, 16)
            sp.dma_start(w_dst[:, :], W_att[D:2 * D, :]).then_inc(params, 16)
            sp.dma_start(row_b[:, 0:D], A["L3_gnn_b_msg"].rearrange("(o f) -> o f", o=1)).then_inc(params, 16)
            sp.dma_start(b_att[:, :], A["L3_gnn_b_att"].partition_broadcast(P)).then_inc(params, 16)
            sp.wait_ge(taken, 2 * len(BLOCKS) - 1)
            sp.dma_start(T.gate_table.rearrange("(t p) f -> p t f", p=P), rows[:, :, :]).then_inc(stored, 16)
            sp.wait_ge(stored, 16)

        @block.tensor
        def _(pe):
            done = 0

            def turn(b):
                t0, n = BLOCKS[b]
                if b >= 2:
                    pe.wait_ge(kept, b - 1)
                for k in range(n):
                    tr = pe.transpose(p_t[b % 2][:, k * P:(k + 1) * P], T.H[:, t0 + k, :], T.ident[:, :])
                tr.then_inc(turned, 1)

            def multiply(b):
                t0, n = BLOCKS[b]
                if b == 0:
                    pe.wait_ge(widened, 1)
                pe.wait_ge(kept, b + 1)
                if b >= 2:
                    pe.wait_ge(taken, 2 * (b - 1))
                    pe.wait_ge(dst_kept, b - 1)
                for k in range(n):
                    at = p_o[b % 2][k // 2][:, k % 2, 0:ROW3]
                    pe.matmul(at, T.H_t[:, (t0 + k) * P:(t0 + k + 1) * P], w[:, :], start=True, stop=False)
                    mm = pe.matmul(at, one[:, :], row_b[:, :], start=False, stop=True)
                mm.then_inc(made, 1)
                pe.matmul(p_d[b % 2][:, 0:n * P], w_dst_wide[:, :], T.H_t[:, t0 * P:(t0 + n) * P], start=True, stop=True).then_inc(dsts, 1)

            staggered(turn, multiply)

        @block.scalar
        def _(act):

            def keep(b):
                t0, n = BLOCKS[b]
                act.wait_ge(turned, b + 1)
                act.activation(T.H_t[:, t0 * P:(t0 + n) * P], p_t[b % 2][:, 0:n * P], ACT.Copy).then_inc(kept, 1)

            def keep_dst(b):
                t0, n = BLOCKS[b]
                act.wait_ge(dsts, b + 1)
                act.activation(T.dst_row[:, t0 * P:(t0 + n) * P], p_d[b % 2][:, 0:n * P], ACT.Identity, bias=b_att[:, 0:1]).then_inc(dst_kept, 1)

            staggered(keep, keep_dst)

        @block.vector
        def _(dve):
            dve.memset(w[:, :], 0.0).then_inc(set_up, 1)
            dve.memset(row_b[:, :], 0.0).then_inc(set_up, 1)
            dve.memset(one[:, :], 1.0).then_inc(set_up, 1)
            dve.wait_ge(params, 80)
            dve.tensor_copy(w_dst_wide[:, :], w_dst[:, 0:1].to_broadcast([D, P])).then_inc(widened, 1)
            for b, (t0, n) in enumerate(BLOCKS):
                dve.wait_ge(made, b + 1)
                for j in range((n + 1) // 2):
                    m = min(2, n - 2 * j)
                    dve.tensor_copy(rows[:, t0 + 2 * j:t0 + 2 * j + m, :], p_o[b % 2][j][:, 0:m, 0:ROW3]).then_inc(taken, 1)


def gate_pass(nc, A, T):
    with ExitStack() as ctx:
        sb, ps, sem = stack(nc, ctx, "gate_pass_")
        idx = sb("idx", [P, 4, G], I32)
        hx = sb("hx", [P, 4, G, ROW3])
        oh = sb("oh", [P, 4, G, P])
        dst_rows = sb("dst_rows", [P, 2, G, P])
        pick = sb("pick", [P, 2, G, P])
        dst_term = sb("dst_term", [P, 2, G])
        z, gate = sb("z", [P, 2, G]), sb("gate", [P, 2, G])
        msg = sb("msg", [P, 2, G, D])
        agg = AggInPsum(sb, ps, sem)
        idx_ready, onehots, rows_ready, messages, summed, gates, terms, dst_terms = (
            sem(n) for n in ("idx_ready", "onehots", "rows_ready", "messages", "summed", "gates", "terms", "dst_terms"))
        picked, opened = sem("picked"), sem("opened")
        block = ctx.enter_context(nc.Block())

        @block.gpsimd
        def _(pool):
            bound = pool.to_reg(NP - 1)

            def step(g, s, r):
                pool.wait_ge(idx_ready, g + 3)
                if past(g, 2):
                    pool.wait_ge(messages, g - 1)
                pool.sem_inc(opened, 1)
                for k in range(G):
                    pool.indirect_dma_start(out=hx[:, r, k, :], out_offset=None, in_=T.gate_table,
                                            in_offset=bass.IndirectOffsetOnAxis(ap=idx[:, r, k:k + 1].bitcast(U32), axis=0),
                                            bounds_check=bound).then_inc(T.gathered[r], 16)

            pipeline(pool, step)

        @block.scalar
        def _(act):
            act.sem_inc(idx_ready, 2)
            act.sem_inc(rows_ready, 2)
            act.sem_inc(gates, 2)
            tiles_of = TurnTiles(nc, act, T)

            def step(g, s, r):
                if within(g):
                    if past(g, 2):
                        act.wait_ge(messages, g - 1)
                    act.activation(idx[:, r, :], T.src[:, bass.ds(g * G, G)], ACT.Copy).then_inc(idx_ready, 1)
                    act.wait_ge(dst_terms, g + 1)
                    for k, t in enumerate(tiles_of(g, r)):
                        ins = act.activation(dst_rows[:, s, k, :], T.dst_row[:, bass.ds(t * P, P)], ACT.Copy)
                    ins.then_inc(rows_ready, 1)
                if past(g, 1):
                    h, q = g - 1, 1 - s
                    act.wait_ge(terms, h + 3)
                    act.activation(gate[:, q, :], z[:, q, :], ACT.Sigmoid).then_inc(gates, 1)

            pipeline(act, step, drain=(GROUPS,))

        @block.tensor
        def _(pe):
            pe.sem_inc(summed, 2)
            agg.sweep(pe, True)
            tiles_of = TurnTiles(nc, pe, T)

            def step(g, s, r):
                tiles = tiles_of(g, r)
                pe.wait_ge(messages, g + 3)
                pe.wait_ge(onehots, g + 3)
                for k in range(G):
                    mm = agg.add(pe, tiles[k], oh[:, r, k, :], msg[:, s, k, :])
                mm.then_inc(summed, 1)

            pipeline(pe, step)
            agg.sweep(pe, False)

        @block.vector
        def _(dve):
            for q in (onehots, messages, terms, dst_terms):
                dve.sem_inc(q, 2)
            agg.clear(dve)

            def step(g, s, r):
                h, q = g - 1, 1 - s
                if past(g, 1):
                    wait_gathers(dve, T, 4, h, (r - 1) % 4)
                    dve.wait_ge(dst_terms, h + 3)
                    dve.wait_ge(gates, h + 1)
                    dve.tensor_tensor(z[:, q, :], hx[:, (r - 1) % 4, :, D], dst_term[:, q, :], ALU.add).then_inc(terms, 1)
                if within(g):
                    if past(g, 2):
                        dve.wait_ge(summed, g - 1)
                    dve.tensor_tensor(oh[:, r, :, :], T.iota[:, :].unsqueeze(1).to_broadcast([P, G, P]),
                                      T.rel[:, bass.ds(g * G, G)].unsqueeze(2).to_broadcast([P, G, P]),
                                      ALU.is_equal).then_inc(onehots, 1)
                    dve.wait_ge(onehots, g + 3)
                    dve.wait_ge(rows_ready, g + 3)
                    dve.wait_ge(dst_terms, g + 1)
                    dve.tensor_tensor(pick[:, s, :, :], oh[:, r, :, :], dst_rows[:, s, :, :], ALU.mult).then_inc(picked, 1)
                    dve.wait_ge(picked, g + 1)
                    dve.wait_ge(terms, g + 1)
                    dve.tensor_reduce(dst_term[:, s, :], pick[:, s, :, :], AX.X, ALU.add).then_inc(dst_terms, 1)
                if past(g, 1):
                    dve.wait_ge(gates, h + 3)
                    dve.wait_ge(summed, h + 1)
                    dve.tensor_tensor(msg[:, q, :, :], hx[:, (r - 1) % 4, :, 0:D], gate[:, q, :].unsqueeze(2).to_broadcast([P, G, D]), ALU.mult).then_inc(messages, 1)

            pipeline(dve, step, drain=(GROUPS,))
            agg.store(dve, T)


def node_gru(nc, A, T, out):
    with ExitStack() as ctx:
        sb, ps, sem = stack(nc, ctx, "node_gru_")
        raw = sb("gru_raw", [P, 2, 3, D])
        w_t = sb("gru_w_t", [P, 2, 3, D])
        bias = sb("gru_bias", [P, 2, 3])
        both = sb("gru_both", [P, 2])
        agg_t = sb("gru_agg_t", [P, 2, 512])
        r, z, nn, hn = (sb("gru_" + n, [P, 2, 512]) for n in ("r", "z", "nn", "hn"))
        Y = sb("gru_Y", [P, NP])
        p_t = [ps(f"gru_p_t{i}", [P, 512]) for i in range(2)]
        p_r, p_z, p_i, p_h = (ps("gru_p_" + n, [P, 512]) for n in "rzih")
        p_b = [ps(f"gru_p_b{i}", [P, 4, D]) for i in range(2)]
        params, chain, w_turned, w_kept, turned, kept, gated, sig, steps, tanhed, biased = (
            sem("gru_" + n) for n in ("params", "chain", "w_turned", "w_kept", "turned", "kept", "gated", "sig", "steps", "tanhed", "biased"))
        back, taken, n_read, i_summed, mixed, done = (sem("gru_" + n) for n in ("back", "taken", "n_read", "i_summed", "mixed", "done"))
        bn = Batchnorm(sb, sem, "bn3_", Y)
        block = ctx.enter_context(nc.Block())
        NB = len(BLOCKS)

        @block.sync
        def _(sp):
            for k, name in enumerate(("ih", "hh")):
                sp.dma_start(raw[:, k, :, :], A["L3_gnn_W_" + name].rearrange("(g p) f -> p g f", p=P)).then_inc(params, 16)
                for g in range(3):
                    sp.dma_start(bias[:, k, g:g + 1], A["L3_gnn_b_" + name][g * P:(g + 1) * P].rearrange("(p o) -> p o", o=1)).then_inc(params, 16)
            bn.load(sp, A["L3_gnn_gamma"], A["L3_gnn_beta"])
            full = N // P
            sp.wait_ge(taken, NB)
            sp.dma_start(out[0:full * P, :].rearrange("(t p) f -> p t f", p=P), T.X[:, 0:full, :]).then_inc(done, 16)
            sp.dma_start(out[full * P:N, :], T.X[0:N - full * P, full, :]).then_inc(done, 16)
            sp.wait_ge(done, 32)

        @block.tensor
        def _(pe):
            pe.wait_ge(params, 128)
            for k in range(2):
                for g in range(3):
                    tr = pe.transpose(p_t[k][:, g * P:(g + 1) * P], raw[:, k, g, :], T.ident[:, :])
                tr.then_inc(w_turned, 1)
            pe.wait_ge(w_kept, 2)

            def turn(b):
                t0, n = BLOCKS[b]
                if b >= 2:
                    pe.wait_ge(kept, b - 1)
                for k in range(n):
                    tr = pe.transpose(p_t[b % 2][:, k * P:(k + 1) * P], T.agg[:, t0 + k, 0:D], T.ident[:, :])
                tr.then_inc(turned, 1)

            def gate(b):
                t0, n = BLOCKS[b]
                pe.wait_ge(kept, b + 1)
                w = n * P
                a, h = agg_t[:, b % 2, 0:w], T.H_t[:, t0 * P:t0 * P + w]
                if b >= 1:
                    pe.wait_ge(sig, 2 * b)
                for g, bank in enumerate((p_r, p_z)):
                    pe.matmul(bank[:, 0:w], w_t[:, 0, g, :], a, start=True, stop=False)
                    pe.matmul(bank[:, 0:w], w_t[:, 1, g, :], h, start=False, stop=True).then_inc(gated, 1)
                if b >= 1:
                    pe.wait_ge(n_read, b)
                    pe.wait_ge(i_summed, b)
                pe.matmul(p_h[:, 0:w], w_t[:, 1, 2, :], h, start=True, stop=True).then_inc(gated, 1)
                pe.matmul(p_i[:, 0:w], w_t[:, 0, 2, :], a, start=True, stop=True).then_inc(gated, 1)

            staggered(turn, gate)
            pe.wait_ge(bn.done, 1)
            for b, (t0, n) in enumerate(BLOCKS):
                if b >= 2:
                    pe.wait_ge(taken, b - 1)
                for k in range(n):
                    tr = pe.transpose(p_b[b % 2][:, k, :], Y[:, (t0 + k) * P:(t0 + k + 1) * P], T.ident[:, :])
                tr.then_inc(back, 1)

        @block.scalar
        def _(act):
            act.wait_ge(params, 128)
            for k in range(2):
                act.wait_ge(w_turned, k + 1)
                act.activation(w_t[:, k, :, :], p_t[k][:, 0:3 * P].rearrange("p (g o) -> p g o", g=3), ACT.Copy).then_inc(w_kept, 1)
            act.wait_ge(biased, 1)

            def keep(b):
                t0, n = BLOCKS[b]
                w, s = n * P, b % 2
                act.wait_ge(turned, b + 1)
                if b >= 2:
                    act.wait_ge(gated, 4 * (b - 1))
                act.activation(agg_t[:, s, 0:w], p_t[s][:, 0:w], ACT.Copy).then_inc(kept, 1)

            def activate(b):
                w, s = BLOCKS[b][1] * P, b % 2
                if b >= 2:
                    act.wait_ge(steps, 3 * (b - 1))
                act.wait_ge(gated, 4 * b + 1)
                act.activation(r[:, s, 0:w], p_r[:, 0:w], ACT.Sigmoid, bias=both[:, 0:1]).then_inc(sig, 1)
                act.wait_ge(gated, 4 * b + 2)
                act.activation(z[:, s, 0:w], p_z[:, 0:w], ACT.Sigmoid, bias=both[:, 1:2]).then_inc(sig, 1)
                act.wait_ge(gated, 4 * b + 3)
                act.activation(hn[:, s, 0:w], p_h[:, 0:w], ACT.Identity, bias=bias[:, 1, 2:3]).then_inc(n_read, 1)

            def tanh(b):
                w, s = BLOCKS[b][1] * P, b % 2
                act.wait_ge(i_summed, b + 1)
                act.activation(nn[:, s, 0:w], nn[:, s, 0:w], ACT.Tanh, bias=bias[:, 0, 2:3]).then_inc(tanhed, 1)

            staggered(keep, activate, tanh)
            bn.on_scalar(act, ACT.Identity)

        @block.vector
        def _(dve):
            then = Chain(dve, chain)
            dve.wait_ge(params, 128)
            dve.tensor_tensor(both[:, :], bias[:, 0, 0:2], bias[:, 1, 0:2], ALU.add).then_inc(biased, 1)

            def mix(b):
                w, s = BLOCKS[b][1] * P, b % 2
                dve.wait_ge(n_read, b + 1)
                dve.tensor_tensor(nn[:, s, 0:w], r[:, s, 0:w], hn[:, s, 0:w], ALU.mult).then_inc(mixed, 1)
                dve.wait_ge(mixed, b + 1)
                dve.wait_ge(gated, 4 * b + 4)
                dve.tensor_tensor(nn[:, s, 0:w], nn[:, s, 0:w], p_i[:, 0:w], ALU.add).then_inc(i_summed, 1)

            def finish(b):
                t0, n = BLOCKS[b]
                w, s = n * P, b % 2
                h, y = T.H_t[:, t0 * P:t0 * P + w], Y[:, t0 * P:t0 * P + w]
                dve.wait_ge(tanhed, b + 1)
                dve.tensor_tensor(y, h, nn[:, s, 0:w], ALU.subtract).then_inc(steps, 1)
                dve.wait_ge(steps, 3 * b + 1)
                dve.tensor_tensor(y, y, z[:, s, 0:w], ALU.mult).then_inc(steps, 1)
                dve.wait_ge(steps, 3 * b + 2)
                dve.tensor_tensor(y, y, nn[:, s, 0:w], ALU.add).then_inc(steps, 1)

            staggered(mix, finish)
            dve.wait_ge(steps, 3 * NB)
            bn.on_vector(dve, then)
            for b, (t0, n) in enumerate(BLOCKS):
                dve.wait_ge(back, b + 1)
                dve.tensor_tensor(T.X[:, t0:t0 + n, :], T.X[:, t0:t0 + n, :], p_b[b % 2][:, 0:n, :], ALU.add).then_inc(taken, 1)


def clear_semaphores(nc):
    free = sorted(nc.free_semaphores)
    assert free == list(range(free[0], free[-1] + 1))
    with nc.Block() as block:
        @block.gpsimd
        def _(pool):
            pool.sem_clear(range(free[0], free[-1] + 1))


def program(nc, A, out):
    T = Tensors()
    with ExitStack() as ctx:
        sb, ps, sem = stack(nc, ctx)
        T.chunk_table = nc.dram_tensor("chunk_table", (CT * P, 3 * P), I32).ap()
        T.attr = nc.dram_tensor("attr_padded", ((VISITS - TILES + 1) * P, EF), F32).ap()
        T.h_table = nc.dram_tensor("h_table", (NP, D), F32).ap()
        T.kv_table = nc.dram_tensor("kv_table", (NP * REL, 2 * D), F32).ap()
        T.m_table = nc.dram_tensor("m_table", (VISITS * P, D), F32).ap()
        T.gate_table = nc.dram_tensor("gate_table", (NP, ROW3), F32).ap()
        T.X = sb("X", [P, TILES, D])
        T.H = sb("H", [P, TILES, D])
        T.agg = sb("agg", [P, TILES, AW])
        T.ident = sb("ident", [P, P])
        T.iota = sb("iota", [P, P])
        T.rel = sb("rel", [P, CT * P])
        T.key = sb("key", [P, CT * P])
        T.src = sb("src", [P, CT * P], I32)
        T.srcrel = sb("srcrel", [P, CT * P], I32)
        T.tile_codes = sb("tile_codes", [1, GROUPS], I32)
        T.gathered = [sem(f"gathered{i}") for i in range(4)]
        T.rows_in = sem("visit_rows_in")
        T.attr_copied = sem("attr_copied")
        with ExitStack() as layer0:
            T.zeros = layer0.enter_context(nc.sbuf_tensor("zeros", [P, 16 * EF], F32))
            setup(nc, A, T)
            layernorm_relu(nc, T, "ln0", True)
            edge_mlp_pass(nc, A, T)
        node_mlp(nc, A, T)
        layernorm_relu(nc, T, "ln1", True)
        sum_pass(nc, A, T)
        node_gin(nc, A, T)
        clear_semaphores(nc)
        layernorm_relu(nc, T, "ln2", False)
        with ExitStack() as layer2:
            sb, ps, sem = stack(nc, layer2)
            T.type_row = sb("type_row", [P, NP])
            T.type_of = sb("type_of", [P, TILES])
            T.Q = sb("Q", [P, TILES, D])
            T.whole = sb("whole_lane", [1, 2, P])
            T.att = sb("att", [P, SV, HEADS])
            T.flag = sb("flag", [P, LE + 1])
            scan_flags(nc, A, T)
            for l in range(LAYERS):
                typed_qkv(nc, A, T, l)
                score_pass(nc, A, T, l)
                softmax_shift(nc, A, T, l)
                message_pass(nc, A, T, l)
                node_update(nc, A, T, l)
                clear_semaphores(nc)
        feed_out(nc, A, T)
        layernorm_relu(nc, T, "ln3", False)
        T.H_t = sb_outer(nc, ctx, "H_t", [P, NP])
        T.dst_row = sb_outer(nc, ctx, "dst_row", [P, NP])
        gate_tables(nc, A, T)
        gate_pass(nc, A, T)
        node_gru(nc, A, T, out)


def sb_outer(nc, ctx, name, shape):
    return ctx.enter_context(nc.sbuf_tensor(name, shape, F32))




def kernel(**inputs):
    import numpy as _np
    import concourse.bacc as _bacc
    from concourse.bass_utils import run_bass_kernel_spmd as _run

    nc = _bacc.Bacc("TRN2", target_bir_lowering=False, num_devices=1)
    arrays, args = {}, {}
    for name, value in inputs.items():
        a = _np.ascontiguousarray(value)
        arrays[f"in_{name}_dram"] = a
        args[name] = nc.dram_tensor(f"in_{name}_dram", a.shape, mybir.dt.from_np(a.dtype), kind="ExternalInput").ap()
    out = nc.dram_tensor("out_dram", (N, D), F32, kind="ExternalOutput").ap()
    program(nc, args, out)
    r = _run(nc, [arrays], core_ids=[0])
    return r.results[0]["out_dram"]
```
